# Optimizing a Trainium2 kernel written in Bass

```python
import numpy as np
import jax
import jax.numpy as jnp

def _softmax(x, axis=-1):
    return jax.nn.softmax(x, axis=axis)

def _gelu(x):
    return jax.nn.gelu(x, approximate=True)

def _silu(x):
    return jax.nn.silu(x)

def _sigmoid(x):
    return jax.nn.sigmoid(x)

def _layernorm(x, axis=-1, eps=1e-05):
    m = jnp.mean(x, axis=axis, keepdims=True)
    v = jnp.var(x, axis=axis, keepdims=True)
    return (x - m) / jnp.sqrt(v + eps)

def _scatter_add(tgt, idx, src, axis=0):
    return tgt.at[idx].add(src)

def _segment_sum(src, seg, n):
    return jax.ops.segment_sum(src, seg, n)
kernel_name = 'mk_xattn_ffn_d2_seqx_r4_aba13f'

def setup_inputs(seed: int=0):
    np.random.seed(seed)
    _w = jnp.asarray

    def _rec_inputs():
        import jax
        import jax.numpy as jnp
        _rk = jax.random.key(seed)
        x = 7.22e-05 + 1 * jax.random.normal(jax.random.fold_in(_rk, 1), (16, 256, 256), jnp.float32)
        _lenS = 256 - jax.random.randint(jax.random.fold_in(_rk, 7), (16,), 0, max(1, 256 // 4) + 1, jnp.int32)
        _lenS2 = 120 - jax.random.randint(jax.random.fold_in(_rk, 8), (16,), 0, max(1, 120 // 4) + 1, jnp.int32)
        _ctx_1024P = jax.random.normal(jax.random.fold_in(_rk, 11), (16, 16, 256), jnp.float32)
        _ctx_1024c = jax.random.dirichlet(jax.random.fold_in(_rk, 511), 0.3 * jnp.ones((16,), jnp.float32), (16, 120))
        _ctx_1024t = jnp.einsum('bsk,bkd->bsd', _ctx_1024c, _ctx_1024P)
        _ctx_1024t = _ctx_1024t * jax.lax.rsqrt(jnp.mean(jnp.square(_ctx_1024t)) + 1e-12) * 0.953939
        ctx_1024 = -0.000514642 + 1.00011 * (_ctx_1024t + 0.3 * jax.random.normal(jax.random.fold_in(_rk, 611), (16, 120, 256), jnp.float32))
        return (x, ctx_1024)
    x, ctx_1024 = _rec_inputs()

    def _L0_xattn_setup():
        import jax, jax.numpy as jnp
        import numpy as np
        B, L_ENC, L_DEC, D = (16, 128, 128, 256)
        key = jax.random.key(seed)
        k1, k2, k3, k4, k5, k6 = jax.random.split(key, 6)
        encoder_hc = jax.random.normal(k1, (B, L_ENC, D), dtype=jnp.float32)
        decoder_hq = jax.random.normal(k2, (B, L_DEC, D), dtype=jnp.float32)
        w_sim = jax.random.normal(k3, (3 * D,), dtype=jnp.float32) * 0.02
        b_sim = jax.random.normal(k4, (1,), dtype=jnp.float32) * 0.02
        W_qv = jax.random.normal(k5, (4 * D, D), dtype=jnp.float32) * 0.02
        b_qv = jax.random.normal(k6, (D,), dtype=jnp.float32) * 0.02
        return {'encoder_hc': encoder_hc, 'decoder_hq': decoder_hq, 'w_sim': w_sim, 'b_sim': b_sim, 'W_qv': W_qv, 'b_qv': b_qv}
    _L0_xattn_all = _L0_xattn_setup()
    _L0_xattn_in = {k: v for k, v in _L0_xattn_all.items() if k in ('w_sim', 'b_sim', 'W_qv', 'b_qv')}
    del _L0_xattn_all

    def _L0_ffn_setup():
        import jax, jax.numpy as jnp
        import numpy as np
        B, T, C = (8, 512, 256)
        E, K = (8, 2)
        H = 4 * C
        CAP_FACTOR = 1.2
        EPS = 1e-09
        key = jax.random.key(seed)
        ks = jax.random.split(key, 6)
        x = jax.random.normal(ks[0], (B, T, C), dtype=jnp.float32)
        router_w = jax.random.normal(ks[1], (E, C), dtype=jnp.float32) * 0.02
        router_b = jnp.zeros((E,), dtype=jnp.float32)
        fc1_w = jax.random.normal(ks[2], (E, H, C), dtype=jnp.float32) * (1.0 / np.sqrt(C))
        fc1_b = jnp.zeros((E, H), dtype=jnp.float32)
        fc2_w = jax.random.normal(ks[3], (E, C, H), dtype=jnp.float32) * (1.0 / np.sqrt(H))
        fc2_b = jnp.zeros((E, C), dtype=jnp.float32)
        layer_scale = jnp.full((E, C), 0.1, dtype=jnp.float32)
        return {'x': x, 'router_w': router_w, 'router_b': router_b, 'fc1_w': fc1_w, 'fc1_b': fc1_b, 'fc2_w': fc2_w, 'fc2_b': fc2_b, 'layer_scale': layer_scale}
    _L0_ffn_all = _L0_ffn_setup()
    _L0_ffn_in = {k: v for k, v in _L0_ffn_all.items() if k in ('router_w', 'router_b', 'fc1_w', 'fc1_b', 'fc2_w', 'fc2_b', 'layer_scale')}
    del _L0_ffn_all

    def _L1_xattn_setup():
        import jax, jax.numpy as jnp
        import numpy as np
        D_MODEL = 256
        NUM_HEADS = 16
        HEAD_DIM = D_MODEL // NUM_HEADS
        key = jax.random.key(seed)
        ks = jax.random.split(key, 10)
        B, SQ, SKV = (2, 512, 512)
        s = 1.0 / np.sqrt(D_MODEL)
        inp = {'query': jax.random.normal(ks[0], (B, SQ, D_MODEL), jnp.float32), 'key_value': jax.random.normal(ks[1], (B, SKV, D_MODEL), jnp.float32), 'Wq': jax.random.normal(ks[2], (D_MODEL, D_MODEL), jnp.float32) * s, 'bq': jnp.zeros((D_MODEL,), jnp.float32), 'Wk': jax.random.normal(ks[3], (D_MODEL, D_MODEL), jnp.float32) * s, 'bk': jnp.zeros((D_MODEL,), jnp.float32), 'Wv': jax.random.normal(ks[4], (D_MODEL, D_MODEL), jnp.float32) * s, 'bv': jnp.zeros((D_MODEL,), jnp.float32), 'Wo': jax.random.normal(ks[5], (D_MODEL, D_MODEL), jnp.float32) * s, 'bo': jnp.zeros((D_MODEL,), jnp.float32)}
        return inp
    _L1_xattn_all = _L1_xattn_setup()
    _L1_xattn_in = {k: v for k, v in _L1_xattn_all.items() if k in ('Wq', 'bq', 'Wk', 'bk', 'Wv', 'bv', 'Wo', 'bo')}
    del _L1_xattn_all

    def _L1_ffn_setup():
        import jax, jax.numpy as jnp
        import numpy as np
        D = 256
        I = 128
        E = 32
        K = 4
        T = 2 * 512
        C = 2 * T * K // E
        key = jax.random.key(seed)
        ks = jax.random.split(key, 9)
        bf = jnp.bfloat16
        std = 0.02
        x = jax.random.normal(ks[0], (2, 512, D), dtype=jnp.float32).astype(bf)
        gate_w = (std * jax.random.normal(ks[1], (E, D), dtype=jnp.float32)).astype(bf)
        bias = jnp.zeros((E,), jnp.float32)
        W1 = (std * jax.random.normal(ks[2], (E, D, I), dtype=jnp.float32)).astype(bf)
        W3 = (std * jax.random.normal(ks[3], (E, D, I), dtype=jnp.float32)).astype(bf)
        W2 = (std * jax.random.normal(ks[4], (E, I, D), dtype=jnp.float32)).astype(bf)
        sw1 = (std * jax.random.normal(ks[5], (I, D), dtype=jnp.float32)).astype(bf)
        sw3 = (std * jax.random.normal(ks[6], (I, D), dtype=jnp.float32)).astype(bf)
        sw2 = (std * jax.random.normal(ks[7], (D, I), dtype=jnp.float32)).astype(bf)
        return {'x': x, 'gate_w': gate_w, 'bias': bias, 'W1': W1, 'W3': W3, 'W2': W2, 'sw1': sw1, 'sw3': sw3, 'sw2': sw2}
    _L1_ffn_all = _L1_ffn_setup()
    _L1_ffn_in = {k: v for k, v in _L1_ffn_all.items() if k in ('gate_w', 'bias', 'W1', 'W3', 'W2', 'sw1', 'sw3', 'sw2')}
    del _L1_ffn_all
    return {'x': x, 'ctx_1024': ctx_1024, 'L0_xattn_w_sim': _L0_xattn_in['w_sim'], 'L0_xattn_b_sim': _L0_xattn_in['b_sim'], 'L0_xattn_W_qv': _L0_xattn_in['W_qv'], 'L0_xattn_b_qv': _L0_xattn_in['b_qv'], 'L0_ffn_router_w': _L0_ffn_in['router_w'], 'L0_ffn_router_b': _L0_ffn_in['router_b'], 'L0_ffn_fc1_w': _L0_ffn_in['fc1_w'], 'L0_ffn_fc1_b': _L0_ffn_in['fc1_b'], 'L0_ffn_fc2_w': _L0_ffn_in['fc2_w'], 'L0_ffn_fc2_b': _L0_ffn_in['fc2_b'], 'L0_ffn_layer_scale': _L0_ffn_in['layer_scale'], 'L1_xattn_Wq': _L1_xattn_in['Wq'], 'L1_xattn_bq': _L1_xattn_in['bq'], 'L1_xattn_Wk': _L1_xattn_in['Wk'], 'L1_xattn_bk': _L1_xattn_in['bk'], 'L1_xattn_Wv': _L1_xattn_in['Wv'], 'L1_xattn_bv': _L1_xattn_in['bv'], 'L1_xattn_Wo': _L1_xattn_in['Wo'], 'L1_xattn_bo': _L1_xattn_in['bo'], 'L1_ffn_gate_w': _L1_ffn_in['gate_w'], 'L1_ffn_bias': _L1_ffn_in['bias'], 'L1_ffn_W1': _L1_ffn_in['W1'], 'L1_ffn_W3': _L1_ffn_in['W3'], 'L1_ffn_W2': _L1_ffn_in['W2'], 'L1_ffn_sw1': _L1_ffn_in['sw1'], 'L1_ffn_sw3': _L1_ffn_in['sw3'], 'L1_ffn_sw2': _L1_ffn_in['sw2']}

def reference(x, ctx_1024, L0_xattn_w_sim, L0_xattn_b_sim, L0_xattn_W_qv, L0_xattn_b_qv, L0_ffn_router_w, L0_ffn_router_b, L0_ffn_fc1_w, L0_ffn_fc1_b, L0_ffn_fc2_w, L0_ffn_fc2_b, L0_ffn_layer_scale, L1_xattn_Wq, L1_xattn_bq, L1_xattn_Wk, L1_xattn_bk, L1_xattn_Wv, L1_xattn_bv, L1_xattn_Wo, L1_xattn_bo, L1_ffn_gate_w, L1_ffn_bias, L1_ffn_W1, L1_ffn_W3, L1_ffn_W2, L1_ffn_sw1, L1_ffn_sw3, L1_ffn_sw2):
    import jax
    import jax.numpy as jnp

    def _L0_xattn_ref(encoder_hc, decoder_hq, w_sim, b_sim, W_qv, b_qv):
        import jax, jax.numpy as jnp
        import numpy as np
        B, L_ENC, L_DEC, D = (16, 128, 128, 256)
        d = encoder_hc.shape[-1]
        w1, w2, w3 = (w_sim[:d], w_sim[d:2 * d], w_sim[2 * d:])
        Sim = (encoder_hc @ w1)[:, :, None] + (decoder_hq @ w2)[:, None, :] + jnp.einsum('bid,bjd->bij', encoder_hc * w3, decoder_hq) + b_sim[0]
        A = jax.nn.softmax(Sim, axis=2)
        hq_hat = jnp.einsum('bij,bjd->bid', A, decoder_hq)
        Batt = jax.nn.softmax(jnp.max(Sim, axis=2), axis=1)
        hc_bar = jnp.einsum('bi,bid->bd', Batt, encoder_hc)[:, None, :]
        hc_hat = jnp.broadcast_to(hc_bar, encoder_hc.shape)
        feats = jnp.concatenate([encoder_hc, hq_hat, encoder_hc * hq_hat, encoder_hc * hc_hat], axis=-1)
        hcq = feats @ W_qv + b_qv
        return hcq

    def _L0_ffn_ref(x, router_w, router_b, fc1_w, fc1_b, fc2_w, fc2_b, layer_scale):
        import jax, jax.numpy as jnp
        import numpy as np
        B, T, C = (8, 512, 256)
        E, K = (8, 2)
        H = 4 * C
        CAP_FACTOR = 1.2
        EPS = 1e-09
        Bb, Tt, Cc = x.shape
        N = Bb * Tt
        KN = K * N
        capacity = int(CAP_FACTOR * (N // E + 1))
        xf = x.reshape(N, Cc)
        logits = xf @ router_w.T + router_b
        probs = jax.nn.softmax(logits, axis=-1)
        top_vals, top_inds = jax.lax.top_k(probs, K)
        top_vals = top_vals / (jnp.sum(top_vals, axis=-1, keepdims=True) + EPS)
        e_flat = top_inds.T.reshape(-1)
        w_flat = top_vals.T.reshape(-1)
        valid = w_flat > EPS
        onehot = (e_flat[:, None] == jnp.arange(E)[None, :]) & valid[:, None]
        pos = jnp.cumsum(onehot.astype(jnp.int32), axis=0) - 1
        pos_own = jnp.take_along_axis(pos, e_flat[:, None], axis=1)[:, 0]
        keep = valid & (pos_own < capacity)
        scores = jnp.where(keep[None, :] & (e_flat[None, :] == jnp.arange(E)[:, None]), jnp.arange(KN)[None, :], KN)
        sel = jnp.sort(scores, axis=1)[:, :capacity]
        slot_valid = sel < KN
        sel_c = jnp.where(slot_valid, sel, 0)
        tok = sel_c % N
        wgt = jnp.where(slot_valid, w_flat[sel_c], 0.0)
        toks = xf[tok]
        h = jax.nn.gelu(jnp.einsum('etc,ehc->eth', toks, fc1_w) + fc1_b[:, None, :], approximate=False)
        y = jnp.einsum('eth,ech->etc', h, fc2_w) + fc2_b[:, None, :]
        y = toks + y * layer_scale[:, None, :]
        out = jnp.zeros((N, Cc), dtype=x.dtype)
        out = out.at[tok.reshape(-1)].add((wgt[..., None] * y).reshape(-1, Cc))
        return out.reshape(Bb, Tt, Cc)

    def _L1_xattn_ref(query, key_value, Wq, bq, Wk, bk, Wv, bv, Wo, bo):
        import jax, jax.numpy as jnp
        import numpy as np
        D_MODEL = 256
        NUM_HEADS = 16
        HEAD_DIM = D_MODEL // NUM_HEADS
        B, SQ, _ = query.shape
        SKV = key_value.shape[1]
        Q = query @ Wq.T + bq
        K = key_value @ Wk.T + bk
        V = key_value @ Wv.T + bv
        Q = Q.reshape(B, SQ, NUM_HEADS, HEAD_DIM).transpose(0, 2, 1, 3)
        K = K.reshape(B, SKV, NUM_HEADS, HEAD_DIM).transpose(0, 2, 1, 3)
        V = V.reshape(B, SKV, NUM_HEADS, HEAD_DIM).transpose(0, 2, 1, 3)
        scores = jnp.einsum('bhqd,bhkd->bhqk', Q, K) / np.sqrt(HEAD_DIM)
        causal = jnp.tril(jnp.ones((SQ, SKV), bool))
        scores = jnp.where(causal[None, None], scores, -jnp.inf)
        attn = jax.nn.softmax(scores, axis=-1)
        out = jnp.einsum('bhqk,bhkd->bhqd', attn, V)
        out = out.transpose(0, 2, 1, 3).reshape(B, SQ, D_MODEL)
        return out @ Wo.T + bo

    def _L1_ffn_ref(x, gate_w, bias, W1, W3, W2, sw1, sw3, sw2):
        import jax, jax.numpy as jnp
        import numpy as np
        D = 256
        I = 128
        E = 32
        K = 4
        T = 2 * 512
        C = 2 * T * K // E
        X = x.reshape(-1, D)
        logits = (X @ gate_w.T).astype(jnp.float32)
        scores = jax.nn.sigmoid(logits)
        _, idx = jax.lax.top_k(scores + bias[None, :], K)
        w = jnp.take_along_axis(scores, idx, axis=-1)
        w = w / jnp.clip(jnp.sum(w, axis=-1, keepdims=True), 1e-12, None)
        w = w.astype(x.dtype)
        eid = idx.reshape(-1)
        onehot = (eid[:, None] == jnp.arange(E)[None, :]).astype(jnp.int32)
        pos = jnp.take_along_axis(jnp.cumsum(onehot, axis=0) - 1, eid[:, None], axis=1)[:, 0]
        valid = pos < C
        posc = jnp.minimum(pos, C - 1)
        Xrep = jnp.repeat(X, K, axis=0)
        xe = jnp.zeros((E, C, D), x.dtype).at[eid, posc].add(jnp.where(valid[:, None], Xrep, jnp.zeros((), x.dtype)))
        h = jax.nn.silu(jnp.einsum('ecd,edi->eci', xe, W1)) * jnp.einsum('ecd,edi->eci', xe, W3)
        ye = jnp.einsum('eci,eid->ecd', h, W2)
        gflat = jnp.where(valid, w.reshape(-1), jnp.zeros((), x.dtype))
        yrows = ye[eid, posc] * gflat[:, None]
        out = yrows.reshape(-1, K, D).sum(axis=1)
        out = out + jax.nn.silu(X @ sw1.T) * (X @ sw3.T) @ sw2.T
        return out.reshape(x.shape)
    x = x + _L0_xattn_ref(_layernorm(x, axis=-1), ctx_1024, L0_xattn_w_sim, L0_xattn_b_sim, L0_xattn_W_qv, L0_xattn_b_qv)
    x = x + _L0_ffn_ref(_layernorm(x, axis=-1), L0_ffn_router_w, L0_ffn_router_b, L0_ffn_fc1_w, L0_ffn_fc1_b, L0_ffn_fc2_w, L0_ffn_fc2_b, L0_ffn_layer_scale)
    x = x + _L1_xattn_ref(_layernorm(x, axis=-1), ctx_1024, L1_xattn_Wq, L1_xattn_bq, L1_xattn_Wk, L1_xattn_bk, L1_xattn_Wv, L1_xattn_bv, L1_xattn_Wo, L1_xattn_bo)
    x = x + _L1_ffn_ref(_layernorm(x, axis=-1), L1_ffn_gate_w, L1_ffn_bias, L1_ffn_W1, L1_ffn_W3, L1_ffn_W2, L1_ffn_sw1, L1_ffn_sw3, L1_ffn_sw2)
    return x

_drawn_inputs = setup_inputs


def setup_inputs(seed=0):
    import zlib

    import numpy as np

    out = dict(_drawn_inputs(seed))
    spreads = {'L0_ffn_router_b': (0.0, 0.1),
     'L0_ffn_fc1_b': (0.0, 0.8),
     'L0_ffn_fc2_b': (0.0, 0.8),
     'L0_ffn_layer_scale': (0.10000000149011612, 0.6),
     'L1_xattn_bq': (0.0, 0.63),
     'L1_xattn_bk': (0.0, 0.8),
     'L1_xattn_bv': (0.0, 0.1),
     'L1_xattn_bo': (0.0, 0.1),
     'L1_ffn_bias': (0.0, 0.8)}
    factors = {'L0_ffn_fc1_w': 2.877,
     'L1_ffn_gate_w': 8.0,
     'L1_ffn_W1': 8.0,
     'L1_ffn_W3': 8.0,
     'L1_ffn_W2': 8.0,
     'L1_ffn_sw1': 8.0,
     'L1_ffn_sw3': 8.0,
     'L1_ffn_sw2': 8.0}
    for name, (base, spread) in spreads.items():
        noise = np.random.default_rng([zlib.crc32(name.encode()), seed]).standard_normal(out[name].shape)
        drawn = base * np.exp(spread * noise) if base else spread * noise
        out[name] = jnp.asarray(drawn.astype(out[name].dtype))
    for name, factor in factors.items():
        out[name] = (out[name] * factor).astype(out[name].dtype)
    return out
```

```python
import concourse.bass as bass
from concourse import mybir
from contextlib import ExitStack

F32, F32R, BF16 = mybir.dt.float32, mybir.dt.float32r, mybir.dt.bfloat16
I32, U32 = mybir.dt.int32, mybir.dt.uint32
ALU, ACT, AX = mybir.AluOpType, mybir.ActivationFunctionType, mybir.AxisListType

P = 128
BATCH, SEQ, D = 16, 256, 256
CTX = 120
DC = D // P
HALVES = SEQ // P
TILES = BATCH * HALVES
TOKENS = BATCH * SEQ
LN_EPS = 1e-5
E0, HID0, TOP0, W_EPS = 8, 1024, 2, 1e-9
CAP0 = int(1.2 * (TOKENS // E0 + 1))
SLOT_TILES0 = -(-CAP0 // P)
SLOTS0 = SLOT_TILES0 * P
HALF0 = SLOTS0 // 2
HC0 = HID0 // P
HI0 = E0 * SLOT_TILES0
HEADS, HD = 16, 16
HPC = P // HD
HPB = 4
GROUPS = HEADS // HPB
SCALE = HD ** -0.5
MASKED = -1e30
E1, INNER, TOP1 = 32, 128, 4
CAP1 = 2 * 1024 * TOP1 // E1
SLOTS1 = E1 * CAP1
SLOT_TILES1 = CAP1 // P
DROPPED = 1 << 20
ROW = D + 16
C_TOK, C_W, C_E = D, D + 1, D + 1 + TOP1
K_ID, K_SU, K_IOTA, K_P, K_HEAD, K_CAUSAL, K_END = 0, 128, 256, 384, 385, 400, 520


class At:

    def __init__(self, n, half, par):
        self.n, self.h, self.p = n, half, par


def wait(eng, sem, count):
    if not isinstance(count, int) or count > 0:
        eng.wait_ge(sem, count)


def pipelined(eng, stages, n, base=0):
    lag = len(stages) - 1
    first = (lag + 3) // 2 * 2
    pairs = (n - first) // 2

    def peeled(s):
        for k, stage in reversed(list(enumerate(stages))):
            if 0 <= s - k < n:
                stage(At(base + s - k, (base + s - k) // 2, (s - k) % 2))

    for s in range(first):
        peeled(s)
    if pairs:
        with eng.Fori(0, pairs) as i:
            for u in range(2):
                for k, stage in reversed(list(enumerate(stages))):
                    stage(At(i * 2 + (base + first + u - k), i + (base + first + u - k) // 2, (u - k) % 2))
    for s in range(first + 2 * pairs, n + lag):
        peeled(s)


def build(nc, a, out, upto=4, dbg=None):
    ctx = ExitStack()
    with ctx:
        def sb(name, shape, dt):
            return ctx.enter_context(nc.sbuf_tensor(name, shape, dt))

        x_res = sb("x_res", [P, TILES, D], F32)
        consts = sb("consts", [P, K_END], F32)
        tri_bf = sb("tri_bf", [P, P], BF16)
        ones_bf = sb("ones_bf", [P, P], BF16)
        logits = sb("logits", [P, TILES, E0], F32)
        top2 = sb("top2", [P, TILES, TOP0], F32)
        exp2 = sb("exp2", [P, TILES, TOP0], F32)
        w_own = sb("w_own", [P, TILES, TOP0], F32)
        slot_own = sb("slot_own", [P, TILES, TOP0], U32)
        gate = ctx.enter_context(nc.semaphore("gate"))

        xn1_d = nc.dram_tensor("xn1_d", (TOKENS, D), F32).ap()
        y0_d = nc.dram_tensor("y0_d", (E0 * SLOTS0, D), F32).ap()
        rows_d = nc.dram_tensor("rows_d", (SLOTS1, ROW), F32).ap()
        xn3_d = nc.dram_tensor("xn3_d", (TOKENS, D), F32).ap()
        env = dict(locals())
        env["sems"] = []
        for phase in (phase_attend, phase_experts, phase_heads, phase_moe)[:upto]:
            phase(nc, env)
            nc.clear_and_free_semaphores(env["sems"])
            nc.all_engine_barrier()
            env["sems"] = []
        if dbg:
            dbg(nc, env)


def wait_apart(eng, sem, count, gate):
    if not isinstance(count, int) or count > 0:
        eng.wait_ge(sem, count)
        if not isinstance(count, int):
            apart(eng, gate)


def apart(eng, gate):
    eng.sem_inc(gate, 1)


def phase_attend(nc, env):
    a, x_res, consts, tri_bf, ones_bf = (env[k] for k in ("a", "x_res", "consts", "tri_bf", "ones_bf"))
    logits, top2, exp2, gate, xn1_d, rows_d = (env[k] for k in ("logits", "top2", "exp2", "gate", "xn1_d", "rows_d"))
    ctx = ExitStack()
    with ctx:
        def sb(name, shape, dt):
            return ctx.enter_context(nc.sbuf_tensor("a_" + name, shape, dt))

        def two(name, shape, dt):
            return [sb(f"{name}{i}", shape, dt) for i in range(2)]

        def sem(name):
            env["sems"].append(nc.alloc_semaphore(name="a_" + name))
            return env["sems"][-1]

        def bank(name, shape, dt=F32):
            return ctx.enter_context(nc.psum_tensor("a_" + name, shape, dt))

        ident = consts[:, K_ID:K_ID + P]
        wqv = sb("wqv", [P, 4 * DC, D], F32)
        wqv_hi = sb("wqv_hi", [P, 2 * DC, D], F32R)
        wqv_lo = sb("wqv_lo", [P, 2 * DC, D], F32R)
        bqv = sb("bqv", [P, HALVES, D], F32)
        wsim = sb("wsim", [P, 3, DC], F32)
        bsim = sb("bsim", [P, 1], F32)
        w2rep = sb("w2rep", [P, DC, P], F32)
        ones_row = sb("ones_row", [1, P], F32)
        router_w = sb("router_w", [P, DC, E0], F32)
        router_b = sb("router_b", [P, E0], F32)
        empty_rows = sb("empty_rows", [P, SLOT_TILES1, ROW], F32)
        cn = two("cn", [CTX, D], F32)
        ct = two("ct", [P, DC, CTX], F32)
        stats = two("stats", [P, HALVES, 6], F32)
        mv = two("mv", [P, HALVES, 2], F32)
        rstd = two("rstd", [P, HALVES], F32)
        newton = two("newton", [P, HALVES], F32)
        lnv = two("lnv", [P, HALVES], F32)
        xn = two("xn", [P, HALVES, D], F32)
        enc_t = two("enc_t", [P, DC, SEQ], F32)
        enc_hi = two("enc_hi", [P, DC, SEQ], F32R)
        enc_lo = two("enc_lo", [P, DC, SEQ], F32R)
        simw = two("simw", [P, DC, CTX], F32)
        rowb = two("rowb", [P, CTX], F32)
        sim = two("sim", [P, HALVES, CTX], F32)
        mx = two("mx", [P, HALVES], F32)
        nmx = two("nmx", [P, HALVES], F32)
        probs = two("probs", [P, HALVES, CTX], F32)
        psums = two("psums", [P, HALVES], F32)
        prec = two("prec", [P, HALVES], F32)
        probs_n = two("probs_n", [P, HALVES, CTX], F32)
        gm = two("gm", [1, 1], F32)
        ngm = two("ngm", [1, 1], F32)
        brow = two("brow", [1, SEQ], F32)
        bsum = two("bsum", [1, 1], F32)
        brec = two("brec", [1, 1], F32)
        brow_n = two("brow_n", [1, SEQ], F32)
        bjunk = two("bjunk", [P, DC, SEQ], F32)
        hc = two("hc", [P, DC], F32)
        wc = two("wc", [P, DC, D], F32)
        wc_hi = two("wc_hi", [P, DC, D], F32R)
        wc_lo = two("wc_lo", [P, DC, D], F32R)
        at_sb = two("at_sb", [CTX, SEQ], F32)
        hq_hi = two("hq_hi", [P, DC, SEQ], F32R)
        hq_lo = two("hq_lo", [P, DC, SEQ], F32R)
        prod = two("prod", [P, DC, SEQ], F32)
        prod_hi = two("prod_hi", [P, DC, SEQ], F32R)
        prod_lo = two("prod_lo", [P, DC, SEQ], F32R)
        xsum = two("xsum", [P, HALVES, D], F32)
        stats1 = two("stats1", [P, HALVES, 6], F32)
        mv1 = two("mv1", [P, HALVES, 2], F32)
        rstd1 = two("rstd1", [P, HALVES], F32)
        newton1 = two("newton1", [P, HALVES], F32)
        lnv1 = two("lnv1", [P, HALVES], F32)
        eps = sb("eps", [P, 1], F32)
        xn1 = two("xn1", [P, HALVES, D], F32)
        x1_t = two("x1_t", [P, DC, SEQ], F32)
        lg = two("lg", [P, HALVES, E0], F32)
        mx8 = two("mx8", [P, HALVES, 8], F32)
        ix8 = two("ix8", [P, HALVES, 8], U32)

        ps_enc = bank("ps_enc", [P, DC, SEQ])
        ps_sim = bank("ps_sim", [P, 4, P])
        ps_row = bank("ps_row", [P, 512])
        ps_bc = bank("ps_bc", [P, 512])
        ps_at = bank("ps_at", [P, 512])
        ps_hq = bank("ps_hq", [P, DC, SEQ])
        ps_out = bank("ps_out", [P, HALVES, D])
        ps_x1 = bank("ps_x1", [P, DC, SEQ])

        s_const, s_par, s_prep, s_empty, s_rows = (sem(n) for n in ("s_const", "s_par", "s_prep", "s_empty", "s_rows"))
        s_w2, s_wqh, s_wql, s_zero = (sem(n) for n in ("s_w2", "s_wqh", "s_wql", "s_zero"))
        loaded = [sem("loaded0"), sem("loaded1")]
        stored = [sem("stored0"), sem("stored1")]
        (st_done, mv_done, rs_done, xn_done, simw_done, enc_ps, enc_sb, enc_h, enc_l, sim_ps, rowb_done, sim_done,
         mx_done, nmx_done, exp_done, prec_done, pn_done, row_ps, gm_done, ngm_done, brow_done, brec_done, bn_done,
         bc_ps, hc_done, wc_done, wch_done, wcl_done, at_ps, at_done, hq_ps, hqh_done, hql_done, pr_done, prh_done,
         prl_done, out_ps, xs_done, x1_done, st1_done, mv1_done, rs1_done, xn1_done, x1t_ps, x1t_sb, lg_ps, lg_done,
         mx8_done, ix8_done, keep_done, ln_done, ln1_done, nw_done, nw1_done) = (sem(n) for n in (
             "st_done mv_done rs_done xn_done simw_done enc_ps enc_sb enc_h enc_l sim_ps rowb_done sim_done "
             "mx_done nmx_done exp_done prec_done pn_done row_ps gm_done ngm_done brow_done brec_done bn_done "
             "bc_ps hc_done wc_done wch_done wcl_done at_ps at_done hq_ps hqh_done hql_done pr_done prh_done "
             "prl_done out_ps xs_done x1_done st1_done mv1_done rs1_done xn1_done x1t_ps x1t_sb lg_ps lg_done "
             "mx8_done ix8_done keep_done ln_done ln1_done nw_done nw1_done").split())
        LOADS = 3 * 16

        def tiles(t):
            return x_res[:, bass.ds(t.n * HALVES, HALVES), :]

        block = ctx.enter_context(nc.Block())

        @block.sync
        def _(sp):
            sp.dma_start(consts[:], a["consts"]).then_inc(s_const, 16)
            sp.dma_start(wsim[:], a["wsim"]).then_inc(s_par, 16)
            sp.dma_start(bsim[:], a["b_sim"].partition_broadcast(P)).then_inc(s_par, 16)

            def load(t):
                wait_apart(sp, loaded[t.p], t.h * LOADS, gate)
                wait_apart(sp, hq_ps, t.n - 1, gate)
                wait_apart(sp, sim_ps, t.n - 1, gate)
                wait_apart(sp, simw_done, (t.n - 1) * DC, gate)
                sp.dma_start(tiles(t), a["x"][:, bass.ds(t.n * HALVES, HALVES), :]).then_inc(loaded[t.p], 16)
                sp.dma_start(cn[t.p][:], a["ctx"][bass.ds(t.n, 1)].rearrange("a j d -> (a j) d")).then_inc(loaded[t.p], 16)
                sp.dma_start(ct[t.p][:], a["ctx_t"][bass.ds(t.n, 1)].rearrange("a p k j -> (a p) k j")).then_inc(loaded[t.p], 16)

            def first_loads():
                load(At(0, 0, 0))
                sp.dma_start(wqv[:], a["wqv"]).then_inc(s_par, 16)
                sp.dma_start(bqv[:], a["bqv2"].partition_broadcast(P)).then_inc(s_par, 16)
                sp.dma_start(router_w[:], a["router_w"]).then_inc(s_par, 16)
                sp.dma_start(router_b[:], a["router_b"].partition_broadcast(P)).then_inc(s_par, 16)
                load(At(1, 0, 1))

            def fetch(t):
                if not isinstance(t.n, int) or t.n >= 2:
                    load(t)

            def store(t):
                wait_apart(sp, stored[t.p], t.h * 16, gate)
                wait_apart(sp, xn1_done, (t.n + 1) * HALVES, gate)
                sp.dma_start(xn1_d.rearrange("(t p) d -> p t d", p=P)[:, bass.ds(t.n * HALVES, HALVES), :],
                             xn1[t.p][:]).then_inc(stored[t.p], 16)

            def nothing(t):
                pass

            first_loads()
            pipelined(sp, [fetch, nothing, nothing, store], BATCH)
            sp.wait_ge(s_empty, 2)
            for c in range(SLOT_TILES1):
                sp.dma_start(rows_d.rearrange("(e c p) r -> c p e r", c=SLOT_TILES1, p=P)[c],
                             empty_rows[:, c:c + 1, :].to_broadcast([P, E1, ROW])).then_inc(s_rows, 16)
            sp.wait_ge(s_rows, SLOT_TILES1 * 16)
            sp.wait_ge(stored[0], BATCH // 2 * 16)
            sp.wait_ge(stored[1], BATCH // 2 * 16)

        @block.gpsimd
        def _(pool):
            pool.memset(empty_rows[:], 0.0).then_inc(s_zero, 1)
            pool.wait_ge(s_const, 16)
            pool.wait_ge(s_zero, 1)
            for c in range(SLOT_TILES1):
                pool.tensor_scalar(empty_rows[:, c, C_TOK:C_TOK + 1], consts[:, K_P:K_P + 1],
                                   float(TOKENS + c * P), None, ALU.add).then_inc(s_empty, 1)
            pool.wait_ge(s_par, 6 * 16)
            pool.wait_ge(s_wqh, 1)
            pool.tensor_tensor(wqv_lo[:], wqv[:, DC:3 * DC, :], wqv_hi[:], ALU.subtract).then_inc(s_wql, 1)

            def split_enc(t):
                wait(pool, enc_sb, t.n + 1)
                wait(pool, enc_h, t.n + 1)
                wait(pool, out_ps, t.n - 1)
                pool.tensor_tensor(enc_lo[t.p][:], enc_t[t.p][:], enc_hi[t.p][:], ALU.subtract).then_inc(enc_l, 1)

            def split_wc(t):
                wait(pool, wc_done, (t.n + 1) * DC)
                wait(pool, wch_done, t.n + 1)
                wait(pool, out_ps, t.n - 1)
                pool.tensor_tensor(wc_lo[t.p][:], wc[t.p][:], wc_hi[t.p][:], ALU.subtract).then_inc(wcl_done, 1)

            def split_prod(t):
                wait(pool, pr_done, t.n + 1)
                wait(pool, prh_done, t.n + 1)
                wait(pool, out_ps, t.n - 1)
                pool.tensor_tensor(prod_lo[t.p][:], prod[t.p][:], prod_hi[t.p][:], ALU.subtract).then_inc(prl_done, 1)

            def split_b(t):
                split_enc(t)
                split_wc(t)
                split_prod(t)

            def nothing(t):
                pass

            pipelined(pool, [nothing, split_b], BATCH)

        @block.tensor
        def _(pe):
            pe.wait_ge(s_const, 16)

            def norm_and_sim(t):
                wait(pe, xn_done, (t.n + 1) * HALVES)
                wait(pe, enc_sb, t.n)
                wait(pe, enc_h, t.n)
                for s in range(HALVES):
                    for k in range(DC):
                        mm = pe.transpose(ps_enc[:, k, s * P:(s + 1) * P], xn[t.p][:, s, k * P:(k + 1) * P], ident)
                mm.then_inc(enc_ps, 1)
                wait(pe, simw_done, (t.n + 1) * DC)
                wait(pe, rowb_done, t.n)
                wait(pe, sim_done, t.n * HALVES)
                pe.wait_ge(s_w2, DC)
                for k in range(DC):
                    pe.matmul(ps_sim[:, 2, 0:CTX], w2rep[:, k, :], ct[t.p][:, k, :], start=k == 0, stop=k == DC - 1)
                wait(pe, enc_sb, t.n + 1)
                for s in range(HALVES):
                    for k in range(DC):
                        mm = pe.matmul(ps_sim[:, s, 0:CTX], enc_t[t.p][:, k, s * P:(s + 1) * P], simw[t.p][:, k, :],
                                       start=k == 0, stop=k == DC - 1)
                mm.then_inc(sim_ps, 1)

            def attend(t):
                wait(pe, mx_done, t.n + 1)
                wait(pe, gm_done, t.n)
                wait(pe, brow_done, t.n)
                for s in range(HALVES):
                    mm = pe.matmul(ps_row[0:1, s * P:(s + 1) * P], mx[t.p][:, s:s + 1], ident, start=True, stop=True)
                mm.then_inc(row_ps, 1)
                wait(pe, pn_done, (t.n + 1) * HALVES)
                wait(pe, at_done, t.n)
                for s in range(HALVES):
                    mm = pe.transpose(ps_at[0:CTX, s * P:(s + 1) * P], probs_n[t.p][:, s, :], ident)
                mm.then_inc(at_ps, 1)
                wait(pe, at_done, t.n + 1)
                wait(pe, hql_done, t.n)
                wait(pe, pr_done, t.n)
                for k in range(DC):
                    mm = pe.matmul(ps_hq[:, k, :], cn[t.p][:, k * P:(k + 1) * P], at_sb[t.p][:], start=True, stop=True)
                mm.then_inc(hq_ps, 1)
                wait(pe, bn_done, t.n + 1)
                wait(pe, hc_done, t.n * DC)
                pe.matmul(ps_bc[:, 0:SEQ], ones_row[:], brow_n[t.p][:], start=True, stop=True).then_inc(bc_ps, 1)

            def project(t):
                wait(pe, xs_done, t.n)
                wait(pe, hqh_done, t.n + 1)
                wait(pe, hql_done, t.n + 1)
                wait(pe, prh_done, t.n + 1)
                wait(pe, enc_l, t.n + 1)
                wait(pe, wch_done, t.n + 1)
                wait(pe, prl_done, t.n + 1)
                wait(pe, wcl_done, t.n + 1)
                pe.wait_ge(s_wql, 1)
                for s in range(HALVES):
                    n = 0
                    for k in range(DC):
                        for xh, xl, wh, wl in ((hq_hi[t.p], hq_lo[t.p], wqv_hi[:, k, :], wqv_lo[:, k, :]),
                                               (enc_hi[t.p], enc_lo[t.p], wc_hi[t.p][:, k, :], wc_lo[t.p][:, k, :]),
                                               (prod_hi[t.p], prod_lo[t.p], wqv_hi[:, DC + k, :], wqv_lo[:, DC + k, :])):
                            for l, r in ((xh, wh), (xh, wl), (xl, wh)):
                                mm = pe.matmul(ps_out[:, s, :], l[:, k, s * P:(s + 1) * P], r, start=n == 0, stop=n == 9 * DC - 1)
                                n += 1
                mm.then_inc(out_ps, 1)

            def router(t):
                wait(pe, xn1_done, (t.n + 1) * HALVES)
                wait(pe, x1t_sb, t.n)
                wait(pe, lg_done, t.n * HALVES)
                for s in range(HALVES):
                    for k in range(DC):
                        mm = pe.transpose(ps_x1[:, k, s * P:(s + 1) * P], xn1[t.p][:, s, k * P:(k + 1) * P], ident)
                mm.then_inc(x1t_ps, 1)
                wait(pe, x1t_sb, t.n + 1)
                for s in range(HALVES):
                    for k in range(DC):
                        mm = pe.matmul(ps_x1[:, 0, s * E0:(s + 1) * E0], x1_t[t.p][:, k, s * P:(s + 1) * P], router_w[:, k, :],
                                       start=k == 0, stop=k == DC - 1)
                mm.then_inc(lg_ps, 1)

            pipelined(pe, [norm_and_sim, attend, project, router], BATCH)

        @block.scalar
        def _(act):
            act.preload_act_table_set("natural_log_exp_and_others")
            act.wait_ge(s_par, 6 * 16)
            act.wait_ge(s_prep, 4)
            act.activation(wqv_hi[:], wqv[:, DC:3 * DC, :], ACT.Copy).then_inc(s_wqh, 1)

            def root(t, m, lv, r, m_s, l_s, r_s, nw_s):
                wait(act, m_s, (t.n + 1) * HALVES)
                wait(act, nw_s, (t.n - 1) * 3)
                act.activation(lv[t.p][:], m[t.p][:, :, 1], ACT.Ln, bias=eps[:]).then_inc(l_s, 1)
                wait(act, l_s, t.n + 1)
                act.activation(r[t.p][:], lv[t.p][:], ACT.Exp, scale=-0.5).then_inc(r_s, 1)

            def sims(t):
                root(t, mv, lnv, rstd, mv_done, ln_done, rs_done, nw_done)
                wait(act, enc_ps, t.n + 1)
                wait(act, sim_ps, t.n - 1)
                wait(act, hc_done, (t.n - 1) * DC)
                wait(act, pr_done, t.n - 1)
                wait(act, enc_l, t.n - 1)
                act.activation(enc_t[t.p][:], ps_enc[:], ACT.Copy).then_inc(enc_sb, 1)
                wait(act, out_ps, t.n - 1)
                act.activation(enc_hi[t.p][:], ps_enc[:], ACT.Copy).then_inc(enc_h, 1)
                wait(act, sim_ps, t.n + 1)
                wait(act, sim_done, (t.n - 1) * HALVES)
                act.activation(rowb[t.p][:], ps_sim[:, 2, 0:CTX], ACT.Identity, bias=bsim[:]).then_inc(rowb_done, 1)
                wait(act, nmx_done, t.n + 1)
                wait(act, sim_done, (t.n + 1) * HALVES)
                wait(act, pn_done, (t.n - 1) * HALVES)
                wait(act, prec_done, t.n - 1)
                for s in range(HALVES):
                    act.activation(probs[t.p][:, s, :], sim[t.p][:, s, :], ACT.Exp, bias=nmx[t.p][:, s:s + 1],
                                   accum_out=psums[t.p][:, s:s + 1]).then_inc(exp_done, 1)

            def parts(t):
                wait(act, row_ps, t.n + 1)
                wait(act, ngm_done, t.n + 1)
                wait(act, bn_done, t.n - 1)
                wait(act, brec_done, t.n - 1)
                act.activation(brow[t.p][:], ps_row[0:1, 0:SEQ], ACT.Exp, bias=ngm[t.p][:], accum_out=bsum[t.p][:]).then_inc(brow_done, 1)
                wait(act, at_ps, t.n + 1)
                wait(act, hq_ps, t.n - 1)
                act.activation(at_sb[t.p][:], ps_at[0:CTX, 0:SEQ], ACT.Copy).then_inc(at_done, 1)
                wait(act, hq_ps, t.n + 1)
                wait(act, out_ps, t.n - 1)
                wait(act, hql_done, t.n - 1)
                act.activation(hq_hi[t.p][:], ps_hq[:], ACT.Copy).then_inc(hqh_done, 1)
                wait(act, pr_done, t.n + 1)
                wait(act, prl_done, t.n - 1)
                act.activation(prod_hi[t.p][:], prod[t.p][:], ACT.Copy).then_inc(prh_done, 1)
                wait(act, wc_done, (t.n + 1) * DC)
                wait(act, wcl_done, t.n - 1)
                act.activation(wc_hi[t.p][:], wc[t.p][:], ACT.Copy).then_inc(wch_done, 1)

            def root1(t):
                root(t, mv1, lnv1, rstd1, mv1_done, ln1_done, rs1_done, nw1_done)

            def turned(t):
                wait(act, x1t_ps, t.n + 1)
                wait(act, lg_ps, t.n - 1)
                act.activation(x1_t[t.p][:], ps_x1[:], ACT.Copy).then_inc(x1t_sb, 1)

            pipelined(act, [sims, parts, root1, turned], BATCH)

        @block.vector
        def _(ve):
            ve.memset(ones_bf[:], 1.0).then_inc(s_prep, 1)
            ve.memset(w2rep[:], 1.0).then_inc(s_prep, 1)
            ve.memset(ones_row[:], 1.0).then_inc(s_prep, 1)
            ve.memset(eps[:], LN_EPS).then_inc(s_prep, 1)
            ve.wait_ge(s_const, 16)
            ve.wait_ge(s_prep, 4)
            ve.tensor_copy(tri_bf[:], consts[:, K_SU:K_SU + P]).then_inc(s_prep, 1)
            ve.wait_ge(s_par, 6 * 16)
            for k in range(DC):
                ve.tensor_scalar(w2rep[:, k, :], w2rep[:, k, :], wsim[:, 1, k:k + 1], None, ALU.mult).then_inc(s_w2, 1)

            def norm(t, src, st, m, r, nw, dst, st_s, m_s, r_s, nw_s, dst_s):
                apart(ve, gate)
                for s in range(HALVES):
                    ve.bn_stats(st[t.p][:, s, :], src[:, s, :]).then_inc(st_s, 1)
                wait(ve, st_s, (t.n + 1) * HALVES)
                apart(ve, gate)
                for s in range(HALVES):
                    ve.bn_aggr(m[t.p][:, s, :], st[t.p][:, s, :]).then_inc(m_s, 1)
                wait(ve, r_s, t.n + 1)
                ve.scalar_tensor_tensor(nw[t.p][:], m[t.p][:, :, 1], LN_EPS, r[t.p][:], ALU.add, ALU.mult).then_inc(nw_s, 1)
                wait(ve, nw_s, t.n * 3 + 1)
                ve.scalar_tensor_tensor(nw[t.p][:], nw[t.p][:], -0.5, r[t.p][:], ALU.mult, ALU.mult).then_inc(nw_s, 1)
                wait(ve, nw_s, t.n * 3 + 2)
                ve.scalar_tensor_tensor(nw[t.p][:], nw[t.p][:], 1.5, r[t.p][:], ALU.add, ALU.mult).then_inc(nw_s, 1)
                wait(ve, nw_s, t.n * 3 + 3)
                for s in range(HALVES):
                    ve.tensor_scalar(dst[t.p][:, s, :], src[:, s, :], m[t.p][:, s, 0:1], nw[t.p][:, s:s + 1],
                                     ALU.subtract, ALU.mult).then_inc(dst_s, 1)

            def sims(t):
                wait(ve, loaded[t.p], (t.h + 1) * LOADS)
                wait(ve, sim_ps, t.n - 1)
                for k in range(DC):
                    ve.tensor_scalar(simw[t.p][:, k, :], ct[t.p][:, k, :], wsim[:, 2, k:k + 1], wsim[:, 0, k:k + 1],
                                     ALU.mult, ALU.add).then_inc(simw_done, 1)
                wait(ve, enc_ps, t.n - 1)
                norm(t, tiles(t), stats, mv, rstd, newton, xn, st_done, mv_done, rs_done, nw_done, xn_done)
                wait(ve, rowb_done, t.n + 1)
                wait(ve, exp_done, (t.n - 1) * HALVES)
                for s in range(HALVES):
                    ve.tensor_tensor(sim[t.p][:, s, :], ps_sim[:, s, 0:CTX], rowb[t.p][:], ALU.add).then_inc(sim_done, 1)
                wait(ve, sim_done, (t.n + 1) * HALVES)
                wait(ve, row_ps, t.n - 1)
                ve.tensor_reduce(mx[t.p][:], sim[t.p][:], AX.X, ALU.max).then_inc(mx_done, 1)
                wait(ve, mx_done, t.n + 1)
                ve.tensor_scalar(nmx[t.p][:], mx[t.p][:], -1.0, None, ALU.mult).then_inc(nmx_done, 1)

            def parts(t):
                wait(ve, exp_done, (t.n + 1) * HALVES)
                ve.reciprocal(prec[t.p][:], psums[t.p][:]).then_inc(prec_done, 1)
                wait(ve, prec_done, t.n + 1)
                wait(ve, at_ps, t.n - 1)
                for s in range(HALVES):
                    ve.tensor_scalar(probs_n[t.p][:, s, :], probs[t.p][:, s, :], prec[t.p][:, s:s + 1], None,
                                     ALU.mult).then_inc(pn_done, 1)
                wait(ve, row_ps, t.n + 1)
                ve.tensor_reduce(gm[t.p][:], ps_row[0:1, 0:SEQ], AX.X, ALU.max).then_inc(gm_done, 1)
                wait(ve, gm_done, t.n + 1)
                wait(ve, brow_done, t.n - 1)
                ve.tensor_scalar(ngm[t.p][:], gm[t.p][:], -1.0, None, ALU.mult).then_inc(ngm_done, 1)
                wait(ve, brow_done, t.n + 1)
                ve.reciprocal(brec[t.p][:], bsum[t.p][:]).then_inc(brec_done, 1)
                wait(ve, brec_done, t.n + 1)
                wait(ve, bc_ps, t.n - 1)
                ve.tensor_scalar(brow_n[t.p][:], brow[t.p][:], brec[t.p][:], None, ALU.mult).then_inc(bn_done, 1)
                wait(ve, hqh_done, t.n + 1)
                wait(ve, enc_sb, t.n + 1)
                wait(ve, prh_done, t.n - 1)
                wait(ve, prl_done, t.n - 1)
                ve.tensor_tensor(prod[t.p][:], ps_hq[:], enc_t[t.p][:], ALU.mult).then_inc(pr_done, 1)
                wait(ve, bc_ps, t.n + 1)
                for k in range(DC):
                    wait(ve, wc_done, (t.n - 1) * DC)
                    ve.tensor_tensor_reduce(bjunk[t.p][:, k, :], enc_t[t.p][:, k, :], ps_bc[:, 0:SEQ], 1.0, 0.0,
                                            ALU.mult, ALU.add, hc[t.p][:, k:k + 1]).then_inc(hc_done, 1)
                wait(ve, hc_done, (t.n + 1) * DC)
                wait(ve, wch_done, t.n - 1)
                wait(ve, wcl_done, t.n - 1)
                for k in range(DC):
                    ve.scalar_tensor_tensor(wc[t.p][:, k, :], wqv[:, 3 * DC + k, :], hc[t.p][:, k:k + 1], wqv[:, k, :],
                                            ALU.mult, ALU.add).then_inc(wc_done, 1)
                wait(ve, out_ps, t.n - 1)
                ve.tensor_tensor(hq_lo[t.p][:], ps_hq[:], hq_hi[t.p][:], ALU.subtract).then_inc(hql_done, 1)

            def add(t):
                wait(ve, out_ps, t.n + 1)
                ve.tensor_tensor(xsum[t.p][:], ps_out[:], bqv[:], ALU.add).then_inc(xs_done, 1)
                wait(ve, xs_done, t.n + 1)
                ve.tensor_tensor(tiles(t), tiles(t), xsum[t.p][:], ALU.add).then_inc(x1_done, 1)
                wait(ve, x1_done, t.n + 1)
                wait(ve, x1t_ps, t.n - 1)
                wait(ve, stored[t.p], t.h * 16)
                norm(t, tiles(t), stats1, mv1, rstd1, newton1, xn1, st1_done, mv1_done, rs1_done, nw1_done, xn1_done)

            def route(t):
                wait(ve, lg_ps, t.n + 1)
                wait(ve, ix8_done, (t.n - 1) * HALVES)
                for s in range(HALVES):
                    ve.tensor_tensor(lg[t.p][:, s, :], ps_x1[:, 0, s * E0:(s + 1) * E0], router_b[:],
                                     ALU.add).then_inc(lg_done, 1)
                wait(ve, lg_done, (t.n + 1) * HALVES)
                apart(ve, gate)
                for s in range(HALVES):
                    ve.max(mx8[t.p][:, s, :], lg[t.p][:, s, :]).then_inc(mx8_done, 1)
                wait(ve, mx8_done, (t.n + 1) * HALVES)
                apart(ve, gate)
                for s in range(HALVES):
                    ve.max_index(ix8[t.p][:, s, :], mx8[t.p][:, s, :], lg[t.p][:, s, :]).then_inc(ix8_done, 1)
                wait(ve, ix8_done, (t.n + 1) * HALVES)
                apart(ve, gate)
                own = bass.ds(t.n * HALVES, HALVES)
                ve.tensor_copy(logits[:, own, :], lg[t.p][:]).then_inc(keep_done, 1)
                ve.tensor_copy(top2[:, own, :], mx8[t.p][:, :, 0:TOP0]).then_inc(keep_done, 1)
                ve.tensor_copy(exp2[:, own, :], ix8[t.p][:, :, 0:TOP0]).then_inc(keep_done, 1)

            pipelined(ve, [sims, parts, add, route], BATCH)


def phase_experts(nc, env):
    a, consts, tri_bf, ones_bf, gate = (env[k] for k in ("a", "consts", "tri_bf", "ones_bf", "gate"))
    logits, top2, exp2, w_own, slot_own, xn1_d, y0_d = (env[k] for k in (
        "logits", "top2", "exp2", "w_own", "slot_own", "xn1_d", "y0_d"))
    NT = TOP0 * TILES
    ctx = ExitStack()
    with ctx:
        def sb(name, shape, dt):
            return ctx.enter_context(nc.sbuf_tensor("e_" + name, shape, dt))

        def two(name, shape, dt):
            return [sb(f"{name}{i}", shape, dt) for i in range(2)]

        def sem(name):
            env["sems"].append(nc.alloc_semaphore(name="e_" + name))
            return env["sems"][-1]

        ident = consts[:, K_ID:K_ID + P]
        expl = sb("expl", [P, TILES, E0], F32)
        zsum = sb("zsum", [P, TILES], F32)
        zrec = sb("zrec", [P, TILES], F32)
        pr = sb("pr", [P, TOP0, TILES], F32)
        den = sb("den", [P, TILES], F32)
        wt = sb("wt", [P, TOP0, TILES], F32)
        valid = sb("valid", [P, TOP0, TILES], F32)
        hot = sb("hot", [P, TOP0, TILES, E0], F32)
        hot_bf = sb("hot_bf", [P, NT * E0], BF16)
        total = sb("total", [P, NT * E0], F32)
        ran = sb("ran", [P, NT * E0], F32)
        ones_nt = sb("ones_nt", [P, NT], F32)
        before = sb("before", [P, NT * E0], F32)
        pos = sb("pos", [P, NT], F32)
        keep = sb("keep", [P, NT], F32)
        slot = sb("slot", [P, NT], F32)
        slot_i = sb("slot_i", [P, NT], I32)
        hi_i = sb("hi_i", [P, NT], I32)
        lo_i = sb("lo_i", [P, NT], I32)
        hi = sb("hi", [P, NT], F32)
        lo = sb("lo", [P, NT], F32)
        tile_no = sb("tile_no", [P, TILES], F32)
        in_lo = sb("in_lo", [P, TILES, P], BF16)
        xg_all = sb("xg_all", [P, 2, SLOT_TILES0, D], F32)
        hid_all = sb("hid_all", [P, 2, SLOTS0], F32)
        is_hi = hid_all[:].rearrange("p a b -> p (a b)").bitcast(BF16).rearrange("p (n h) -> p n h", h=HI0)
        in_hi = xg_all[:].rearrange("p a b c -> p (a b c)").bitcast(BF16).rearrange("p (n a h) -> p n a h", a=2, h=HI0)
        tok = sb("tok", [P, 2, HI0], F32)
        tok_of = sb("tok_of", [P, HI0], U32)
        fc1 = sb("fc1", [P, DC, HID0], F32)
        fc2 = sb("fc2", [P, HC0, D], F32)
        fc1_hi, fc1_lo = two("fc1_hi", [P, DC, HID0], F32R), two("fc1_lo", [P, DC, HID0], F32R)
        fc2_hi, fc2_lo = [sb("fc2_hi", [P, HC0, D], F32R)] * 2, [sb("fc2_lo", [P, HC0, D], F32R)] * 2
        b1 = two("b1", [P, HC0], F32)
        b2 = two("b2", [P, D], F32)
        ls = two("ls", [P, D], F32)
        b2ls = [sb("b2ls", [P, D], F32)] * 2
        own = two("own", [P, SLOT_TILES0], U32)
        xg = [xg_all[:, i] for i in range(2)]
        xt_hi, xt_lo = two("xt_hi", [P, DC, SLOTS0], F32R), two("xt_lo", [P, DC, SLOTS0], F32R)
        hid = [hid_all[:, i] for i in range(2)]
        hid_hi, hid_lo = sb("hid_hi", [P, HC0, SLOTS0], F32R), sb("hid_lo", [P, HC0, SLOTS0], F32R)
        ys = two("ys", [P, D], F32)
        yo = two("yo", [P, D], F32)

        ps_x = [ctx.enter_context(nc.psum_tensor(f"e_ps_x{i}", [P, 512], F32)) for i in range(2)]
        ps_f = [ctx.enter_context(nc.psum_tensor(f"e_ps_f{i}", [P, 2, 512], F32)) for i in range(2)]
        ps_y = [ctx.enter_context(nc.psum_tensor(f"e_ps_y{i}", [P, 512], F32)) for i in range(2)]

        s_chain, s_exp, s_hot, s_pre, s_oh, s_tok, s_own, s_tile = (sem(n) for n in (
            "s_chain", "s_exp", "s_hot", "s_pre", "s_oh", "s_tok", "s_own", "s_tile"))
        (w_ld, w_hi, w_lo, b_ld, b2_done, own_done, xt_ps, xth_done, xtl_done, f_ps, hid_done, hh_done, hl_done,
         y_ps, ys_done, yt_done, yo_done, w2_ld, w2_hi, w2_lo) = (sem(n) for n in (
             "w_ld w_hi w_lo b_ld b2_done own_done xt_ps xth_done xtl_done f_ps hid_done hh_done hl_done "
             "y_ps ys_done yt_done yo_done w2_ld w2_hi w2_lo").split())
        gathered = [sem("gathered0"), sem("gathered1")]
        y_st = [sem("y_st0"), sem("y_st1")]
        CH = HC0
        ST = SLOT_TILES0

        block = ctx.enter_context(nc.Block())

        @block.sync
        def _(sp):
            def load(t):
                e = bass.ds(t.n, 1)
                wait_apart(sp, w_ld, t.n * 16, gate)
                wait_apart(sp, w_hi, t.n, gate)
                wait_apart(sp, w_lo, t.n, gate)
                sp.dma_start(fc1[:], a["fc1_t"][e].rearrange("e p k h -> (e p) k h")).then_inc(w_ld, 16)
                wait_apart(sp, w2_ld, t.n * 16, gate)
                wait_apart(sp, w2_hi, t.n, gate)
                wait_apart(sp, w2_lo, t.n, gate)
                sp.dma_start(fc2[:], a["fc2_t"][e].rearrange("e p m c -> (e p) m c")).then_inc(w2_ld, 16)
                wait_apart(sp, b_ld, t.n * 48, gate)
                wait_apart(sp, hid_done, (t.n - 1) * CH, gate)
                wait_apart(sp, yo_done, (t.n - 1) * ST, gate)
                sp.dma_start(b1[t.p][:], a["fc1_b"][e].rearrange("e p m -> (e p) m")).then_inc(b_ld, 16)
                sp.dma_start(b2[t.p][:], a["fc2_b"][e].rearrange("e c -> (e c)").partition_broadcast(P)).then_inc(b_ld, 16)
                sp.dma_start(ls[t.p][:], a["ls"][e].rearrange("e c -> (e c)").partition_broadcast(P)).then_inc(b_ld, 16)

            def store(t):
                for c in range(ST):
                    q = (t.p * ST + c) % 2
                    wait_apart(sp, yo_done, t.n * ST + c + 1, gate)
                    sp.dma_start(y0_d.rearrange("(e c p) d -> c p e d", c=ST, p=P)[c][:, bass.ds(t.n, 1), :].rearrange("p e d -> p (e d)"),
                                 yo[q][:]).then_inc(y_st[q], 16)

            def nothing(t):
                pass

            pipelined(sp, [load, nothing, store], E0)
            for q in range(2):
                sp.wait_ge(y_st[q], E0 * ST // 2 * 16)

        @block.gpsimd
        def _(pool):
            pool.iota(tile_no[:], [[1, TILES]], base=0, channel_multiplier=0,
                      allow_small_or_imprecise_dtypes=True).then_inc(s_tile, 1)

            def gather(t):
                wait(pool, own_done, t.n + 1)
                wait(pool, xt_ps, (t.n - 1) * ST)
                wait(pool, yt_done, (t.n - 1) * ST)
                apart(pool, gate)
                for c in range(ST):
                    pool.indirect_dma_start(xg[t.p][:, c, :], None, xn1_d,
                                            bass.IndirectOffsetOnAxis(ap=own[t.p][:, c:c + 1], axis=0)
                                            ).then_inc(gathered[t.p], 16)

            def split(t):
                wait(pool, w_ld, (t.n + 1) * 16)
                wait(pool, w_hi, t.n + 1)
                wait(pool, f_ps, (t.n - 1) * CH)
                pool.tensor_tensor(fc1_lo[t.p][:], fc1[:], fc1_hi[t.p][:], ALU.subtract).then_inc(w_lo, 1)
                wait(pool, w2_ld, (t.n + 1) * 16)
                wait(pool, w2_hi, t.n + 1)
                wait(pool, y_ps, t.n * ST)
                pool.tensor_tensor(fc2_lo[t.p][:], fc2[:], fc2_hi[t.p][:], ALU.subtract).then_inc(w2_lo, 1)

            pipelined(pool, [gather, split], E0)

        @block.tensor
        def _(pe):
            pe.wait_ge(s_hot, 1)
            pe.matmul(ps_y[0][:], tri_bf[:], hot_bf[:], start=True, stop=True)
            pe.matmul(ps_y[1][:], ones_bf[:], hot_bf[:], start=True, stop=True).then_inc(s_pre, 1)
            for k in range(TOP0):
                pe.wait_ge(s_oh, k + 1)
                for n in range(TILES):
                    mm = pe.matmul(ps_x[0][:, 0:2 * HI0], in_lo[:, n, :],
                                   in_hi[:, k * TILES + n, :, :].rearrange("p a b -> p (a b)"),
                                   start=k == 0 and n == 0, stop=k == TOP0 - 1 and n == TILES - 1)
                mm.then_inc(s_tok, 1)

            def turn(t):
                wait(pe, gathered[t.p], (t.h + 1) * ST * 16)
                for c in range(ST):
                    q = (t.p * ST + c) % 2
                    wait(pe, xtl_done, t.n * ST + c - 1)
                    for k in range(DC):
                        mm = pe.transpose(ps_x[q][:, k * P:(k + 1) * P], xg[t.p][:, c, k * P:(k + 1) * P], ident)
                    mm.then_inc(xt_ps, 1)

            def up(t):
                wait(pe, xtl_done, (t.n + 1) * ST)
                wait(pe, w_lo, t.n + 1)
                for m in range(CH):
                    wait(pe, hid_done, t.n * CH + m - 1)
                    for n in range(2):
                        i = 0
                        for k in range(DC):
                            for l, r in ((fc1_hi, xt_hi), (fc1_hi, xt_lo), (fc1_lo, xt_hi)):
                                mm = pe.matmul(ps_f[m % 2][:, n, 0:HALF0], l[t.p][:, k, m * P:(m + 1) * P],
                                               r[t.p][:, k, n * HALF0:(n + 1) * HALF0], start=i == 0, stop=i == 3 * DC - 1)
                                i += 1
                    mm.then_inc(f_ps, 1)

            def down(t):
                wait(pe, w2_lo, t.n + 1)
                for c in range(ST):
                    q = (t.p * ST + c) % 2
                    wait(pe, ys_done, t.n * ST + c - 1)
                    i = 0
                    for m in range(CH):
                        if c == 0:
                            wait(pe, hl_done, t.n * CH + m + 1)
                        for l, r in ((hid_hi, fc2_hi), (hid_hi, fc2_lo), (hid_lo, fc2_hi)):
                            mm = pe.matmul(ps_y[q][:, 0:D], l[:, m, c * P:(c + 1) * P], r[t.p][:, m, :],
                                           start=i == 0, stop=i == 3 * CH - 1)
                            i += 1
                    mm.then_inc(y_ps, 1)

            def both(t):
                up(t)
                down(t)

            pipelined(pe, [turn, both], E0)

        @block.scalar
        def _(act):
            act.preload_act_table_set("exp_and_others")
            act.wait_ge(s_chain, 2)
            act.activation(expl[:], expl[:], ACT.Exp).then_inc(s_exp, 1)
            act.activation(pr[:, 1, :], pr[:, 1, :], ACT.Exp).then_inc(s_exp, 1)

            def split(t):
                wait(act, w_ld, (t.n + 1) * 16)
                wait(act, f_ps, (t.n - 1) * CH)
                wait(act, w_lo, t.n - 1)
                act.activation(fc1_hi[t.p][:], fc1[:], ACT.Copy).then_inc(w_hi, 1)
                wait(act, w2_ld, (t.n + 1) * 16)
                wait(act, y_ps, t.n * ST)
                wait(act, w2_lo, t.n)
                act.activation(fc2_hi[t.p][:], fc2[:], ACT.Copy).then_inc(w2_hi, 1)

            def turned(t):
                for c in range(ST):
                    q = (t.p * ST + c) % 2
                    wait(act, xt_ps, t.n * ST + c + 1)
                    if c == 0:
                        wait(act, f_ps, (t.n - 1) * CH)
                    act.activation(xt_hi[t.p][:, :, c * P:(c + 1) * P], ps_x[q][:, 0:DC * P].rearrange("p (k s) -> p k s", k=DC),
                                   ACT.Copy).then_inc(xth_done, 1)

            def gelu(t):
                wait(act, b_ld, (t.n + 1) * 48)
                for m in range(CH):
                    wait(act, f_ps, t.n * CH + m + 1)
                    wait(act, hl_done, t.n * CH + m - 1)
                    act.activation(hid[m % 2].rearrange("p (n s) -> p n s", n=2), ps_f[m % 2][:, :, 0:HALF0], ACT.Gelu,
                                   bias=b1[t.p][:, m:m + 1]).then_inc(hid_done, 1)

            def first(t):
                split(t)
                turned(t)

            pipelined(act, [first, gelu], E0)

        @block.vector
        def _(ve):
            n_chain = [0]

            def link(ins):
                n_chain[0] += 1
                ins.then_inc(s_chain, 1)
                ve.wait_ge(s_chain, n_chain[0])

            def wide(ap, n):
                return ap.unsqueeze(2).to_broadcast([P, TILES, n])

            ve.tensor_tensor(expl[:], logits[:], wide(top2[:, :, 0], E0), ALU.subtract).then_inc(s_chain, 1)
            n_chain[0] += 1
            link(ve.tensor_tensor(pr[:, 1, :], top2[:, :, 1], top2[:, :, 0], ALU.subtract))
            ve.memset(ones_nt[:], 1.0).then_inc(s_own, 1)
            ve.wait_ge(s_exp, 2)
            link(ve.tensor_reduce(zsum[:], expl[:], AX.X, ALU.add))
            link(ve.reciprocal(pr[:, 0, :], zsum[:]))
            link(ve.tensor_tensor(pr[:, 1, :], pr[:, 1, :], pr[:, 0, :], ALU.mult))
            link(ve.scalar_tensor_tensor(den[:], pr[:, 0, :], W_EPS, pr[:, 1, :], ALU.add, ALU.add))
            link(ve.reciprocal(zrec[:], den[:]))
            for k in range(TOP0):
                link(ve.tensor_tensor(wt[:, k, :], pr[:, k, :], zrec[:], ALU.mult))
            link(ve.tensor_scalar(valid[:], wt[:], W_EPS, None, ALU.is_gt))
            for k in range(TOP0):
                link(ve.tensor_tensor(hot[:, k], wide(exp2[:, :, k], E0),
                                      consts[:, K_IOTA:K_IOTA + E0].unsqueeze(1).to_broadcast([P, TILES, E0]), ALU.is_equal))
                link(ve.tensor_tensor(hot[:, k], hot[:, k], wide(valid[:, k, :], E0), ALU.mult))
            ve.tensor_copy(hot_bf[:], hot[:].rearrange("p k t e -> p (k t e)")).then_inc(s_hot, 1)
            ve.wait_ge(s_pre, 1)
            ve.wait_ge(s_own, 1)
            link(ve.tensor_copy(total[:], ps_y[1][:]))
            for e in range(E0):
                v = slice(e, NT * E0, E0)
                link(ve.tensor_tensor_scan(ran[:, v], ones_nt[:], total[:, v], 0.0, ALU.mult, ALU.add))
            link(ve.tensor_tensor(before[:], ran[:], total[:], ALU.subtract))
            link(ve.tensor_tensor(before[:], before[:], ps_y[0][:], ALU.add))
            link(ve.tensor_tensor(before[:], before[:], hot[:].rearrange("p k t e -> p (k t e)"), ALU.mult))
            link(ve.tensor_reduce(pos[:], before[:].rearrange("p (n e) -> p n e", e=E0), AX.X, ALU.add))
            link(ve.tensor_scalar(keep[:], pos[:], float(CAP0), None, ALU.is_lt))
            link(ve.tensor_tensor(keep[:], keep[:], valid[:].rearrange("p k t -> p (k t)"), ALU.mult))
            for k in range(TOP0):
                n = slice(k * TILES, (k + 1) * TILES)
                link(ve.scalar_tensor_tensor(slot[:, n], exp2[:, :, k], float(SLOTS0), pos[:, n], ALU.mult, ALU.add))
                link(ve.tensor_tensor(slot[:, n], slot[:, n], keep[:, n], ALU.mult))
                link(ve.tensor_copy(slot_own[:, :, k], slot[:, n]))
                link(ve.tensor_tensor(w_own[:, :, k], wt[:, k, :], keep[:, n], ALU.mult))
            link(ve.tensor_copy(slot_i[:], slot[:]))
            link(ve.tensor_scalar(hi_i[:], slot_i[:], 7, None, ALU.logical_shift_right))
            link(ve.tensor_scalar(lo_i[:], slot_i[:], P - 1, None, ALU.bitwise_and))
            link(ve.tensor_copy(hi[:], hi_i[:]))
            link(ve.tensor_copy(lo[:], lo_i[:]))
            link(ve.scalar_tensor_tensor(lo[:], lo[:], 1.0, keep[:], ALU.add, ALU.mult))
            link(ve.tensor_scalar(lo[:], lo[:], -1.0, None, ALU.add))
            link(ve.tensor_tensor(is_hi, hi[:].unsqueeze(2).to_broadcast([P, NT, HI0]),
                                  consts[:, K_IOTA:K_IOTA + HI0].unsqueeze(1).to_broadcast([P, NT, HI0]), ALU.is_equal))
            ve.wait_ge(s_tile, 1)
            for k in range(TOP0):
                n = slice(k * TILES, (k + 1) * TILES)
                link(ve.tensor_tensor(in_hi[:, n, 0, :], is_hi[:, n, :], wide(tile_no[:], HI0), ALU.mult))
            link(ve.tensor_scalar(in_hi[:, :, 1, :], is_hi, consts[:, K_P:K_P + 1], None, ALU.mult))
            for k in range(TOP0):
                if k:
                    ve.wait_ge(s_tok, k)
                ve.tensor_tensor(in_lo[:], lo[:, k * TILES:(k + 1) * TILES].unsqueeze(2).to_broadcast([P, TILES, P]),
                                 consts[:, K_IOTA:K_IOTA + P].unsqueeze(1).to_broadcast([P, TILES, P]),
                                 ALU.is_equal).then_inc(s_oh, 1)
            ve.wait_ge(s_tok, TOP0)
            link(ve.tensor_copy(tok[:], ps_x[0][:, 0:2 * HI0].rearrange("p (a b) -> p a b", a=2)))
            link(ve.scalar_tensor_tensor(tok_of[:], tok[:, 0, :], float(P), tok[:, 1, :], ALU.mult, ALU.add))

            def turned(t):
                wait(ve, gathered[t.p], t.h * ST * 16)
                ve.tensor_copy(own[t.p][:], tok_of[:, bass.ds(t.n * ST, ST)]).then_inc(own_done, 1)
                for c in range(ST):
                    q = (t.p * ST + c) % 2
                    wait(ve, xth_done, t.n * ST + c + 1)
                    if c == 0:
                        wait(ve, f_ps, (t.n - 1) * CH)
                    ve.tensor_tensor(xt_lo[t.p][:, :, c * P:(c + 1) * P], ps_x[q][:, 0:DC * P].rearrange("p (k s) -> p k s", k=DC),
                                     xt_hi[t.p][:, :, c * P:(c + 1) * P], ALU.subtract).then_inc(xtl_done, 1)

            def hidden(t):
                wait(ve, y_ps, t.n * ST)
                for m in range(CH):
                    wait(ve, hid_done, t.n * CH + m + 1)
                    ve.tensor_copy(hid_hi[:, m, :], hid[m % 2]).then_inc(hh_done, 1)
                    wait(ve, hh_done, t.n * CH + m + 1)
                    ve.tensor_tensor(hid_lo[:, m, :], hid[m % 2], hid_hi[:, m, :], ALU.subtract).then_inc(hl_done, 1)

            def rows(t):
                wait(ve, b_ld, (t.n + 1) * 48)
                ve.tensor_tensor(b2ls[t.p][:], b2[t.p][:], ls[t.p][:], ALU.mult).then_inc(b2_done, 1)
                for c in range(ST):
                    q = (t.p * ST + c) % 2
                    wait(ve, y_ps, t.n * ST + c + 1)
                    ve.tensor_tensor(ys[q][:], ps_y[q][:, 0:D], ls[t.p][:], ALU.mult).then_inc(ys_done, 1)
                    wait(ve, ys_done, t.n * ST + c + 1)
                    if c == 0:
                        wait(ve, b2_done, t.n + 1)
                    if t.p == 0:
                        wait(ve, y_st[q], t.h * ST * 16 + (c // 2) * 16)
                    else:
                        wait(ve, y_st[q], t.h * ST * 16 + ((ST + c) // 2) * 16)
                    ve.tensor_tensor(ys[q][:], ys[q][:], b2ls[t.p][:], ALU.add).then_inc(yt_done, 1)
                    wait(ve, yt_done, t.n * ST + c + 1)
                    ve.tensor_tensor(yo[q][:], ys[q][:], xg[t.p][:, c, :], ALU.add).then_inc(yo_done, 1)

            def both(t):
                hidden(t)
                rows(t)

            pipelined(ve, [turned, both], E0)


def phase_heads(nc, env):
    a, x_res, consts, tri_bf, ones_bf, gate = (env[k] for k in ("a", "x_res", "consts", "tri_bf", "ones_bf", "gate"))
    w_own, slot_own, y0_d, rows_d, xn3_d = (env[k] for k in ("w_own", "slot_own", "y0_d", "rows_d", "xn3_d"))
    NC = HALVES * TOP0
    NR = HALVES * TOP1
    NG = HALVES * GROUPS
    ctx = ExitStack()
    with ctx:
        def sb(name, shape, dt):
            return ctx.enter_context(nc.sbuf_tensor("h_" + name, shape, dt))

        def two(name, shape, dt):
            return [sb(f"{name}{i}", shape, dt) for i in range(2)]

        def sem(name):
            env["sems"].append(nc.alloc_semaphore(name="h_" + name))
            return env["sems"][-1]

        ident = consts[:, K_ID:K_ID + P]
        wq, wk, wv, wo = (sb(n, [P, DC, D], F32) for n in ("wq", "wk", "wv", "wo"))
        bq, bk = sb("bq", [P, DC], F32), sb("bk", [P, DC], F32)
        bv, bo = sb("bv", [P, D], F32), sb("bo", [P, HALVES, D], F32)
        gate_w16, gate_w = sb("gate_w16", [P, DC, E1], BF16), sb("gate_w", [P, DC, E1], F32)
        gate_b = sb("gate_b", [P, E1], F32)
        ident_bf = sb("ident_bf", [P, P], BF16)
        causal_bf = sb("causal_bf", [P, HPB, CTX], BF16)
        eps = sb("eps", [P, 1], F32)
        tok_no = sb("tok_no", [P, TILES], F32)
        counts = two("counts", [P, E1], BF16)

        slots = two("slots", [P, NC], U32)
        wts = two("wts", [P, NC], F32)
        yg = two("yg", [P, NC, D], F32)
        ct = two("ct", [P, DC, CTX], F32)
        stats, mv = two("stats", [P, HALVES, 6], F32), two("mv", [P, HALVES, 2], F32)
        lnv, rstd, newton = (two(n, [P, HALVES], F32) for n in ("lnv", "rstd", "newton"))
        stats3, mv3 = two("stats3", [P, HALVES, 6], F32), two("mv3", [P, HALVES, 2], F32)
        lnv3, rstd3, newton3 = (two(n, [P, HALVES], F32) for n in ("lnv3", "rstd3", "newton3"))
        xn = two("xn", [P, HALVES, D], F32)
        x_t = two("x_t", [P, DC, SEQ], F32)
        qf = [sb("qf", [P, DC, SEQ], F32)] * 2
        q_hi, q_lo = two("q_hi", [P, DC, SEQ], F32R), two("q_lo", [P, DC, SEQ], F32R)
        kf, k_hi, k_lo = (sb(n, [P, DC, CTX], d) for n, d in (("kf", F32), ("k_hi", F32R), ("k_lo", F32)))
        kd_hi, kd_lo = two("kd_hi", [P, DC, HPC, CTX], F32R), two("kd_lo", [P, DC, HPC, CTX], F32R)
        vm = two("vm", [CTX, HEADS, 2 * HD], F32)
        mx, nmx, sums, rec = (two(n, [P, HPB], F32) for n in ("mx", "nmx", "sums", "rec"))
        pr, pn = two("pr", [P, HPB, CTX], F32), two("pn", [P, HPB, CTX], F32)
        pt = sb("pt", [CTX, HEADS, SEQ], F32)
        o_t = two("o_t", [P, DC, SEQ], F32)
        xsum = [sb("xsum", [P, HALVES, D], F32)] * 2
        row = two("row", [P, HALVES, ROW], F32)
        x3_t = [sb("x3_t", [P, DC, SEQ], F32)] * 2
        ex, sg, sel = (two(n, [P, HALVES, E1], F32) for n in ("ex", "sg", "sel"))
        top8, idx8 = two("top8", [P, HALVES, 8], F32), two("idx8", [P, HALVES, 8], U32)
        idf = two("idf", [P, HALVES, TOP1], F32)
        hot = two("hot", [P, NR, E1], F32)
        hot_any = two("hot_any", [P, HALVES, E1], BF16)
        own = [sb("own", [P, NR, E1], F32)] * 2
        wk8, wsum, wrec = two("wk8", [P, NR], F32), two("wsum", [P, HALVES], F32), two("wrec", [P, HALVES], F32)
        csum = sb("csum", [P, E1], BF16)
        pfx = [sb("pfx", [P, HALVES, E1], F32)] * 2
        pos, over = two("pos", [P, NR], F32), two("over", [P, NR], F32)
        dest = two("dest", [P, NR], U32)

        def bank(name):
            return ctx.enter_context(nc.psum_tensor("h_" + name, [P, 512], F32))

        ps_s = [bank(f"ps_s{i}") for i in range(GROUPS)]
        ps_p, ps_q, ps_kv, ps_w = bank("ps_p"), bank("ps_q"), bank("ps_kv"), bank("ps_w")

        names = ("par prep tokn yi_done mixed0 mixed st_done mv_done ln_done rs_done nw_done xn_done xt_ps xt_sb q_ps "
                 "qf_done qh_done ql_done kv_ps kf_done kh_done kl_done kdh_done kdl_done v_done s_ps mx_done nmx_done "
                 "exp_done rec_done pn_done p_ps pt_done o_ps ot_done w_ps xs_done x_done st3_done mv3_done ln3_done "
                 "rs3_done nw3_done xn3_done x3t_ps x3t_sb lg_ps ex_done e1_done sg_done sel_done t8_done i8_done "
                 "idf_done hot_done any_done own_done wk_done ws_done wr_done wn_done cs_done cnt_done pf_ps pf_done "
                 "own2_done pos_done ov_done dest_done rowx_done zero").split()
        S = {n: sem(n) for n in names}
        loaded = [sem("loaded0"), sem("loaded1")]
        yin = [sem("yin0"), sem("yin1")]
        sent = [sem("sent0"), sem("sent1")]
        stored = [sem("stored0"), sem("stored1")]
        PARAMS = 12
        ROWX = 3

        def tiles(t):
            return x_res[:, bass.ds(t.n * HALVES, HALVES), :]

        def nothing(t):
            pass

        block = ctx.enter_context(nc.Block())

        @block.sync
        def _(sp):
            for dst, src in ((wk[:], a["wk_t"]), (wv[:], a["wv_t"]), (wq[:], a["wq_t"]), (wo[:], a["wo_t"]),
                             (bq[:], a["bq"]), (bk[:], a["bk"]), (bv[:], a["bv"].partition_broadcast(P)),
                             (bo[:], a["bo2"].partition_broadcast(P)), (gate_w16[:], a["gate_w"]),
                             (gate_b[:], a["gate_b"].partition_broadcast(P))):
                sp.dma_start(dst, src).then_inc(S["par"], 16)

            def load(t):
                wait_apart(sp, loaded[t.p], t.h * 16, gate)
                wait_apart(sp, S["kv_ps"], t.n - 1, gate)
                sp.dma_start(ct[t.p][:], a["ctx_t"][bass.ds(t.n, 1)].rearrange("a p k j -> (a p) k j")).then_inc(loaded[t.p], 16)

            def store(t):
                wait_apart(sp, stored[t.p], t.h * 16, gate)
                wait_apart(sp, S["xn3_done"], (t.n + 1) * HALVES, gate)
                sp.dma_start(xn3_d.rearrange("(t p) d -> p t d", p=P)[:, bass.ds(t.n * HALVES, HALVES), :],
                             row[t.p][:, :, 0:D]).then_inc(stored[t.p], 16)

            pipelined(sp, [load, nothing, nothing, nothing, store], BATCH)
            for q in range(2):
                sp.wait_ge(stored[q], BATCH // 2 * 16)

        @block.gpsimd
        def _(pool):
            pool.iota(tok_no[:], [[P, TILES]], base=0, channel_multiplier=1,
                      allow_small_or_imprecise_dtypes=True).then_inc(S["tokn"], 1)

            def gather(t):
                wait(pool, S["yi_done"], (t.n + 1) * 2)
                wait(pool, S["mixed"], (t.n - 1) * NC)
                apart(pool, gate)
                for c in range(NC):
                    pool.indirect_dma_start(yg[t.p][:, c, :], None, y0_d,
                                            bass.IndirectOffsetOnAxis(ap=slots[t.p][:, c:c + 1], axis=0)
                                            ).then_inc(yin[t.p], 16)

            def split(t):
                wait(pool, S["qf_done"], (t.n + 1) * DC)
                wait(pool, S["qh_done"], t.n + 1)
                wait(pool, S["s_ps"], (t.n - 1) * NG)
                pool.tensor_tensor(q_lo[t.p][:], qf[t.p][:], q_hi[t.p][:], ALU.subtract).then_inc(S["ql_done"], 1)
                wait(pool, S["kl_done"], t.n + 1)
                for c in range(DC):
                    pool.tensor_tensor(kd_lo[t.p][:, c], k_lo[:, c, :].unsqueeze(1).to_broadcast([P, HPC, CTX]),
                                       consts[:, K_HEAD:K_HEAD + HPC].unsqueeze(2).to_broadcast([P, HPC, CTX]),
                                       ALU.mult).then_inc(S["kdl_done"], 1)

            def scatter(t):
                wait(pool, S["dest_done"], t.n + 1)
                wait(pool, S["rowx_done"], (t.n + 1) * ROWX)
                wait(pool, S["xn3_done"], (t.n + 1) * HALVES)
                apart(pool, gate)
                for n in range(NR):
                    pool.indirect_dma_start(rows_d, bass.IndirectOffsetOnAxis(ap=dest[t.p][:, n:n + 1], axis=0),
                                            row[t.p][:, n // TOP1, :], None, bounds_check=SLOTS1 - 1,
                                            oob_is_err=False).then_inc(sent[t.p], 16)

            pipelined(pool, [gather, split, nothing, nothing, nothing, scatter], BATCH)
            for q in range(2):
                pool.wait_ge(sent[q], BATCH // 2 * NR * 16)

        @block.tensor
        def _(pe):
            pe.wait_ge(S["par"], 10 * 16)
            pe.wait_ge(S["prep"], 1)

            def pre(t):
                wait(pe, loaded[t.p], (t.h + 1) * 16)
                wait(pe, S["ot_done"], t.n)
                wait(pe, S["kf_done"], t.n * DC)
                wait(pe, S["v_done"], t.n * 2)
                for o in range(DC):
                    for k in range(DC):
                        pe.matmul(ps_kv[:, o * CTX:(o + 1) * CTX], wk[:, k, o * P:(o + 1) * P], ct[t.p][:, k, :],
                                  start=k == 0, stop=k == DC - 1)
                for k in range(DC):
                    mm = pe.matmul(ps_kv[0:CTX, D:2 * D], ct[t.p][:, k, :], wv[:, k, :], start=k == 0, stop=k == DC - 1)
                mm.then_inc(S["kv_ps"], 1)
                wait(pe, S["xn_done"], (t.n + 1) * HALVES)
                wait(pe, S["qf_done"], t.n * DC)
                for s in range(HALVES):
                    for k in range(DC):
                        mm = pe.transpose(ps_q[:, k * SEQ + s * P:k * SEQ + (s + 1) * P], xn[t.p][:, s, k * P:(k + 1) * P], ident)
                mm.then_inc(S["xt_ps"], 1)
                wait(pe, S["xt_sb"], t.n + 1)
                for o in range(DC):
                    for k in range(DC):
                        mm = pe.matmul(ps_q[:, o * SEQ:(o + 1) * SEQ], wq[:, k, o * P:(o + 1) * P], x_t[t.p][:, k, :],
                                       start=k == 0, stop=k == DC - 1)
                mm.then_inc(S["q_ps"], 1)

            def attend(t):
                def scores(n):
                    s, g = n // GROUPS, n % GROUPS
                    c, h = g * HPB // HPC, g * HPB % HPC
                    wait(pe, S["exp_done"], (t.n * NG + n - GROUPS + 1) * HPB)
                    i = 0
                    terms = ((q_hi, kd_hi), (q_hi, kd_lo), (q_lo, kd_hi))
                    for l, r in terms:
                        mm = pe.matmul(ps_s[g][:, 0:HPB * CTX], l[t.p][:, c, s * P:(s + 1) * P],
                                       r[t.p][:, c, h:h + HPB, :].rearrange("p h j -> p (h j)"),
                                       start=i == 0, stop=s > 0 and i == len(terms) - 1)
                        i += 1
                    if s == 0:
                        mm = pe.matmul(ps_s[g][:, 0:HPB * CTX], ident_bf[:], causal_bf[:].rearrange("p h j -> p (h j)"),
                                       start=False, stop=True)
                    mm.then_inc(S["s_ps"], 1)

                def turn(n):
                    wait(pe, S["pn_done"], t.n * NG + n + 1)
                    wait(pe, S["pt_done"], t.n * NG + n)
                    for h in range(HPB):
                        mm = pe.transpose(ps_p[0:CTX, h * P:(h + 1) * P], pn[n % 2][:, h, :], ident)
                    mm.then_inc(S["p_ps"], 1)

                wait(pe, S["qh_done"], t.n + 1)
                wait(pe, S["ql_done"], t.n + 1)
                wait(pe, S["kdh_done"], (t.n + 1) * DC)
                wait(pe, S["kdl_done"], (t.n + 1) * DC)
                for n in range(NG + 2):
                    if n < NG:
                        scores(n)
                    if n >= 2:
                        turn(n - 2)
                wait(pe, S["pt_done"], (t.n + 1) * NG)
                wait(pe, S["v_done"], (t.n + 1) * 2)
                wait(pe, S["kf_done"], (t.n + 1) * DC)
                for c in range(DC):
                    for odd in range(2):
                        for j in range(HPC // 2):
                            h = c * HPC + 2 * j + odd
                            mm = pe.matmul(ps_kv[32 * j:32 * (j + 1), c * SEQ:(c + 1) * SEQ], vm[t.p][:, h, :], pt[:, h, :],
                                           start=odd == 0, stop=odd == 1, tile_position=(0, 32 * j),
                                           skip_group_check=True)
                mm.then_inc(S["o_ps"], 1)

            def project(t):
                wait(pe, S["ot_done"], t.n + 1)
                wait(pe, S["ex_done"], t.n)
                for s in range(HALVES):
                    for c in range(DC):
                        mm = pe.matmul(ps_w[:, s * D:(s + 1) * D], o_t[t.p][:, c, s * P:(s + 1) * P], wo[:, c, :],
                                       start=c == 0, stop=c == DC - 1)
                mm.then_inc(S["w_ps"], 1)

            def gates(t):
                wait(pe, S["xn3_done"], (t.n + 1) * HALVES)
                wait(pe, S["pf_done"], t.n)
                wait(pe, S["xs_done"], t.n + 1)
                for s in range(HALVES):
                    for k in range(DC):
                        mm = pe.transpose(ps_w[:, k * SEQ + s * P:k * SEQ + (s + 1) * P], row[t.p][:, s, k * P:(k + 1) * P], ident)
                mm.then_inc(S["x3t_ps"], 1)
                wait(pe, S["x3t_sb"], t.n + 1)
                for s in range(HALVES):
                    for k in range(DC):
                        mm = pe.matmul(ps_w[:, s * E1:(s + 1) * E1], x3_t[t.p][:, k, s * P:(s + 1) * P], gate_w[:, k, :],
                                       start=k == 0, stop=k == DC - 1)
                mm.then_inc(S["lg_ps"], 1)

            def prefix(t):
                wait(pe, S["any_done"], t.n + 1)
                wait(pe, S["cnt_done"], t.n)
                wait(pe, S["ex_done"], t.n + 1)
                wait(pe, S["xs_done"], min(t.n + 2, BATCH) if isinstance(t.n, int) else t.n + 2)
                for s in range(HALVES):
                    out = ps_w[:, s * E1:(s + 1) * E1]
                    pe.matmul(out, tri_bf[:], hot_any[t.p][:, s, :], start=True, stop=False)
                    if s:
                        pe.matmul(out, ones_bf[:], hot_any[t.p][:, 0, :], start=False, stop=False)
                    mm = pe.matmul(out, ones_bf[:], counts[t.p][:], start=False, stop=True)
                mm.then_inc(S["pf_ps"], 1)

            pipelined(pe, [nothing, pre, attend, project, gates, prefix], BATCH)

        @block.scalar
        def _(act):
            act.preload_act_table_set("natural_log_exp_and_others")
            act.wait_ge(S["par"], 10 * 16)
            act.wait_ge(S["prep"], 1)

            def root(t, m, lv, r, m_s, l_s, r_s, nw_s):
                wait(act, S[m_s], (t.n + 1) * HALVES)
                wait(act, S[nw_s], (t.n - 1) * 3)
                act.activation(lv[t.p][:], m[t.p][:, :, 1], ACT.Ln, bias=eps[:]).then_inc(S[l_s], 1)
                wait(act, S[l_s], t.n + 1)
                act.activation(r[t.p][:], lv[t.p][:], ACT.Exp, scale=-0.5).then_inc(S[r_s], 1)

            def pre(t):
                wait(act, S["kv_ps"], t.n + 1)
                wait(act, S["kh_done"], t.n)
                wait(act, S["kl_done"], t.n)
                for o in range(DC):
                    act.activation(kf[:, o, :], ps_kv[:, o * CTX:(o + 1) * CTX], ACT.Identity, bias=bk[:, o:o + 1]
                                   ).then_inc(S["kf_done"], 1)
                root(t, mv, lnv, rstd, "mv_done", "ln_done", "rs_done", "nw_done")
                wait(act, S["xt_ps"], t.n + 1)
                wait(act, S["q_ps"], t.n - 1)
                act.activation(x_t[t.p][:], ps_q[:].rearrange("p (k i) -> p k i", k=DC), ACT.Copy).then_inc(S["xt_sb"], 1)
                wait(act, S["q_ps"], t.n + 1)
                wait(act, S["qh_done"], t.n)
                wait(act, S["ql_done"], t.n)
                for o in range(DC):
                    act.activation(qf[t.p][:, o, :], ps_q[:, o * SEQ:(o + 1) * SEQ], ACT.Identity, bias=bq[:, o:o + 1]
                                   ).then_inc(S["qf_done"], 1)

            def attend(t):
                def exps(n):
                    g = n % GROUPS
                    wait(act, S["nmx_done"], t.n * NG + n + 1)
                    wait(act, S["pn_done"], t.n * NG + n - 1)
                    wait(act, S["rec_done"], t.n * NG + n - 1)
                    for h in range(HPB):
                        act.activation(pr[n % 2][:, h, :], ps_s[g][:, h * CTX:(h + 1) * CTX], ACT.Exp,
                                       bias=nmx[n % 2][:, h:h + 1], scale=SCALE, accum_out=sums[n % 2][:, h:h + 1]
                                       ).then_inc(S["exp_done"], 1)

                def keep(n):
                    s, g = n // GROUPS, n % GROUPS
                    wait(act, S["p_ps"], t.n * NG + n + 1)
                    if n == 0:
                        wait(act, S["o_ps"], t.n)
                    act.activation(pt[:, g * HPB:(g + 1) * HPB, s * P:(s + 1) * P],
                                   ps_p[0:CTX, :].rearrange("p (h i) -> p h i", h=HPB), ACT.Copy).then_inc(S["pt_done"], 1)

                for n in range(NG + 2):
                    if n < NG:
                        exps(n)
                    if n >= 2:
                        keep(n - 2)
                wait(act, S["o_ps"], t.n + 1)
                wait(act, S["w_ps"], t.n - 1)
                act.activation(o_t[t.p][:], ps_kv[:].rearrange("p (k i) -> p k i", k=DC), ACT.Copy).then_inc(S["ot_done"], 1)

            def root3(t):
                root(t, mv3, lnv3, rstd3, "mv3_done", "ln3_done", "rs3_done", "nw3_done")

            def gates(t):
                wait(act, S["x3t_ps"], t.n + 1)
                wait(act, S["lg_ps"], t.n)
                act.activation(x3_t[t.p][:], ps_w[:].rearrange("p (k i) -> p k i", k=DC), ACT.Copy).then_inc(S["x3t_sb"], 1)
                wait(act, S["lg_ps"], t.n + 1)
                wait(act, S["e1_done"], t.n - 1)
                act.activation(ex[t.p][:].rearrange("p s e -> p (s e)"), ps_w[:, 0:HALVES * E1], ACT.Exp, scale=-1.0
                               ).then_inc(S["ex_done"], 1)

            pipelined(act, [nothing, pre, attend, root3, gates], BATCH)

        @block.vector
        def _(ve):
            ve.memset(eps[:], LN_EPS).then_inc(S["zero"], 1)
            for i in range(2):
                ve.memset(vm[i][:], 0.0).then_inc(S["zero"], 1)
                ve.memset(counts[i][:], 0.0).then_inc(S["zero"], 1)
                ve.memset(row[i][:], 0.0).then_inc(S["zero"], 1)
            ve.tensor_copy(ident_bf[:], ident).then_inc(S["zero"], 1)
            ve.tensor_copy(causal_bf[:], consts[:, K_CAUSAL:K_CAUSAL + CTX].unsqueeze(1).to_broadcast([P, HPB, CTX])).then_inc(S["zero"], 1)
            ve.wait_ge(S["par"], 10 * 16)
            ve.wait_ge(S["zero"], 9)
            ve.wait_ge(S["tokn"], 1)
            ve.tensor_copy(gate_w[:], gate_w16[:]).then_inc(S["prep"], 1)

            def norm(t, src, st, m, r, nw, dst, st_s, m_s, r_s, nw_s, dst_s):
                apart(ve, gate)
                for s in range(HALVES):
                    ve.bn_stats(st[t.p][:, s, :], src[:, s, :]).then_inc(S[st_s], 1)
                wait(ve, S[st_s], (t.n + 1) * HALVES)
                apart(ve, gate)
                for s in range(HALVES):
                    ve.bn_aggr(m[t.p][:, s, :], st[t.p][:, s, :]).then_inc(S[m_s], 1)
                wait(ve, S[r_s], t.n + 1)
                ve.scalar_tensor_tensor(nw[t.p][:], m[t.p][:, :, 1], LN_EPS, r[t.p][:], ALU.add, ALU.mult).then_inc(S[nw_s], 1)
                wait(ve, S[nw_s], t.n * 3 + 1)
                ve.scalar_tensor_tensor(nw[t.p][:], nw[t.p][:], -0.5, r[t.p][:], ALU.mult, ALU.mult).then_inc(S[nw_s], 1)
                wait(ve, S[nw_s], t.n * 3 + 2)
                ve.scalar_tensor_tensor(nw[t.p][:], nw[t.p][:], 1.5, r[t.p][:], ALU.add, ALU.mult).then_inc(S[nw_s], 1)
                wait(ve, S[nw_s], t.n * 3 + 3)
                for s in range(HALVES):
                    ve.tensor_scalar(dst[t.p][:, s, 0:D], src[:, s, :], m[t.p][:, s, 0:1], nw[t.p][:, s:s + 1],
                                     ALU.subtract, ALU.mult).then_inc(S[dst_s], 1)

            def pick(t):
                wait(ve, yin[t.p], t.h * NC * 16)
                wait(ve, S["mixed"], (t.n - 1) * NC)
                own_tiles = bass.ds(t.n * HALVES, HALVES)
                ve.tensor_copy(slots[t.p][:].rearrange("p (s k) -> p s k", k=TOP0), slot_own[:, own_tiles, :]).then_inc(S["yi_done"], 1)
                ve.tensor_copy(wts[t.p][:].rearrange("p (s k) -> p s k", k=TOP0), w_own[:, own_tiles, :]).then_inc(S["yi_done"], 1)

            def pre(t):
                wait(ve, yin[t.p], (t.h + 1) * NC * 16)
                wait(ve, S["yi_done"], (t.n + 1) * 2)
                for k in range(TOP0):
                    if k:
                        wait(ve, S["mixed"], t.n * NC + k * HALVES)
                    for s in range(HALVES):
                        c = s * TOP0 + k
                        xt = x_res[:, bass.ds(t.n * HALVES + s, 1), :].rearrange("p a d -> p (a d)")
                        ve.scalar_tensor_tensor(xt, yg[t.p][:, c, :], wts[t.p][:, c:c + 1], xt, ALU.mult, ALU.add
                                                ).then_inc(S["mixed"], 1)
                wait(ve, S["mixed"], (t.n + 1) * NC)
                wait(ve, S["xt_ps"], t.n - 1)
                norm(t, tiles(t), stats, mv, rstd, newton, xn, "st_done", "mv_done", "rs_done", "nw_done", "xn_done")
                wait(ve, S["kf_done"], (t.n + 1) * DC)
                wait(ve, S["o_ps"], t.n - 1)
                for odd in range(2):
                    ve.tensor_tensor(vm[t.p][:, odd::2, odd * HD:(odd + 1) * HD],
                                     ps_kv[0:CTX, D:2 * D].rearrange("p (h x) -> p h x", x=HD)[:, odd::2, :],
                                     bv[0:CTX, :].rearrange("p (h x) -> p h x", x=HD)[:, odd::2, :], ALU.add
                                     ).then_inc(S["v_done"], 1)
                wait(ve, S["kdh_done"], t.n * DC)
                ve.tensor_copy(k_hi[:], kf[:]).then_inc(S["kh_done"], 1)
                wait(ve, S["kh_done"], t.n + 1)
                wait(ve, S["kdl_done"], t.n * DC)
                ve.tensor_tensor(k_lo[:], kf[:], k_hi[:], ALU.subtract).then_inc(S["kl_done"], 1)
                wait(ve, S["s_ps"], (t.n - 1) * NG)
                for c in range(DC):
                    ve.tensor_tensor(kd_hi[t.p][:, c], k_hi[:, c, :].unsqueeze(1).to_broadcast([P, HPC, CTX]),
                                     consts[:, K_HEAD:K_HEAD + HPC].unsqueeze(2).to_broadcast([P, HPC, CTX]),
                                     ALU.mult).then_inc(S["kdh_done"], 1)
                wait(ve, S["qf_done"], (t.n + 1) * DC)
                wait(ve, S["ql_done"], t.n - 1)
                ve.tensor_copy(q_hi[t.p][:], qf[t.p][:]).then_inc(S["qh_done"], 1)

            def attend(t):
                def peaks(n):
                    g = n % GROUPS
                    wait(ve, S["s_ps"], t.n * NG + n + 1)
                    wait(ve, S["nmx_done"], t.n * NG + n - 1)
                    ve.tensor_reduce(mx[n % 2][:], ps_s[g][:, 0:HPB * CTX].rearrange("p (h j) -> p h j", h=HPB), AX.X, ALU.max
                                     ).then_inc(S["mx_done"], 1)
                    wait(ve, S["mx_done"], t.n * NG + n + 1)
                    wait(ve, S["exp_done"], (t.n * NG + n - 1) * HPB)
                    ve.tensor_scalar(nmx[n % 2][:], mx[n % 2][:], -SCALE, None, ALU.mult).then_inc(S["nmx_done"], 1)

                def scale(n):
                    wait(ve, S["exp_done"], (t.n * NG + n + 1) * HPB)
                    wait(ve, S["pn_done"], t.n * NG + n - 1)
                    ve.reciprocal(rec[n % 2][:], sums[n % 2][:]).then_inc(S["rec_done"], 1)
                    wait(ve, S["rec_done"], t.n * NG + n + 1)
                    wait(ve, S["p_ps"], t.n * NG + n - 1)
                    ve.tensor_tensor(pn[n % 2][:], pr[n % 2][:], rec[n % 2][:].unsqueeze(2).to_broadcast([P, HPB, CTX]),
                                     ALU.mult).then_inc(S["pn_done"], 1)

                for n in range(NG + 1):
                    if n < NG:
                        peaks(n)
                    if n >= 1:
                        scale(n - 1)

            def project(t):
                wait(ve, S["w_ps"], t.n + 1)
                wait(ve, S["x_done"], t.n)
                ve.tensor_tensor(xsum[t.p][:], ps_w[:].rearrange("p (s d) -> p s d", s=HALVES), bo[:], ALU.add).then_inc(S["xs_done"], 1)
                wait(ve, S["xs_done"], t.n + 1)
                ve.tensor_tensor(tiles(t), tiles(t), xsum[t.p][:], ALU.add).then_inc(S["x_done"], 1)
                wait(ve, S["x_done"], t.n + 1)
                wait(ve, S["x3t_ps"], t.n - 1)
                wait(ve, stored[t.p], t.h * 16)
                wait(ve, sent[t.p], t.h * NR * 16)
                norm(t, tiles(t), stats3, mv3, rstd3, newton3, row, "st3_done", "mv3_done", "rs3_done", "nw3_done", "xn3_done")

            def gates(t):
                wait(ve, S["ex_done"], t.n + 1)
                ve.tensor_scalar(ex[t.p][:], ex[t.p][:], 1.0, None, ALU.add).then_inc(S["e1_done"], 1)
                wait(ve, S["e1_done"], t.n + 1)
                ve.reciprocal(sg[t.p][:], ex[t.p][:]).then_inc(S["sg_done"], 1)
                wait(ve, S["sg_done"], t.n + 1)
                ve.tensor_tensor(sel[t.p][:], sg[t.p][:], gate_b[:].unsqueeze(1).to_broadcast([P, HALVES, E1]), ALU.add
                                 ).then_inc(S["sel_done"], 1)
                wait(ve, S["sel_done"], t.n + 1)
                apart(ve, gate)
                for s in range(HALVES):
                    ve.max(top8[t.p][:, s, :], sel[t.p][:, s, :]).then_inc(S["t8_done"], 1)
                wait(ve, S["t8_done"], (t.n + 1) * HALVES)
                apart(ve, gate)
                for s in range(HALVES):
                    ve.max_index(idx8[t.p][:, s, :], top8[t.p][:, s, :], sel[t.p][:, s, :]).then_inc(S["i8_done"], 1)
                wait(ve, S["i8_done"], (t.n + 1) * HALVES)
                ve.tensor_copy(idf[t.p][:], idx8[t.p][:, :, 0:TOP1]).then_inc(S["idf_done"], 1)
                wait(ve, S["idf_done"], t.n + 1)
                ve.tensor_tensor(hot[t.p][:], idf[t.p][:].rearrange("p s k -> p (s k)").unsqueeze(2).to_broadcast([P, NR, E1]),
                                 consts[:, K_IOTA:K_IOTA + E1].unsqueeze(1).to_broadcast([P, NR, E1]), ALU.is_equal
                                 ).then_inc(S["hot_done"], 1)
                wait(ve, S["hot_done"], t.n + 1)
                wait(ve, S["pf_ps"], t.n - 1)
                with nc.allow_low_precision(reason="sums of zeros and at most one 1"):
                    ve.tensor_reduce(hot_any[t.p][:], hot[t.p][:].rearrange("p (s k) e -> p s e k", k=TOP1), AX.X,
                                     ALU.add).then_inc(S["any_done"], 1)
                wait(ve, S["pos_done"], t.n)
                for s in range(HALVES):
                    k = slice(s * TOP1, (s + 1) * TOP1)
                    ve.tensor_tensor(own[t.p][:, k, :], hot[t.p][:, k, :],
                                     sg[t.p][:, s:s + 1, :].to_broadcast([P, TOP1, E1]), ALU.mult).then_inc(S["own_done"], 1)
                wait(ve, S["own_done"], (t.n + 1) * HALVES)
                ve.tensor_reduce(wk8[t.p][:], own[t.p][:], AX.X, ALU.add).then_inc(S["wk_done"], 1)
                wait(ve, S["wk_done"], t.n + 1)
                ve.tensor_reduce(wsum[t.p][:], wk8[t.p][:].rearrange("p (s k) -> p s k", k=TOP1), AX.X, ALU.add
                                 ).then_inc(S["ws_done"], 1)
                wait(ve, S["ws_done"], t.n * 2 + 1)
                ve.tensor_scalar(wsum[t.p][:], wsum[t.p][:], 1e-12, None, ALU.max).then_inc(S["ws_done"], 1)
                wait(ve, S["ws_done"], t.n * 2 + 2)
                ve.reciprocal(wrec[t.p][:], wsum[t.p][:]).then_inc(S["wr_done"], 1)
                wait(ve, S["wr_done"], t.n + 1)
                ve.tensor_tensor(row[t.p][:, :, C_W:C_W + TOP1], wk8[t.p][:].rearrange("p (s k) -> p s k", k=TOP1),
                                 wrec[t.p][:].unsqueeze(2).to_broadcast([P, HALVES, TOP1]), ALU.mult).then_inc(S["rowx_done"], 1)
                ve.tensor_copy(row[t.p][:, :, C_E:C_E + TOP1], idf[t.p][:]).then_inc(S["rowx_done"], 1)
                ve.tensor_copy(row[t.p][:, :, C_TOK:C_TOK + 1], tok_no[:, bass.ds(t.n * HALVES, HALVES)].unsqueeze(2)
                               ).then_inc(S["rowx_done"], 1)

            def prefix(t):
                wait(ve, S["pf_ps"], t.n + 1)
                wait(ve, S["pos_done"], t.n)
                ve.tensor_copy(pfx[t.p][:], ps_w[:, 0:HALVES * E1].rearrange("p (s e) -> p s e", s=HALVES)).then_inc(S["pf_done"], 1)
                wait(ve, S["cnt_done"], t.n)
                ve.tensor_tensor(csum[:], counts[t.p][:], hot_any[t.p][:, 0, :], ALU.add).then_inc(S["cs_done"], 1)
                wait(ve, S["cs_done"], t.n + 1)
                ve.tensor_tensor(counts[1 - t.p][:], csum[:], hot_any[t.p][:, 1, :], ALU.add).then_inc(S["cnt_done"], 1)
                wait(ve, S["pf_done"], t.n + 1)
                wait(ve, S["wk_done"], t.n + 1)
                for s in range(HALVES):
                    k = slice(s * TOP1, (s + 1) * TOP1)
                    ve.tensor_tensor(own[t.p][:, k, :], hot[t.p][:, k, :],
                                     pfx[t.p][:, s:s + 1, :].to_broadcast([P, TOP1, E1]), ALU.mult).then_inc(S["own2_done"], 1)
                wait(ve, S["own2_done"], (t.n + 1) * HALVES)
                ve.tensor_reduce(pos[t.p][:], own[t.p][:], AX.X, ALU.add).then_inc(S["pos_done"], 1)
                wait(ve, S["pos_done"], t.n + 1)
                ve.tensor_scalar(over[t.p][:], pos[t.p][:], float(CAP1), float(DROPPED), ALU.is_ge, ALU.mult).then_inc(S["ov_done"], 1)
                wait(ve, S["ov_done"], t.n * 2 + 1)
                ve.tensor_tensor(over[t.p][:], over[t.p][:], pos[t.p][:], ALU.add).then_inc(S["ov_done"], 1)
                wait(ve, S["ov_done"], t.n * 2 + 2)
                wait(ve, sent[t.p], t.h * NR * 16)
                ve.scalar_tensor_tensor(dest[t.p][:], idf[t.p][:].rearrange("p s k -> p (s k)"), float(CAP1), over[t.p][:],
                                        ALU.mult, ALU.add).then_inc(S["dest_done"], 1)

            pipelined(ve, [pick, pre, attend, project, gates, prefix], BATCH)


def phase_moe(nc, env):
    a, x_res, consts, gate, rows_d, xn3_d, out = (env[k] for k in ("a", "x_res", "consts", "gate", "rows_d", "xn3_d", "out"))
    W_UP = 2 * DC * INNER
    ctx = ExitStack()
    with ctx:
        def sb(name, shape, dt):
            return ctx.enter_context(nc.sbuf_tensor("m_" + name, shape, dt))

        def two(name, shape, dt):
            return [sb(f"{name}{i}", shape, dt) for i in range(2)]

        def sem(name):
            env["sems"].append(nc.alloc_semaphore(name="m_" + name))
            return env["sems"][-1]

        ident = consts[:, K_ID:K_ID + P]
        sw16 = sb("sw16", [P, W_UP + D], BF16)
        sw = sb("sw", [P, W_UP + D], F32R)
        w16 = two("w16", [P, W_UP + D], BF16)
        w = two("w", [P, W_UP + D], F32R)
        xr = two("xr", [P, HALVES, ROW], F32)
        x_hi, x_lo = two("x_hi", [P, DC, SEQ], F32R), two("x_lo", [P, DC, SEQ], F32R)
        s1, hid = two("s1", [P, SEQ], F32), two("hid", [P, SEQ], F32)
        h_hi, h_lo = two("h_hi", [P, SEQ], F32R), two("h_lo", [P, SEQ], F32R)
        yo = two("yo", [P, HALVES, D], F32)
        wsel, wrow = two("wsel", [P, HALVES, TOP1], F32), two("wrow", [P, HALVES], F32)
        tok = two("tok", [P, HALVES], U32)
        spare = sb("spare", [P, SLOT_TILES1 * D], F32)

        def banks(name):
            return [ctx.enter_context(nc.psum_tensor(f"m_{name}{i}", [P, 512], F32)) for i in range(2)]

        ps_t, ps_1, ps_3, ps_y = banks("ps_t"), banks("ps_1"), banks("ps_3"), banks("ps_y")
        names = ("sw_ld sw_done spare_z spare_st w_ld0 w_ld1 w_done x_ld0 x_ld1 tok_done wsel_done wrow_done t_ps xh_done "
                 "xl_done up_ps s1_done hid_done hh_done hl_done y_ps yo_done st0 st1 added").split()
        S = {n: sem(n) for n in names}
        w_ld, x_ld, st = ([S[f"{n}{i}"] for i in range(2)] for n in ("w_ld", "x_ld", "st"))

        def loops(eng, shared, experts):
            pipelined(eng, shared, BATCH)
            pipelined(eng, experts, E1, BATCH)

        def nothing(t):
            pass

        block = ctx.enter_context(nc.Block())

        @block.sync
        def _(sp):
            sp.dma_start(sw16[:], a["sw"]).then_inc(S["sw_ld"], 16)
            sp.wait_ge(S["spare_z"], 1)
            sp.dma_start(out[TOKENS:, :].rearrange("(p c) d -> p (c d)", c=SLOT_TILES1), spare[:]).then_inc(S["spare_st"], 16)

            def free(t):
                wait_apart(sp, x_ld[t.p], t.h * 16, gate)
                wait_apart(sp, S["t_ps"], t.n - 1, gate)

            def load_tokens(t):
                free(t)
                sp.dma_start(xr[t.p][:, :, 0:D], xn3_d.rearrange("(t p) d -> p t d", p=P)[:, bass.ds(t.n * HALVES, HALVES), :]
                             ).then_inc(x_ld[t.p], 16)

            def load_slots(t):
                free(t)
                wait_apart(sp, S["wsel_done"], t.n - 1 - BATCH, gate)
                wait_apart(sp, S["tok_done"], t.n - 1 - BATCH, gate)
                sp.dma_start(xr[t.p][:], rows_d.rearrange("(t p) d -> p t d", p=P)[:, bass.ds((t.n - BATCH) * SLOT_TILES1, SLOT_TILES1), :]
                             ).then_inc(x_ld[t.p], 16)
                wait_apart(sp, w_ld[t.p], (t.h - BATCH // 2) * 16, gate)
                wait_apart(sp, S["w_done"], t.n - 1 - BATCH, gate)
                sp.dma_start(w16[t.p][:], a["moe_w"][bass.ds(t.n - BATCH, 1)].rearrange("e p n -> (e p) n")).then_inc(w_ld[t.p], 16)

            def store(t):
                wait_apart(sp, S["yo_done"], (t.n + 1) * HALVES, gate)
                wait_apart(sp, st[t.p], t.h * 16, gate)
                sp.dma_start(out[0:TOKENS, :].rearrange("(t p) d -> p t d", p=P)[:, bass.ds(t.n * HALVES, HALVES), :], yo[t.p][:]
                             ).then_inc(st[t.p], 16)

            loops(sp, [load_tokens, nothing, nothing, store], [load_slots])
            sp.wait_ge(S["spare_st"], 16)
            sp.wait_ge(S["added"], E1 * SLOT_TILES1 * 16)

        @block.gpsimd
        def _(pool):
            pool.memset(spare[:], 0.0).then_inc(S["spare_z"], 1)
            pool.wait_ge(S["spare_st"], 16)
            for q in range(2):
                pool.wait_ge(st[q], BATCH // 2 * 16)

            def add(t):
                e = t.n - BATCH
                wait(pool, S["added"], e * SLOT_TILES1 * 16)
                wait(pool, S["tok_done"], e + 1)
                wait(pool, S["yo_done"], (t.n + 1) * HALVES)
                apart(pool, gate)
                for c in range(SLOT_TILES1):
                    pool.indirect_dma_start(out, bass.IndirectOffsetOnAxis(ap=tok[t.p][:, c:c + 1], axis=0), yo[t.p][:, c, :],
                                            None, compute_op=ALU.add).then_inc(S["added"], 16)

            pipelined(pool, [nothing, nothing, add], E1, BATCH)

        @block.tensor
        def _(pe):
            def turn(t):
                wait(pe, x_ld[t.p], (t.h + 1) * 16)
                wait(pe, S["xl_done"], t.n - 1)
                for s in range(HALVES):
                    for k in range(DC):
                        mm = pe.transpose(ps_t[t.p][:, k * SEQ + s * P:k * SEQ + (s + 1) * P], xr[t.p][:, s, k * P:(k + 1) * P], ident)
                mm.then_inc(S["t_ps"], 1)

            def up(t, wts):
                wait(pe, S["xl_done"], t.n + 1)
                wait(pe, S["hid_done"], t.n - 1)
                for n, ps in enumerate((ps_1, ps_3)):
                    i = 0
                    for k in range(DC):
                        for x in (x_hi, x_lo):
                            c = (n * DC + k) * INNER
                            mm = pe.matmul(ps[t.p][:, 0:SEQ], wts[:, c:c + INNER], x[t.p][:, k, :], start=i == 0, stop=i == 2 * DC - 1)
                            i += 1
                mm.then_inc(S["up_ps"], 1)

            def down(t, wts):
                wait(pe, S["hl_done"], t.n + 1)
                wait(pe, S["yo_done"], (t.n - 1) * HALVES)
                for s in range(HALVES):
                    for i, h in enumerate((h_hi, h_lo)):
                        mm = pe.matmul(ps_y[t.p][:, s * D:(s + 1) * D], h[t.p][:, s * P:(s + 1) * P], wts[:, W_UP:W_UP + D],
                                       start=i == 0, stop=i == 1)
                mm.then_inc(S["y_ps"], 1)

            def up_shared(t):
                up(t, sw)

            def down_shared(t):
                down(t, sw)

            def up_expert(t):
                wait(pe, S["w_done"], t.n - BATCH + 1)
                up(t, w[t.p])

            def down_expert(t):
                down(t, w[t.p])

            pe.wait_ge(S["sw_done"], 1)
            loops(pe, [turn, up_shared, down_shared], [turn, up_expert, down_expert])

        @block.scalar
        def _(act):
            def turn(t):
                wait(act, S["t_ps"], t.n + 1)
                wait(act, S["up_ps"], t.n - 1)
                act.activation(x_hi[t.p][:], ps_t[t.p][:].rearrange("p (k i) -> p k i", k=DC), ACT.Copy).then_inc(S["xh_done"], 1)

            def up(t):
                wait(act, S["up_ps"], t.n + 1)
                wait(act, S["hid_done"], t.n - 1)
                act.activation(s1[t.p][:], ps_1[t.p][:, 0:SEQ], ACT.Silu).then_inc(S["s1_done"], 1)
                wait(act, S["hid_done"], t.n + 1)
                wait(act, S["y_ps"], t.n - 1)
                act.activation(h_hi[t.p][:], hid[t.p][:], ACT.Copy).then_inc(S["hh_done"], 1)

            def down_expert(t):
                wait(act, S["y_ps"], t.n + 1)
                wait(act, S["wrow_done"], t.n - BATCH + 1)
                wait(act, S["added"], (t.n - 1 - BATCH) * SLOT_TILES1 * 16)
                for s in range(HALVES):
                    act.activation(yo[t.p][:, s, :], ps_y[t.p][:, s * D:(s + 1) * D], ACT.Copy, scale=wrow[t.p][:, s:s + 1]
                                   ).then_inc(S["yo_done"], 1)

            def first_expert(t):
                for q in range(2):
                    act.wait_ge(st[q], BATCH // 2 * 16)

            pipelined(act, [turn, up], BATCH)
            first_expert(None)
            pipelined(act, [turn, up, down_expert], E1, BATCH)

        @block.vector
        def _(ve):
            ve.wait_ge(S["sw_ld"], 16)
            ve.tensor_copy(sw[:], sw16[:]).then_inc(S["sw_done"], 1)

            def turn(t):
                wait(ve, S["xh_done"], t.n + 1)
                wait(ve, S["up_ps"], t.n - 1)
                ve.tensor_tensor(x_lo[t.p][:], ps_t[t.p][:].rearrange("p (k i) -> p k i", k=DC), x_hi[t.p][:], ALU.subtract
                                 ).then_inc(S["xl_done"], 1)

            def turn_expert(t):
                e = t.n - BATCH
                wait(ve, w_ld[t.p], (t.h - BATCH // 2 + 1) * 16)
                wait(ve, S["y_ps"], t.n - 1)
                ve.tensor_copy(w[t.p][:], w16[t.p][:]).then_inc(S["w_done"], 1)
                turn(t)
                wait(ve, x_ld[t.p], (t.h + 1) * 16)
                wait(ve, S["yo_done"], (t.n - 1) * HALVES)
                ve.scalar_tensor_tensor(wsel[t.p][:], xr[t.p][:, :, C_E:C_E + TOP1], consts[:, bass.ds(e + K_IOTA, 1)],
                                        xr[t.p][:, :, C_W:C_W + TOP1], ALU.is_equal, ALU.mult).then_inc(S["wsel_done"], 1)
                wait(ve, S["added"], (e - 1) * SLOT_TILES1 * 16)
                ve.tensor_copy(tok[t.p][:], xr[t.p][:, :, C_TOK]).then_inc(S["tok_done"], 1)
                wait(ve, S["wsel_done"], e + 1)
                ve.tensor_reduce(wrow[t.p][:], wsel[t.p][:], AX.X, ALU.add).then_inc(S["wrow_done"], 1)

            def up(t):
                wait(ve, S["s1_done"], t.n + 1)
                wait(ve, S["hh_done"], t.n - 1)
                wait(ve, S["hl_done"], t.n - 1)
                ve.tensor_tensor(hid[t.p][:], s1[t.p][:], ps_3[t.p][:, 0:SEQ], ALU.mult).then_inc(S["hid_done"], 1)
                wait(ve, S["hh_done"], t.n + 1)
                wait(ve, S["y_ps"], t.n - 1)
                ve.tensor_tensor(h_lo[t.p][:], hid[t.p][:], h_hi[t.p][:], ALU.subtract).then_inc(S["hl_done"], 1)

            def down_shared(t):
                wait(ve, S["y_ps"], t.n + 1)
                wait(ve, st[t.p], t.h * 16)
                for s in range(HALVES):
                    ve.tensor_tensor(yo[t.p][:, s, :], ps_y[t.p][:, s * D:(s + 1) * D],
                                     x_res[:, bass.ds(t.n * HALVES + s, 1), :].rearrange("p a d -> p (a d)"), ALU.add
                                     ).then_inc(S["yo_done"], 1)

            loops(ve, [turn, up, down_shared], [turn_expert, up])


def kernel(**inputs):
    import numpy as np
    import concourse.bacc as bacc
    from concourse.bass_utils import run_bass_kernel_spmd

    nc = bacc.Bacc("TRN2", target_bir_lowering=False, num_devices=1)
    arrays, aps = lay_out(np, inputs), {}
    for name, array in arrays.items():
        aps[name] = nc.dram_tensor(f"in_{name}", array.shape, mybir.dt.from_np(array.dtype), kind="ExternalInput").ap()
    out = nc.dram_tensor("out", (TOKENS + SLOT_TILES1 * P, D), F32, kind="ExternalOutput").ap()
    build(nc, aps, out)
    r = run_bass_kernel_spmd(nc, [{f"in_{k}": v for k, v in arrays.items()}], core_ids=[0])
    return r.results[0]["out"][:TOKENS].reshape(BATCH, SEQ, D)


def lay_out(np, inputs):
    g = {k: np.asarray(v) for k, v in inputs.items()}

    def chunks(w):
        return np.ascontiguousarray(w.reshape(-1, P, w.shape[-1]).transpose(1, 0, 2))

    def unit(w):
        return w.reshape(-1, DC, P, INNER).transpose(0, 2, 1, 3).reshape(-1, P, DC * INNER)

    c = np.zeros((P, K_END), np.float32)
    p = np.arange(P)
    c[:, K_ID:K_ID + P] = np.eye(P)
    c[:, K_SU:K_SU + P] = p[:, None] < p[None, :]
    c[:, K_IOTA:K_IOTA + P] = p[None, :]
    c[:, K_P] = p
    c[:, K_HEAD:K_HEAD + HPC] = p[:, None] // HD == np.arange(HPC)[None, :]
    c[:, K_CAUSAL:K_CAUSAL + CTX] = np.where(np.arange(CTX)[None, :] > p[:, None], MASKED, 0.0)
    ctx = g["ctx_1024"]
    return {
        "consts": c,
        "x": np.ascontiguousarray(g["x"].reshape(TILES, P, D).transpose(1, 0, 2)),
        "ctx": ctx,
        "ctx_t": np.ascontiguousarray(ctx.transpose(0, 2, 1).reshape(BATCH, DC, P, CTX).transpose(0, 2, 1, 3)),
        "wsim": np.ascontiguousarray(g["L0_xattn_w_sim"].reshape(3, DC, P).transpose(2, 0, 1)),
        "b_sim": g["L0_xattn_b_sim"],
        "wqv": chunks(g["L0_xattn_W_qv"]),
        "bqv2": np.stack([g["L0_xattn_b_qv"]] * HALVES),
        "router_w": chunks(g["L0_ffn_router_w"].T),
        "router_b": g["L0_ffn_router_b"],
        "fc1_t": np.ascontiguousarray(g["L0_ffn_fc1_w"].transpose(0, 2, 1).reshape(E0, DC, P, HID0).transpose(0, 2, 1, 3)),
        "fc1_b": np.ascontiguousarray(g["L0_ffn_fc1_b"].reshape(E0, HC0, P).transpose(0, 2, 1)),
        "fc2_t": np.ascontiguousarray(g["L0_ffn_fc2_w"].transpose(0, 2, 1).reshape(E0, HC0, P, D).transpose(0, 2, 1, 3)),
        "fc2_b": g["L0_ffn_fc2_b"],
        "ls": g["L0_ffn_layer_scale"],
        "wq_t": chunks(g["L1_xattn_Wq"].T),
        "wk_t": chunks(g["L1_xattn_Wk"].T),
        "wv_t": chunks(g["L1_xattn_Wv"].T),
        "wo_t": chunks(g["L1_xattn_Wo"].T),
        "bq": np.ascontiguousarray(g["L1_xattn_bq"].reshape(DC, P).T),
        "bk": np.ascontiguousarray(g["L1_xattn_bk"].reshape(DC, P).T),
        "bv": g["L1_xattn_bv"],
        "bo2": np.stack([g["L1_xattn_bo"]] * HALVES),
        "gate_w": chunks(g["L1_ffn_gate_w"].T),
        "gate_b": g["L1_ffn_bias"],
        "moe_w": np.concatenate([unit(g["L1_ffn_W1"]), unit(g["L1_ffn_W3"]), g["L1_ffn_W2"]], axis=2),
        "sw": np.concatenate([unit(g["L1_ffn_sw1"].T[None]), unit(g["L1_ffn_sw3"].T[None]), g["L1_ffn_sw2"].T[None]], axis=2)[0],
    }
```

```python
import concourse.bass as bass
from concourse import mybir
from contextlib import ExitStack

F32, F32R, BF16 = mybir.dt.float32, mybir.dt.float32r, mybir.dt.bfloat16
I32, U32 = mybir.dt.int32, mybir.dt.uint32
ALU, ACT, AX = mybir.AluOpType, mybir.ActivationFunctionType, mybir.AxisListType

P = 128
BATCH, SEQ, D = 16, 256, 256
CTX = 120
DC = D // P
HALVES = SEQ // P
TILES = BATCH * HALVES
TOKENS = BATCH * SEQ
LN_EPS = 1e-5
E0, HID0, TOP0, W_EPS = 8, 1024, 2, 1e-9
CAP0 = int(1.2 * (TOKENS // E0 + 1))
SLOT_TILES0 = -(-CAP0 // P)
SLOTS0 = SLOT_TILES0 * P
HALF0 = SLOTS0 // 2
HC0 = HID0 // P
HI0 = E0 * SLOT_TILES0
HEADS, HD = 16, 16
HPC = P // HD
HPB = 4
GROUPS = HEADS // HPB
SCALE = HD ** -0.5
MASKED = -1e30
E1, INNER, TOP1 = 32, 128, 4
CAP1 = 2 * 1024 * TOP1 // E1
SLOTS1 = E1 * CAP1
SLOT_TILES1 = CAP1 // P
DROPPED = 1 << 20
ROW = D + 16
C_TOK, C_W, C_E = D, D + 1, D + 1 + TOP1
K_ID, K_SU, K_IOTA, K_P, K_HEAD, K_CAUSAL, K_END = 0, 128, 256, 384, 385, 400, 520


class At:

    def __init__(self, n, half, par):
        self.n, self.h, self.p = n, half, par


def wait(eng, sem, count):
    if not isinstance(count, int) or count > 0:
        eng.wait_ge(sem, count)


def pipelined(eng, stages, n, base=0):
    parts = [(place, -k, i, part) for k, stage in enumerate(stages) for i, (place, part) in enumerate(stage)]
    parts.sort(key=lambda x: x[:3])
    lag = len(stages) - 1
    first = (lag + 3) // 2 * 2
    pairs = (n - first) // 2

    def peeled(s):
        for _, k, _, part in parts:
            if 0 <= s + k < n:
                part(At(base + s + k, (base + s + k) // 2, (s + k) % 2))

    for s in range(first):
        peeled(s)
    if pairs:
        with eng.Fori(0, pairs) as i:
            for u in range(2):
                for _, k, _, part in parts:
                    part(At(i * 2 + (base + first + u + k), i + (base + first + u + k) // 2, (u + k) % 2))
    for s in range(first + 2 * pairs, n + lag):
        peeled(s)


def placed(part, places):
    return [(place, part(n)) for n, place in enumerate(places)]


def build(nc, a, out, upto=4, dbg=None):
    ctx = ExitStack()
    with ctx:
        def sb(name, shape, dt):
            return ctx.enter_context(nc.sbuf_tensor(name, shape, dt))

        x_res = sb("x_res", [P, TILES, D], F32)
        consts = sb("consts", [P, K_END], F32)
        tri_bf = sb("tri_bf", [P, P], BF16)
        ones_bf = sb("ones_bf", [P, P], BF16)
        logits = sb("logits", [P, TILES, E0], F32)
        top2 = sb("top2", [P, TILES, TOP0], F32)
        exp2 = sb("exp2", [P, TILES, TOP0], F32)
        w_own = sb("w_own", [P, TILES, TOP0], F32)
        slot_own = sb("slot_own", [P, TILES, TOP0], U32)
        gate = ctx.enter_context(nc.semaphore("gate"))

        xn1_d = nc.dram_tensor("xn1_d", (TOKENS, D), F32).ap()
        y0_d = nc.dram_tensor("y0_d", (E0 * SLOTS0, D), F32).ap()
        rows_d = nc.dram_tensor("rows_d", (SLOTS1, ROW), F32).ap()
        xn3_d = nc.dram_tensor("xn3_d", (TOKENS, D), F32).ap()
        sums_d = [nc.dram_tensor(f"sums{i}_d", (TOKENS + CAP1, D), F32).ap() for i in range(2)]
        env = dict(locals())
        env["sems"] = []
        for phase in (phase_attend, phase_experts, phase_heads, phase_moe)[:upto]:
            phase(nc, env)
            nc.clear_and_free_semaphores(env["sems"])
            nc.all_engine_barrier()
            env["sems"] = []
        if dbg:
            dbg(nc, env)


def wait_apart(eng, sem, count, gate):
    if not isinstance(count, int) or count > 0:
        eng.wait_ge(sem, count)
        if not isinstance(count, int):
            apart(eng, gate)


def apart(eng, gate):
    eng.sem_inc(gate, 1)


def phase_attend(nc, env):
    a, x_res, consts, tri_bf, ones_bf = (env[k] for k in ("a", "x_res", "consts", "tri_bf", "ones_bf"))
    logits, top2, exp2, gate, xn1_d, rows_d, sums_d = (env[k] for k in (
        "logits", "top2", "exp2", "gate", "xn1_d", "rows_d", "sums_d"))
    ctx = ExitStack()
    with ctx:
        def sb(name, shape, dt):
            return ctx.enter_context(nc.sbuf_tensor("a_" + name, shape, dt))

        def two(name, shape, dt):
            return [sb(f"{name}{i}", shape, dt) for i in range(2)]

        def sem(name):
            env["sems"].append(nc.alloc_semaphore(name="a_" + name))
            return env["sems"][-1]

        def bank(name, shape, dt=F32):
            return ctx.enter_context(nc.psum_tensor("a_" + name, shape, dt))

        ident = consts[:, K_ID:K_ID + P]
        wqv = sb("wqv", [P, 4 * DC, D], F32)
        wqv_hi = sb("wqv_hi", [P, 2 * DC, D], F32R)
        wqv_lo = sb("wqv_lo", [P, 2 * DC, D], F32R)
        bqv = sb("bqv", [P, HALVES, D], F32)
        wsim = sb("wsim", [P, 3, DC], F32)
        bsim = sb("bsim", [P, 1], F32)
        w2rep = sb("w2rep", [P, DC, P], F32)
        ones_row = sb("ones_row", [1, P], F32)
        router_w = sb("router_w", [P, DC, E0], F32)
        router_b = sb("router_b", [P, E0], F32)
        empty_rows = sb("empty_rows", [P, SLOT_TILES1, ROW], F32)
        zeros = sb("zeros", [P, D], F32)
        cn = two("cn", [CTX, D], F32)
        ct = two("ct", [P, DC, CTX], F32)
        stats = two("stats", [P, HALVES, 6], F32)
        mv = two("mv", [P, HALVES, 2], F32)
        rstd = two("rstd", [P, HALVES], F32)
        newton = two("newton", [P, HALVES], F32)
        lnv = two("lnv", [P, HALVES], F32)
        xn = two("xn", [P, HALVES, D], F32)
        enc_t = two("enc_t", [P, DC, SEQ], F32)
        enc_hi = two("enc_hi", [P, DC, SEQ], F32R)
        enc_lo = two("enc_lo", [P, DC, SEQ], F32R)
        simw = two("simw", [P, DC, CTX], F32)
        rowb = two("rowb", [P, CTX], F32)
        sim = two("sim", [P, HALVES, CTX], F32)
        mx = two("mx", [P, HALVES], F32)
        nmx = two("nmx", [P, HALVES], F32)
        probs = two("probs", [P, HALVES, CTX], F32)
        psums = two("psums", [P, HALVES], F32)
        prec = two("prec", [P, HALVES], F32)
        probs_n = two("probs_n", [P, HALVES, CTX], F32)
        gm = two("gm", [1, 1], F32)
        ngm = two("ngm", [1, 1], F32)
        brow = two("brow", [1, SEQ], F32)
        bsum = two("bsum", [1, 1], F32)
        brec = two("brec", [1, 1], F32)
        brow_n = two("brow_n", [1, SEQ], F32)
        bjunk = two("bjunk", [P, DC, SEQ], F32)
        hc = two("hc", [P, DC], F32)
        wc = two("wc", [P, DC, D], F32)
        wc_hi = two("wc_hi", [P, DC, D], F32R)
        wc_lo = two("wc_lo", [P, DC, D], F32R)
        at_sb = two("at_sb", [CTX, SEQ], F32)
        hq_hi = two("hq_hi", [P, DC, SEQ], F32R)
        hq_lo = two("hq_lo", [P, DC, SEQ], F32R)
        prod = two("prod", [P, DC, SEQ], F32)
        prod_hi = two("prod_hi", [P, DC, SEQ], F32R)
        prod_lo = two("prod_lo", [P, DC, SEQ], F32R)
        x_in, x1 = two("x_in", [P, HALVES, D], F32), two("x1", [P, HALVES, D], F32)
        xb = two("xb", [P, HALVES, D], F32)
        stats1 = two("stats1", [P, HALVES, 6], F32)
        mv1 = two("mv1", [P, HALVES, 2], F32)
        rstd1 = two("rstd1", [P, HALVES], F32)
        newton1 = two("newton1", [P, HALVES], F32)
        lnv1 = two("lnv1", [P, HALVES], F32)
        eps = sb("eps", [P, 1], F32)
        xn1 = two("xn1", [P, HALVES, D], F32)
        x1_t = two("x1_t", [P, DC, SEQ], F32)
        lg = two("lg", [P, HALVES, E0], F32)
        mx8 = two("mx8", [P, HALVES, 8], F32)
        ix8 = two("ix8", [P, HALVES, 8], U32)

        ps_enc = bank("ps_enc", [P, DC, SEQ])
        ps_sim = bank("ps_sim", [P, 4, P])
        ps_row = bank("ps_row", [P, 512])
        ps_bc = bank("ps_bc", [P, 512])
        ps_at = bank("ps_at", [P, 512])
        ps_hq = bank("ps_hq", [P, DC, SEQ])
        ps_out = bank("ps_out", [P, HALVES, D])
        ps_x1 = bank("ps_x1", [P, DC, SEQ])

        s_const, s_par, s_prep, s_empty, s_rows = (sem(n) for n in ("s_const", "s_par", "s_prep", "s_empty", "s_rows"))
        s_w2, s_wqh, s_wql, s_zero = (sem(n) for n in ("s_w2", "s_wqh", "s_wql", "s_zero"))
        loaded = [sem("loaded0"), sem("loaded1")]
        stored = [sem("stored0"), sem("stored1")]
        stored_x = [sem("stored_x0"), sem("stored_x1")]
        cn_loaded = [sem("cn_loaded0"), sem("cn_loaded1")]
        (st_done, mv_done, rs_done, xn_done, simw_done, enc_ps, enc_sb, enc_h, enc_l, sim_ps, rowb_done, sim_done,
         mx_done, nmx_done, exp_done, prec_done, pn_done, row_ps, gm_done, ngm_done, brow_done, brec_done, bn_done,
         bc_ps, hc_done, wc_done, wch_done, wcl_done, at_ps, at_done, hq_ps, hqh_done, hql_done, pr_done, prh_done,
         prl_done, out_ps, xs_done, x1_done, st1_done, mv1_done, rs1_done, xn1_done, x1t_ps, x1t_sb, lg_ps, lg_done,
         mx8_done, ix8_done, keep_done, ln_done, ln1_done, nw_done, nw1_done) = (sem(n) for n in (
             "st_done mv_done rs_done xn_done simw_done enc_ps enc_sb enc_h enc_l sim_ps rowb_done sim_done "
             "mx_done nmx_done exp_done prec_done pn_done row_ps gm_done ngm_done brow_done brec_done bn_done "
             "bc_ps hc_done wc_done wch_done wcl_done at_ps at_done hq_ps hqh_done hql_done pr_done prh_done "
             "prl_done out_ps xs_done x1_done st1_done mv1_done rs1_done xn1_done x1t_ps x1t_sb lg_ps lg_done "
             "mx8_done ix8_done keep_done ln_done ln1_done nw_done nw1_done").split())
        LOADS = 2 * 16
        CLEARED = E1 // BATCH

        block = ctx.enter_context(nc.Block())

        @block.sync
        def _(sp):
            sp.dma_start(consts[:], a["consts"]).then_inc(s_const, 16)
            sp.dma_start(wsim[:], a["wsim"]).then_inc(s_par, 16)
            sp.dma_start(bsim[:], a["b_sim"].partition_broadcast(P)).then_inc(s_par, 16)

            def load(t):
                wait_apart(sp, loaded[t.p], t.h * LOADS, gate)
                wait_apart(sp, sim_ps, t.n - 1, gate)
                wait_apart(sp, simw_done, (t.n - 1) * DC, gate)
                wait_apart(sp, xs_done, t.n - 1, gate)
                wait_apart(sp, xn_done, (t.n - 1) * HALVES, gate)
                sp.dma_start(x_in[t.p][:], a["x"][:, bass.ds(t.n * HALVES, HALVES), :]).then_inc(loaded[t.p], 16)
                sp.dma_start(ct[t.p][:], a["ctx_t"][bass.ds(t.n, 1)].rearrange("a p k j -> (a p) k j")).then_inc(loaded[t.p], 16)

            def load_cn(t):
                wait_apart(sp, cn_loaded[t.p], t.h * 16, gate)
                wait_apart(sp, hq_ps, t.n - 1, gate)
                sp.dma_start(cn[t.p][:], a["ctx"][bass.ds(t.n, 1)].rearrange("a j d -> (a j) d")).then_inc(cn_loaded[t.p], 16)

            def first_loads():
                load(At(0, 0, 0))
                sp.dma_start(wqv[:], a["wqv"]).then_inc(s_par, 16)
                sp.dma_start(bqv[:], a["bqv2"].partition_broadcast(P)).then_inc(s_par, 16)
                sp.dma_start(router_w[:], a["router_w"]).then_inc(s_par, 16)
                sp.dma_start(router_b[:], a["router_b"].partition_broadcast(P)).then_inc(s_par, 16)
                load(At(1, 0, 1))

            def fetch(t):
                if not isinstance(t.n, int) or t.n >= 2:
                    load(t)

            def store(t):
                wait_apart(sp, stored[t.p], t.h * 16, gate)
                wait_apart(sp, xn1_done, (t.n + 1) * HALVES, gate)
                wait_apart(sp, stored_x[t.p], t.h * 16, gate)
                sp.dma_start(x_res[:, bass.ds(t.n * HALVES, HALVES), :], x1[t.p][:]).then_inc(stored_x[t.p], 16)
                sp.dma_start(xn1_d.rearrange("(t p) d -> p t d", p=P)[:, bass.ds(t.n * HALVES, HALVES), :],
                             xn1[t.p][:]).then_inc(stored[t.p], 16)

            first_loads()
            def clear_sums(tiles):
                for sums in sums_d:
                    sp.dma_start(sums.rearrange("(c p) d -> p c d", p=P)[:, tiles, :],
                                 zeros[:].unsqueeze(1).to_broadcast([P, HALVES, D])).then_inc(s_rows, 16)

            def clear(t):
                if isinstance(t.n, int) and t.n == 0:
                    sp.wait_ge(s_empty, SLOT_TILES1)
                    sp.wait_ge(s_zero, 2)
                for c in range(SLOT_TILES1):
                    sp.dma_start(rows_d.rearrange("(e c p) r -> c p e r", c=SLOT_TILES1, p=P)[c][:, bass.ds(t.n * CLEARED, CLEARED), :],
                                 empty_rows[:, c:c + 1, :].to_broadcast([P, CLEARED, ROW])).then_inc(s_rows, 16)
                clear_sums(bass.ds(t.n * HALVES, HALVES))

            pipelined(sp, [[(1, fetch)],
                           [(0, load_cn), (2, clear)],
                           [],
                           [(3, store)]], BATCH)
            clear_sums(slice(TILES, TILES + SLOT_TILES1))
            sp.wait_ge(s_rows, (BATCH * (SLOT_TILES1 + len(sums_d)) + len(sums_d)) * 16)
            for q in range(2):
                sp.wait_ge(stored[q], BATCH // 2 * 16)
                sp.wait_ge(stored_x[q], BATCH // 2 * 16)

        @block.gpsimd
        def _(pool):
            pool.memset(empty_rows[:], 0.0).then_inc(s_zero, 1)
            pool.memset(zeros[:], 0.0).then_inc(s_zero, 1)
            pool.wait_ge(s_const, 16)
            pool.wait_ge(s_zero, 2)
            for c in range(SLOT_TILES1):
                pool.tensor_scalar(empty_rows[:, c, C_TOK:C_TOK + 1], consts[:, K_P:K_P + 1],
                                   float(TOKENS + c * P), None, ALU.add).then_inc(s_empty, 1)
            pool.wait_ge(s_par, 6 * 16)
            pool.wait_ge(s_wqh, 1)
            pool.tensor_tensor(wqv_lo[:], wqv[:, DC:3 * DC, :], wqv_hi[:], ALU.subtract).then_inc(s_wql, 1)

            def split_enc(t):
                wait(pool, enc_sb, t.n + 1)
                wait(pool, enc_h, t.n + 1)
                wait(pool, out_ps, t.n - 1)
                pool.tensor_tensor(enc_lo[t.p][:], enc_t[t.p][:], enc_hi[t.p][:], ALU.subtract).then_inc(enc_l, 1)

            def split_wc(t):
                wait(pool, wc_done, (t.n + 1) * DC)
                wait(pool, wch_done, t.n + 1)
                wait(pool, out_ps, t.n - 1)
                pool.tensor_tensor(wc_lo[t.p][:], wc[t.p][:], wc_hi[t.p][:], ALU.subtract).then_inc(wcl_done, 1)

            def split_prod(t):
                wait(pool, pr_done, t.n + 1)
                wait(pool, prh_done, t.n + 1)
                wait(pool, out_ps, t.n - 1)
                pool.tensor_tensor(prod_lo[t.p][:], prod[t.p][:], prod_hi[t.p][:], ALU.subtract).then_inc(prl_done, 1)

            def biased(t):
                wait(pool, loaded[t.p], (t.h + 1) * LOADS)
                wait(pool, x1_done, t.n - 1)
                pool.tensor_tensor(xb[t.p][:], x_in[t.p][:], bqv[:], ALU.add).then_inc(xs_done, 1)

            pipelined(pool, [[],
                             [(2, split_enc), (3, biased)],
                             [(0, split_wc), (1, split_prod)]], BATCH)

        @block.tensor
        def _(pe):
            pe.wait_ge(s_const, 16)

            def turn(t):
                wait(pe, xn_done, (t.n + 1) * HALVES)
                wait(pe, enc_sb, t.n)
                for s in range(HALVES):
                    for k in range(DC):
                        mm = pe.transpose(ps_enc[:, k, s * P:(s + 1) * P], xn[t.p][:, s, k * P:(k + 1) * P], ident)
                mm.then_inc(enc_ps, 1)

            def similarity(t):
                wait(pe, simw_done, (t.n + 1) * DC)
                wait(pe, rowb_done, t.n)
                wait(pe, sim_done, t.n * HALVES)
                pe.wait_ge(s_w2, DC)
                for k in range(DC):
                    pe.matmul(ps_sim[:, 2, 0:CTX], w2rep[:, k, :], ct[t.p][:, k, :], start=k == 0, stop=k == DC - 1)
                wait(pe, enc_sb, t.n + 1)
                for s in range(HALVES):
                    for k in range(DC):
                        mm = pe.matmul(ps_sim[:, s, 0:CTX], enc_t[t.p][:, k, s * P:(s + 1) * P], simw[t.p][:, k, :],
                                       start=k == 0, stop=k == DC - 1)
                mm.then_inc(sim_ps, 1)

            def peaks(t):
                wait(pe, mx_done, t.n + 1)
                wait(pe, gm_done, t.n)
                wait(pe, brow_done, t.n)
                for s in range(HALVES):
                    mm = pe.matmul(ps_row[0:1, s * P:(s + 1) * P], mx[t.p][:, s:s + 1], ident, start=True, stop=True)
                mm.then_inc(row_ps, 1)

            def turn_probs(t):
                wait(pe, pn_done, (t.n + 1) * HALVES)
                wait(pe, at_done, t.n)
                for s in range(HALVES):
                    mm = pe.transpose(ps_at[0:CTX, s * P:(s + 1) * P], probs_n[t.p][:, s, :], ident)
                mm.then_inc(at_ps, 1)

            def attend(t):
                wait(pe, cn_loaded[t.p], (t.h + 1) * 16)
                wait(pe, at_done, t.n + 1)
                wait(pe, hql_done, t.n)
                wait(pe, pr_done, t.n)
                for k in range(DC):
                    mm = pe.matmul(ps_hq[:, k, :], cn[t.p][:, k * P:(k + 1) * P], at_sb[t.p][:], start=True, stop=True)
                mm.then_inc(hq_ps, 1)

            def spread(t):
                wait(pe, bn_done, t.n + 1)
                wait(pe, hc_done, t.n * DC)
                pe.matmul(ps_bc[:, 0:SEQ], ones_row[:], brow_n[t.p][:], start=True, stop=True).then_inc(bc_ps, 1)

            def project(s, part):
                def step(t):
                    if part == 0:
                        if s == 0:
                            wait(pe, x1_done, t.n)
                            wait(pe, hqh_done, t.n + 1)
                            wait(pe, hql_done, t.n + 1)
                            pe.wait_ge(s_wql, 1)
                        xh, xl, wh, wl = hq_hi, hq_lo, wqv_hi[:, 0:DC], wqv_lo[:, 0:DC]
                    elif part == 1:
                        if s == 0:
                            wait(pe, prh_done, t.n + 1)
                            wait(pe, prl_done, t.n + 1)
                        xh, xl, wh, wl = prod_hi, prod_lo, wqv_hi[:, DC:2 * DC], wqv_lo[:, DC:2 * DC]
                    else:
                        if s == 0:
                            wait(pe, enc_l, t.n + 1)
                            wait(pe, wch_done, t.n + 1)
                            wait(pe, wcl_done, t.n + 1)
                        xh, xl, wh, wl = enc_hi, enc_lo, wc_hi[t.p], wc_lo[t.p]
                    n = 0
                    for k in range(DC):
                        for l, r in ((xh, wh), (xh, wl), (xl, wh)):
                            mm = pe.matmul(ps_out[:, s, :], l[t.p][:, k, s * P:(s + 1) * P], r[:, k, :],
                                           start=part == 0 and n == 0, stop=part == 2 and n == 3 * DC - 1)
                            n += 1
                    if s == HALVES - 1 and part == 2:
                        mm.then_inc(out_ps, 1)
                return step

            def turn_x1(t):
                wait(pe, xn1_done, (t.n + 1) * HALVES)
                wait(pe, x1t_sb, t.n)
                wait(pe, lg_done, t.n * HALVES)
                for s in range(HALVES):
                    for k in range(DC):
                        mm = pe.transpose(ps_x1[:, k, s * P:(s + 1) * P], xn1[t.p][:, s, k * P:(k + 1) * P], ident)
                mm.then_inc(x1t_ps, 1)

            def router(t):
                wait(pe, x1t_sb, t.n + 1)
                for s in range(HALVES):
                    for k in range(DC):
                        mm = pe.matmul(ps_x1[:, 0, s * E0:(s + 1) * E0], x1_t[t.p][:, k, s * P:(s + 1) * P], router_w[:, k, :],
                                       start=k == 0, stop=k == DC - 1)
                mm.then_inc(lg_ps, 1)

            pipelined(pe, [[],
                           [(0, turn), (1, similarity), (5, peaks), (9, turn_probs), (10, spread), (11, attend)],
                           [(2, project(0, 0)), (3, project(0, 1)), (6, project(0, 2)), (7, project(1, 0)), (12, project(1, 1)),
                           (13, project(1, 2))],
                           [(4, turn_x1), (8, router)]], BATCH)

        @block.scalar
        def _(act):
            act.preload_act_table_set("natural_log_exp_and_others")
            act.wait_ge(s_par, 6 * 16)
            act.wait_ge(s_prep, 4)
            act.activation(wqv_hi[:], wqv[:, DC:3 * DC, :], ACT.Copy).then_inc(s_wqh, 1)

            def root(t, m, lv, r, m_s, l_s, r_s, nw_s):
                wait(act, m_s, (t.n + 1) * HALVES)
                wait(act, nw_s, (t.n - 1) * 3)
                act.activation(lv[t.p][:], m[t.p][:, :, 1], ACT.Ln, bias=eps[:]).then_inc(l_s, 1)
                wait(act, l_s, t.n + 1)
                act.activation(r[t.p][:], lv[t.p][:], ACT.Exp, scale=-0.5).then_inc(r_s, 1)

            def root0(t):
                root(t, mv, lnv, rstd, mv_done, ln_done, rs_done, nw_done)

            def turned(t):
                wait(act, enc_ps, t.n + 1)
                wait(act, sim_ps, t.n - 1)
                wait(act, hc_done, (t.n - 1) * DC)
                wait(act, pr_done, t.n - 1)
                wait(act, enc_l, t.n - 1)
                act.activation(enc_t[t.p][:], ps_enc[:], ACT.Copy).then_inc(enc_sb, 1)

            def split_enc(t):
                wait(act, enc_sb, t.n + 1)
                wait(act, out_ps, t.n - 1)
                act.activation(enc_hi[t.p][:], enc_t[t.p][:], ACT.Copy).then_inc(enc_h, 1)

            def row_bias(t):
                wait(act, sim_ps, t.n + 1)
                wait(act, sim_done, (t.n - 1) * HALVES)
                act.activation(rowb[t.p][:], ps_sim[:, 2, 0:CTX], ACT.Identity, bias=bsim[:]).then_inc(rowb_done, 1)

            def exps(t):
                wait(act, nmx_done, t.n + 1)
                wait(act, sim_done, (t.n + 1) * HALVES)
                wait(act, pn_done, (t.n - 1) * HALVES)
                wait(act, prec_done, t.n - 1)
                for s in range(HALVES):
                    act.activation(probs[t.p][:, s, :], sim[t.p][:, s, :], ACT.Exp, bias=nmx[t.p][:, s:s + 1],
                                   accum_out=psums[t.p][:, s:s + 1]).then_inc(exp_done, 1)

            def exps_row(t):
                wait(act, row_ps, t.n + 1)
                wait(act, ngm_done, t.n + 1)
                wait(act, bn_done, t.n - 1)
                wait(act, brec_done, t.n - 1)
                act.activation(brow[t.p][:], ps_row[0:1, 0:SEQ], ACT.Exp, bias=ngm[t.p][:], accum_out=bsum[t.p][:]).then_inc(brow_done, 1)

            def probs_t(t):
                wait(act, at_ps, t.n + 1)
                wait(act, hq_ps, t.n - 1)
                act.activation(at_sb[t.p][:], ps_at[0:CTX, 0:SEQ], ACT.Copy).then_inc(at_done, 1)

            def attended(t):
                wait(act, hq_ps, t.n + 1)
                wait(act, out_ps, t.n - 1)
                wait(act, hql_done, t.n - 1)
                act.activation(hq_hi[t.p][:], ps_hq[:], ACT.Copy).then_inc(hqh_done, 1)

            def product(t):
                wait(act, pr_done, t.n + 1)
                wait(act, prl_done, t.n - 1)
                act.activation(prod_hi[t.p][:], prod[t.p][:], ACT.Copy).then_inc(prh_done, 1)

            def weights(t):
                wait(act, wc_done, (t.n + 1) * DC)
                wait(act, wcl_done, t.n - 1)
                act.activation(wc_hi[t.p][:], wc[t.p][:], ACT.Copy).then_inc(wch_done, 1)

            def root1(t):
                root(t, mv1, lnv1, rstd1, mv1_done, ln1_done, rs1_done, nw1_done)

            def turned_x1(t):
                wait(act, x1t_ps, t.n + 1)
                wait(act, lg_ps, t.n - 1)
                act.activation(x1_t[t.p][:], ps_x1[:], ACT.Copy).then_inc(x1t_sb, 1)

            pipelined(act, [[(8, root0)],
                            [(0, turned), (4, split_enc), (5, row_bias), (6, exps), (9, exps_row), (10, probs_t), (11, attended)],
                            [(1, weights), (2, product)],
                            [(3, root1), (7, turned_x1)]], BATCH)

        @block.vector
        def _(ve):
            ve.memset(ones_bf[:], 1.0).then_inc(s_prep, 1)
            ve.memset(w2rep[:], 1.0).then_inc(s_prep, 1)
            ve.memset(ones_row[:], 1.0).then_inc(s_prep, 1)
            ve.memset(eps[:], LN_EPS).then_inc(s_prep, 1)
            ve.wait_ge(s_const, 16)
            ve.wait_ge(s_prep, 4)
            ve.tensor_copy(tri_bf[:], consts[:, K_SU:K_SU + P]).then_inc(s_prep, 1)
            ve.wait_ge(s_par, 6 * 16)
            for k in range(DC):
                ve.tensor_scalar(w2rep[:, k, :], w2rep[:, k, :], wsim[:, 1, k:k + 1], None, ALU.mult).then_inc(s_w2, 1)

            def moments(t, src, st, m, st_s, m_s):
                apart(ve, gate)
                for s in range(HALVES):
                    ve.bn_stats(st[t.p][:, s, :], src[:, s, :]).then_inc(st_s, 1)
                wait(ve, st_s, (t.n + 1) * HALVES)
                apart(ve, gate)
                for s in range(HALVES):
                    ve.bn_aggr(m[t.p][:, s, :], st[t.p][:, s, :]).then_inc(m_s, 1)

            def newton_step(t, m, r, nw, r_s, nw_s):
                wait(ve, r_s, t.n + 1)
                ve.scalar_tensor_tensor(nw[t.p][:], m[t.p][:, :, 1], LN_EPS, r[t.p][:], ALU.add, ALU.mult).then_inc(nw_s, 1)
                wait(ve, nw_s, t.n * 3 + 1)
                ve.scalar_tensor_tensor(nw[t.p][:], nw[t.p][:], -0.5, r[t.p][:], ALU.mult, ALU.mult).then_inc(nw_s, 1)
                wait(ve, nw_s, t.n * 3 + 2)
                ve.scalar_tensor_tensor(nw[t.p][:], nw[t.p][:], 1.5, r[t.p][:], ALU.add, ALU.mult).then_inc(nw_s, 1)

            def normed(t, src, m, nw, dst, nw_s, dst_s):
                wait(ve, nw_s, t.n * 3 + 3)
                for s in range(HALVES):
                    ve.tensor_scalar(dst[t.p][:, s, :], src[:, s, :], m[t.p][:, s, 0:1], nw[t.p][:, s:s + 1],
                                     ALU.subtract, ALU.mult).then_inc(dst_s, 1)

            def normed0(t):
                wait(ve, enc_ps, t.n - 1)
                normed(t, x_in[t.p], mv, newton, xn, nw_done, xn_done)

            def normed1(t):
                wait(ve, x1t_ps, t.n - 1)
                wait(ve, stored[t.p], t.h * 16)
                normed(t, x1[t.p], mv1, newton1, xn1, nw1_done, xn1_done)

            def context(t):
                wait(ve, loaded[t.p], (t.h + 1) * LOADS)
                wait(ve, sim_ps, t.n - 1)
                for k in range(DC):
                    ve.tensor_scalar(simw[t.p][:, k, :], ct[t.p][:, k, :], wsim[:, 2, k:k + 1], wsim[:, 0, k:k + 1],
                                     ALU.mult, ALU.add).then_inc(simw_done, 1)
                moments(t, x_in[t.p], stats, mv, st_done, mv_done)

            def newton0(t):
                newton_step(t, mv, rstd, newton, rs_done, nw_done)

            def sims(t):
                wait(ve, rowb_done, t.n + 1)
                wait(ve, exp_done, (t.n - 1) * HALVES)
                for s in range(HALVES):
                    ve.tensor_tensor(sim[t.p][:, s, :], ps_sim[:, s, 0:CTX], rowb[t.p][:], ALU.add).then_inc(sim_done, 1)
                wait(ve, sim_done, (t.n + 1) * HALVES)
                wait(ve, row_ps, t.n - 1)
                ve.tensor_reduce(mx[t.p][:], sim[t.p][:], AX.X, ALU.max).then_inc(mx_done, 1)
                wait(ve, mx_done, t.n + 1)
                ve.tensor_scalar(nmx[t.p][:], mx[t.p][:], -1.0, None, ALU.mult).then_inc(nmx_done, 1)

            def probs_norm(t):
                wait(ve, exp_done, (t.n + 1) * HALVES)
                ve.reciprocal(prec[t.p][:], psums[t.p][:]).then_inc(prec_done, 1)
                wait(ve, prec_done, t.n + 1)
                wait(ve, at_ps, t.n - 1)
                for s in range(HALVES):
                    ve.tensor_scalar(probs_n[t.p][:, s, :], probs[t.p][:, s, :], prec[t.p][:, s:s + 1], None,
                                     ALU.mult).then_inc(pn_done, 1)

            def peak(t):
                wait(ve, row_ps, t.n + 1)
                ve.tensor_reduce(gm[t.p][:], ps_row[0:1, 0:SEQ], AX.X, ALU.max).then_inc(gm_done, 1)
                wait(ve, gm_done, t.n + 1)
                wait(ve, brow_done, t.n - 1)
                ve.tensor_scalar(ngm[t.p][:], gm[t.p][:], -1.0, None, ALU.mult).then_inc(ngm_done, 1)

            def row_norm(t):
                wait(ve, brow_done, t.n + 1)
                ve.reciprocal(brec[t.p][:], bsum[t.p][:]).then_inc(brec_done, 1)
                wait(ve, brec_done, t.n + 1)
                wait(ve, bc_ps, t.n - 1)
                ve.tensor_scalar(brow_n[t.p][:], brow[t.p][:], brec[t.p][:], None, ALU.mult).then_inc(bn_done, 1)

            def product(t):
                wait(ve, hqh_done, t.n + 1)
                wait(ve, enc_sb, t.n + 1)
                wait(ve, prh_done, t.n - 1)
                wait(ve, prl_done, t.n - 1)
                ve.tensor_tensor(prod[t.p][:], ps_hq[:], enc_t[t.p][:], ALU.mult).then_inc(pr_done, 1)
                wait(ve, out_ps, t.n - 1)
                ve.tensor_tensor(hq_lo[t.p][:], ps_hq[:], hq_hi[t.p][:], ALU.subtract).then_inc(hql_done, 1)

            def weights(t):
                wait(ve, bc_ps, t.n + 1)
                for k in range(DC):
                    wait(ve, wc_done, (t.n - 1) * DC)
                    ve.tensor_tensor_reduce(bjunk[t.p][:, k, :], enc_t[t.p][:, k, :], ps_bc[:, 0:SEQ], 1.0, 0.0,
                                            ALU.mult, ALU.add, hc[t.p][:, k:k + 1]).then_inc(hc_done, 1)
                wait(ve, hc_done, (t.n + 1) * DC)
                wait(ve, wch_done, t.n - 1)
                wait(ve, wcl_done, t.n - 1)
                for k in range(DC):
                    ve.scalar_tensor_tensor(wc[t.p][:, k, :], wqv[:, 3 * DC + k, :], hc[t.p][:, k:k + 1], wqv[:, k, :],
                                            ALU.mult, ALU.add).then_inc(wc_done, 1)

            def add(t):
                wait(ve, out_ps, t.n + 1)
                wait(ve, xs_done, t.n + 1)
                wait(ve, xn1_done, (t.n - 1) * HALVES)
                wait(ve, stored_x[t.p], t.h * 16)
                ve.tensor_tensor(x1[t.p][:], ps_out[:], xb[t.p][:], ALU.add).then_inc(x1_done, 1)
                wait(ve, x1_done, t.n + 1)
                moments(t, x1[t.p], stats1, mv1, st1_done, mv1_done)

            def newton1_step(t):
                newton_step(t, mv1, rstd1, newton1, rs1_done, nw1_done)

            def route(t):
                wait(ve, lg_ps, t.n + 1)
                wait(ve, ix8_done, (t.n - 1) * HALVES)
                for s in range(HALVES):
                    ve.tensor_tensor(lg[t.p][:, s, :], ps_x1[:, 0, s * E0:(s + 1) * E0], router_b[:],
                                     ALU.add).then_inc(lg_done, 1)

            def largest(t):
                wait(ve, lg_done, (t.n + 1) * HALVES)
                apart(ve, gate)
                for s in range(HALVES):
                    ve.max(mx8[t.p][:, s, :], lg[t.p][:, s, :]).then_inc(mx8_done, 1)

            def places(t):
                wait(ve, mx8_done, (t.n + 1) * HALVES)
                apart(ve, gate)
                for s in range(HALVES):
                    ve.max_index(ix8[t.p][:, s, :], mx8[t.p][:, s, :], lg[t.p][:, s, :]).then_inc(ix8_done, 1)

            def keep(t):
                wait(ve, ix8_done, (t.n + 1) * HALVES)
                apart(ve, gate)
                own = bass.ds(t.n * HALVES, HALVES)
                ve.tensor_copy(logits[:, own, :], lg[t.p][:]).then_inc(keep_done, 1)
                ve.tensor_copy(top2[:, own, :], mx8[t.p][:, :, 0:TOP0]).then_inc(keep_done, 1)
                ve.tensor_copy(exp2[:, own, :], ix8[t.p][:, :, 0:TOP0]).then_inc(keep_done, 1)

            pipelined(ve, [[(4, context), (7, newton0), (10, normed0)],
                           [(3, sims), (5, peak), (6, probs_norm), (8, row_norm), (12, weights), (14, product)],
                           [],
                           [(0, add), (1, newton1_step), (2, normed1), (9, route), (11, largest), (13, places), (15, keep)]], BATCH)


def phase_experts(nc, env):
    a, consts, tri_bf, ones_bf, gate = (env[k] for k in ("a", "consts", "tri_bf", "ones_bf", "gate"))
    logits, top2, exp2, w_own, slot_own, xn1_d, y0_d = (env[k] for k in (
        "logits", "top2", "exp2", "w_own", "slot_own", "xn1_d", "y0_d"))
    NT = TOP0 * TILES
    CHUNK = NT // 4
    ctx = ExitStack()
    with ctx:
        def sb(name, shape, dt):
            return ctx.enter_context(nc.sbuf_tensor("e_" + name, shape, dt))

        def two(name, shape, dt):
            return [sb(f"{name}{i}", shape, dt) for i in range(2)]

        def sem(name):
            env["sems"].append(nc.alloc_semaphore(name="e_" + name))
            return env["sems"][-1]

        ident = consts[:, K_ID:K_ID + P]
        expl = sb("expl", [P, TILES, E0], F32)
        zsum = sb("zsum", [P, TILES], F32)
        zrec = sb("zrec", [P, TILES], F32)
        pr = sb("pr", [P, TOP0, TILES], F32)
        den = sb("den", [P, TILES], F32)
        wt = sb("wt", [P, TOP0, TILES], F32)
        valid = sb("valid", [P, TOP0, TILES], F32)
        hot = sb("hot", [P, TOP0, TILES, E0], F32)
        hot_bf = sb("hot_bf", [P, NT * E0], BF16)
        total = sb("total", [P, NT * E0], F32)
        ran = sb("ran", [P, NT * E0], F32)
        ones_nt = sb("ones_nt", [P, NT], F32)
        before = sb("before", [P, NT * E0], F32)
        pos = sb("pos", [P, NT], F32)
        keep = sb("keep", [P, NT], F32)
        slot = sb("slot", [P, NT], F32)
        slot_i = sb("slot_i", [P, NT], I32)
        hi_i = sb("hi_i", [P, NT], I32)
        lo_i = sb("lo_i", [P, NT], I32)
        hi = sb("hi", [P, NT], F32)
        lo = sb("lo", [P, NT], F32)
        tile_no = sb("tile_no", [P, TILES], F32)
        in_lo = sb("in_lo", [P, 2, CHUNK, P], BF16)
        xg_all = sb("xg_all", [P, 2, SLOT_TILES0, D], F32)
        hid_all = sb("hid_all", [P, 2, SLOTS0], F32)
        is_hi = hid_all[:].rearrange("p a b -> p (a b)").bitcast(BF16).rearrange("p (n h) -> p n h", h=HI0)
        in_hi = xg_all[:].rearrange("p a b c -> p (a b c)").bitcast(BF16).rearrange("p (n a h) -> p n a h", a=2, h=HI0)
        tok = sb("tok", [P, 2, HI0], F32)
        tok_of = sb("tok_of", [P, HI0], U32)
        fc1 = sb("fc1", [P, DC, HID0], F32)
        fc2 = sb("fc2", [P, HC0, D], F32)
        fc1_hi, fc1_lo = two("fc1_hi", [P, DC, HID0], F32R), two("fc1_lo", [P, DC, HID0], F32R)
        fc2_hi, fc2_lo = [sb("fc2_hi", [P, HC0, D], F32R)] * 2, [sb("fc2_lo", [P, HC0, D], F32R)] * 2
        b1 = two("b1", [P, HC0], F32)
        b2 = two("b2", [P, D], F32)
        ls = two("ls", [P, D], F32)
        b2ls = [sb("b2ls", [P, D], F32)] * 2
        own = two("own", [P, SLOT_TILES0], U32)
        xg = [xg_all[:, i] for i in range(2)]
        xt_hi, xt_lo = two("xt_hi", [P, DC, SLOTS0], F32R), two("xt_lo", [P, DC, SLOTS0], F32R)
        hid = [hid_all[:, i] for i in range(2)]
        hid_hi, hid_lo = sb("hid_hi", [P, HC0, SLOTS0], F32R), sb("hid_lo", [P, HC0, SLOTS0], F32R)
        ys = two("ys", [P, D], F32)
        yo = two("yo", [P, D], F32)

        ps_x = [ctx.enter_context(nc.psum_tensor(f"e_ps_x{i}", [P, 512], F32)) for i in range(2)]
        ps_f = [ctx.enter_context(nc.psum_tensor(f"e_ps_f{i}", [P, 2, 512], F32)) for i in range(2)]
        ps_y = [ctx.enter_context(nc.psum_tensor(f"e_ps_y{i}", [P, 512], F32)) for i in range(2)]

        s_chain, s_exp, s_hot, s_pre, s_oh, s_tok, s_own, s_tile = (sem(n) for n in (
            "s_chain", "s_exp", "s_hot", "s_pre", "s_oh", "s_tok", "s_own", "s_tile"))
        (w_ld, w_hi, w_lo, b_ld, b2_done, own_done, xt_ps, xth_done, xtl_done, f_ps, hid_done, hh_done, hl_done,
         y_ps, ys_done, yt_done, yo_done, w2_ld, w2_hi, w2_lo) = (sem(n) for n in (
             "w_ld w_hi w_lo b_ld b2_done own_done xt_ps xth_done xtl_done f_ps hid_done hh_done hl_done "
             "y_ps ys_done yt_done yo_done w2_ld w2_hi w2_lo").split())
        gathered = [sem("gathered0"), sem("gathered1")]
        y_st = [sem("y_st0"), sem("y_st1")]
        CH = HC0
        ST = SLOT_TILES0
        TURN_SLOTS = [5, 5.2] + [c + 4.4 for c in range(2, ST)]

        block = ctx.enter_context(nc.Block())

        @block.sync
        def _(sp):
            def load(t):
                e = bass.ds(t.n, 1)
                wait_apart(sp, w_ld, t.n * 16, gate)
                wait_apart(sp, w_hi, t.n, gate)
                wait_apart(sp, w_lo, t.n, gate)
                sp.dma_start(fc1[:], a["fc1_t"][e].rearrange("e p k h -> (e p) k h")).then_inc(w_ld, 16)
                wait_apart(sp, w2_ld, t.n * 16, gate)
                wait_apart(sp, w2_hi, t.n, gate)
                wait_apart(sp, w2_lo, t.n, gate)
                sp.dma_start(fc2[:], a["fc2_t"][e].rearrange("e p m c -> (e p) m c")).then_inc(w2_ld, 16)
                wait_apart(sp, b_ld, t.n * 48, gate)
                wait_apart(sp, hid_done, (t.n - 1) * CH, gate)
                wait_apart(sp, yo_done, (t.n - 1) * ST, gate)
                sp.dma_start(b1[t.p][:], a["fc1_b"][e].rearrange("e p m -> (e p) m")).then_inc(b_ld, 16)
                sp.dma_start(b2[t.p][:], a["fc2_b"][e].rearrange("e c -> (e c)").partition_broadcast(P)).then_inc(b_ld, 16)
                sp.dma_start(ls[t.p][:], a["ls"][e].rearrange("e c -> (e c)").partition_broadcast(P)).then_inc(b_ld, 16)

            def store(c):
                def part(t):
                    q = (t.p * ST + c) % 2
                    wait_apart(sp, yo_done, t.n * ST + c + 1, gate)
                    sp.dma_start(y0_d.rearrange("(e c p) d -> c p e d", c=ST, p=P)[c][:, bass.ds(t.n, 1), :].rearrange("p e d -> p (e d)"),
                                 yo[q][:]).then_inc(y_st[q], 16)
                return part

            pipelined(sp, [[(0, load)], [(6 + c, store(c)) for c in range(ST)]], E0)
            for q in range(2):
                sp.wait_ge(y_st[q], E0 * ST // 2 * 16)

        @block.gpsimd
        def _(pool):
            pool.iota(tile_no[:], [[1, TILES]], base=0, channel_multiplier=0,
                      allow_small_or_imprecise_dtypes=True).then_inc(s_tile, 1)

            def gather(t):
                wait(pool, own_done, t.n + 1)
                wait(pool, xt_ps, (t.n - 1) * ST)
                wait(pool, yt_done, (t.n - 1) * ST)
                apart(pool, gate)
                for c in range(ST):
                    pool.indirect_dma_start(xg[t.p][:, c, :], None, xn1_d,
                                            bass.IndirectOffsetOnAxis(ap=own[t.p][:, c:c + 1], axis=0)
                                            ).then_inc(gathered[t.p], 16)

            def split_up(t):
                wait(pool, w_ld, (t.n + 1) * 16)
                wait(pool, w_hi, t.n + 1)
                wait(pool, f_ps, (t.n - 1) * CH)
                pool.tensor_tensor(fc1_lo[t.p][:], fc1[:], fc1_hi[t.p][:], ALU.subtract).then_inc(w_lo, 1)

            def split_later_up(t):
                if not isinstance(t.n, int) or t.n > 0:
                    split_up(t)

            def split_down(t):
                wait(pool, w2_ld, (t.n + 1) * 16)
                wait(pool, w2_hi, t.n + 1)
                wait(pool, y_ps, t.n * ST)
                pool.tensor_tensor(fc2_lo[t.p][:], fc2[:], fc2_hi[t.p][:], ALU.subtract).then_inc(w2_lo, 1)

            split_up(At(0, 0, 0))
            pipelined(pool, [[(0, gather), (4, split_later_up)], [(-1, split_down)]], E0)

        @block.tensor
        def _(pe):
            pe.wait_ge(s_hot, 1)
            pe.matmul(ps_y[0][:], tri_bf[:], hot_bf[:], start=True, stop=True)
            pe.matmul(ps_y[1][:], ones_bf[:], hot_bf[:], start=True, stop=True).then_inc(s_pre, 1)
            for c in range(NT // CHUNK):
                pe.wait_ge(s_oh, c + 1)
                for n in range(CHUNK):
                    mm = pe.matmul(ps_x[0][:, 0:2 * HI0], in_lo[:, c % 2, n, :],
                                   in_hi[:, c * CHUNK + n, :, :].rearrange("p a b -> p (a b)"),
                                   start=c == 0 and n == 0, stop=c == NT // CHUNK - 1 and n == CHUNK - 1)
                mm.then_inc(s_tok, 1)

            def turn(c):
                def part(t):
                    wait(pe, gathered[t.p], (t.h + 1) * ST * 16)
                    q = (t.p * ST + c) % 2
                    wait(pe, xtl_done, t.n * ST + c - 1)
                    for k in range(DC):
                        mm = pe.transpose(ps_x[q][:, k * P:(k + 1) * P], xg[t.p][:, c, k * P:(k + 1) * P], ident)
                    mm.then_inc(xt_ps, 1)
                return part

            def up(t):
                wait(pe, xtl_done, (t.n + 1) * ST)
                wait(pe, w_lo, t.n + 1)
                for m in range(CH):
                    wait(pe, hid_done, t.n * CH + m - 1)
                    for n in range(2):
                        i = 0
                        for k in range(DC):
                            for l, r in ((fc1_hi, xt_hi), (fc1_hi, xt_lo), (fc1_lo, xt_hi)):
                                mm = pe.matmul(ps_f[m % 2][:, n, 0:HALF0], l[t.p][:, k, m * P:(m + 1) * P],
                                               r[t.p][:, k, n * HALF0:(n + 1) * HALF0], start=i == 0, stop=i == 3 * DC - 1)
                                i += 1
                    mm.then_inc(f_ps, 1)

            def down(c):
                def part(t):
                    if c == 0:
                        wait(pe, w2_lo, t.n + 1)
                    q = (t.p * ST + c) % 2
                    wait(pe, ys_done, t.n * ST + c - 1)
                    i = 0
                    for m in range(CH):
                        if c == 0:
                            wait(pe, hl_done, t.n * CH + m + 1)
                        for l, r in ((hid_hi, fc2_hi), (hid_hi, fc2_lo), (hid_lo, fc2_hi)):
                            mm = pe.matmul(ps_y[q][:, 0:D], l[:, m, c * P:(c + 1) * P], r[t.p][:, m, :],
                                           start=i == 0, stop=i == 3 * CH - 1)
                            i += 1
                    mm.then_inc(y_ps, 1)
                return part

            pipelined(pe, [[(TURN_SLOTS[c], turn(c)) for c in range(ST)], [(0, up)] + [(6 + c, down(c)) for c in range(ST)]], E0)

        @block.scalar
        def _(act):
            act.preload_act_table_set("exp_and_others")
            act.wait_ge(w_ld, 16)
            act.activation(fc1_hi[0][:], fc1[:], ACT.Copy).then_inc(w_hi, 1)
            act.wait_ge(s_chain, 2)
            act.activation(expl[:], expl[:], ACT.Exp).then_inc(s_exp, 1)
            act.activation(pr[:, 1, :], pr[:, 1, :], ACT.Exp).then_inc(s_exp, 1)

            def split_up(t):
                wait(act, w_ld, (t.n + 1) * 16)
                wait(act, f_ps, (t.n - 1) * CH)
                wait(act, w_lo, t.n - 1)
                act.activation(fc1_hi[t.p][:], fc1[:], ACT.Copy).then_inc(w_hi, 1)

            def split_later_up(t):
                if not isinstance(t.n, int) or t.n > 0:
                    split_up(t)

            def split_down(t):
                wait(act, w2_ld, (t.n + 1) * 16)
                wait(act, y_ps, t.n * ST)
                wait(act, w2_lo, t.n)
                act.activation(fc2_hi[t.p][:], fc2[:], ACT.Copy).then_inc(w2_hi, 1)

            def turned(c):
                def part(t):
                    q = (t.p * ST + c) % 2
                    wait(act, xt_ps, t.n * ST + c + 1)
                    if c == 0:
                        wait(act, f_ps, (t.n - 1) * CH)
                    act.activation(xt_hi[t.p][:, :, c * P:(c + 1) * P], ps_x[q][:, 0:DC * P].rearrange("p (k s) -> p k s", k=DC),
                                   ACT.Copy).then_inc(xth_done, 1)
                return part

            def gelu(m):
                def part(t):
                    wait(act, b_ld, (t.n + 1) * 48)
                    wait(act, f_ps, t.n * CH + m + 1)
                    wait(act, hl_done, t.n * CH + m - 1)
                    act.activation(hid[m % 2].rearrange("p (n s) -> p n s", n=2), ps_f[m % 2][:, :, 0:HALF0], ACT.Gelu,
                                   bias=b1[t.p][:, m:m + 1]).then_inc(hid_done, 1)
                return part

            pipelined(act, [[(4.5, split_later_up)] + [(TURN_SLOTS[c], turned(c)) for c in range(ST)],
                            [(-1, split_down)] + [(m / 2, gelu(m)) for m in range(CH)]], E0)

        @block.vector
        def _(ve):
            n_chain = [0]

            def link(ins):
                n_chain[0] += 1
                ins.then_inc(s_chain, 1)
                ve.wait_ge(s_chain, n_chain[0])

            def wide(ap, n):
                return ap.unsqueeze(2).to_broadcast([P, TILES, n])

            ve.tensor_tensor(expl[:], logits[:], wide(top2[:, :, 0], E0), ALU.subtract).then_inc(s_chain, 1)
            n_chain[0] += 1
            link(ve.tensor_tensor(pr[:, 1, :], top2[:, :, 1], top2[:, :, 0], ALU.subtract))
            ve.memset(ones_nt[:], 1.0).then_inc(s_own, 1)
            ve.wait_ge(s_exp, 2)
            link(ve.tensor_reduce(zsum[:], expl[:], AX.X, ALU.add))
            link(ve.reciprocal(pr[:, 0, :], zsum[:]))
            link(ve.tensor_tensor(pr[:, 1, :], pr[:, 1, :], pr[:, 0, :], ALU.mult))
            link(ve.scalar_tensor_tensor(den[:], pr[:, 0, :], W_EPS, pr[:, 1, :], ALU.add, ALU.add))
            link(ve.reciprocal(zrec[:], den[:]))
            for k in range(TOP0):
                link(ve.tensor_tensor(wt[:, k, :], pr[:, k, :], zrec[:], ALU.mult))
            link(ve.tensor_scalar(valid[:], wt[:], W_EPS, None, ALU.is_gt))
            for k in range(TOP0):
                link(ve.tensor_tensor(hot[:, k], wide(exp2[:, :, k], E0),
                                      consts[:, K_IOTA:K_IOTA + E0].unsqueeze(1).to_broadcast([P, TILES, E0]), ALU.is_equal))
                link(ve.tensor_tensor(hot[:, k], hot[:, k], wide(valid[:, k, :], E0), ALU.mult))
            ve.tensor_copy(hot_bf[:], hot[:].rearrange("p k t e -> p (k t e)")).then_inc(s_hot, 1)
            ve.wait_ge(s_pre, 1)
            ve.wait_ge(s_own, 1)
            link(ve.tensor_copy(total[:], ps_y[1][:]))
            for e in range(E0):
                v = slice(e, NT * E0, E0)
                link(ve.tensor_tensor_scan(ran[:, v], ones_nt[:], total[:, v], 0.0, ALU.mult, ALU.add))
            link(ve.tensor_tensor(before[:], ran[:], total[:], ALU.subtract))
            link(ve.tensor_tensor(before[:], before[:], ps_y[0][:], ALU.add))
            link(ve.tensor_tensor(before[:], before[:], hot[:].rearrange("p k t e -> p (k t e)"), ALU.mult))
            link(ve.tensor_reduce(pos[:], before[:].rearrange("p (n e) -> p n e", e=E0), AX.X, ALU.add))
            link(ve.tensor_scalar(keep[:], pos[:], float(CAP0), None, ALU.is_lt))
            link(ve.tensor_tensor(keep[:], keep[:], valid[:].rearrange("p k t -> p (k t)"), ALU.mult))
            for k in range(TOP0):
                n = slice(k * TILES, (k + 1) * TILES)
                link(ve.scalar_tensor_tensor(slot[:, n], exp2[:, :, k], float(SLOTS0), pos[:, n], ALU.mult, ALU.add))
                link(ve.tensor_tensor(slot[:, n], slot[:, n], keep[:, n], ALU.mult))
                link(ve.tensor_copy(slot_own[:, :, k], slot[:, n]))
                link(ve.tensor_tensor(w_own[:, :, k], wt[:, k, :], keep[:, n], ALU.mult))
            link(ve.tensor_copy(slot_i[:], slot[:]))
            link(ve.tensor_scalar(hi_i[:], slot_i[:], 7, None, ALU.logical_shift_right))
            link(ve.tensor_scalar(lo_i[:], slot_i[:], P - 1, None, ALU.bitwise_and))
            link(ve.tensor_copy(hi[:], hi_i[:]))
            link(ve.tensor_copy(lo[:], lo_i[:]))
            link(ve.scalar_tensor_tensor(lo[:], lo[:], 1.0, keep[:], ALU.add, ALU.mult))
            link(ve.tensor_scalar(lo[:], lo[:], -1.0, None, ALU.add))
            link(ve.tensor_tensor(is_hi, hi[:].unsqueeze(2).to_broadcast([P, NT, HI0]),
                                  consts[:, K_IOTA:K_IOTA + HI0].unsqueeze(1).to_broadcast([P, NT, HI0]), ALU.is_equal))
            ve.wait_ge(s_tile, 1)
            for k in range(TOP0):
                n = slice(k * TILES, (k + 1) * TILES)
                link(ve.tensor_tensor(in_hi[:, n, 0, :], is_hi[:, n, :], wide(tile_no[:], HI0), ALU.mult))
            link(ve.tensor_scalar(in_hi[:, :, 1, :], is_hi, consts[:, K_P:K_P + 1], None, ALU.mult))
            for c in range(NT // CHUNK):
                if c >= 2:
                    ve.wait_ge(s_tok, c - 1)
                ve.tensor_tensor(in_lo[:, c % 2], lo[:, c * CHUNK:(c + 1) * CHUNK].unsqueeze(2).to_broadcast([P, CHUNK, P]),
                                 consts[:, K_IOTA:K_IOTA + P].unsqueeze(1).to_broadcast([P, CHUNK, P]),
                                 ALU.is_equal).then_inc(s_oh, 1)
            ve.wait_ge(s_tok, NT // CHUNK)
            link(ve.tensor_copy(tok[:], ps_x[0][:, 0:2 * HI0].rearrange("p (a b) -> p a b", a=2)))
            link(ve.scalar_tensor_tensor(tok_of[:], tok[:, 0, :], float(P), tok[:, 1, :], ALU.mult, ALU.add))

            def pick(t):
                wait(ve, gathered[t.p], t.h * ST * 16)
                ve.tensor_copy(own[t.p][:], tok_of[:, bass.ds(t.n * ST, ST)]).then_inc(own_done, 1)

            def turned(c):
                def part(t):
                    q = (t.p * ST + c) % 2
                    wait(ve, xth_done, t.n * ST + c + 1)
                    if c == 0:
                        wait(ve, f_ps, (t.n - 1) * CH)
                    ve.tensor_tensor(xt_lo[t.p][:, :, c * P:(c + 1) * P], ps_x[q][:, 0:DC * P].rearrange("p (k s) -> p k s", k=DC),
                                     xt_hi[t.p][:, :, c * P:(c + 1) * P], ALU.subtract).then_inc(xtl_done, 1)
                return part

            def hidden(m):
                def part(t):
                    wait(ve, y_ps, t.n * ST)
                    wait(ve, hid_done, t.n * CH + m + 1)
                    ve.tensor_copy(hid_hi[:, m, :], hid[m % 2]).then_inc(hh_done, 1)
                    wait(ve, hh_done, t.n * CH + m + 1)
                    ve.tensor_tensor(hid_lo[:, m, :], hid[m % 2], hid_hi[:, m, :], ALU.subtract).then_inc(hl_done, 1)
                return part

            def bias(t):
                wait(ve, b_ld, (t.n + 1) * 48)
                ve.tensor_tensor(b2ls[t.p][:], b2[t.p][:], ls[t.p][:], ALU.mult).then_inc(b2_done, 1)

            def rows(c):
                def part(t):
                    q = (t.p * ST + c) % 2
                    wait(ve, y_ps, t.n * ST + c + 1)
                    ve.tensor_tensor(ys[q][:], ps_y[q][:, 0:D], ls[t.p][:], ALU.mult).then_inc(ys_done, 1)
                    wait(ve, ys_done, t.n * ST + c + 1)
                    if c == 0:
                        wait(ve, b2_done, t.n + 1)
                    if t.p == 0:
                        wait(ve, y_st[q], t.h * ST * 16 + (c // 2) * 16)
                    else:
                        wait(ve, y_st[q], t.h * ST * 16 + ((ST + c) // 2) * 16)
                    ve.tensor_tensor(ys[q][:], ys[q][:], b2ls[t.p][:], ALU.add).then_inc(yt_done, 1)
                    wait(ve, yt_done, t.n * ST + c + 1)
                    ve.tensor_tensor(yo[q][:], ys[q][:], xg[t.p][:, c, :], ALU.add).then_inc(yo_done, 1)
                return part

            pipelined(ve, [[(-1, pick)] + [(TURN_SLOTS[c], turned(c)) for c in range(ST)],
                           [(m / 2 + 0.1, hidden(m)) for m in range(CH)] + [(5.5, bias)] +
                           [(6.7 + c, rows(c)) for c in range(ST)]], E0)


def phase_heads(nc, env):
    a, x_res, consts, tri_bf, ones_bf, gate = (env[k] for k in ("a", "x_res", "consts", "tri_bf", "ones_bf", "gate"))
    w_own, slot_own, y0_d, rows_d, xn3_d = (env[k] for k in ("w_own", "slot_own", "y0_d", "rows_d", "xn3_d"))
    NC = HALVES * TOP0
    NR = HALVES * TOP1
    NG = HALVES * GROUPS
    ctx = ExitStack()
    with ctx:
        def sb(name, shape, dt):
            return ctx.enter_context(nc.sbuf_tensor("h_" + name, shape, dt))

        def two(name, shape, dt):
            return [sb(f"{name}{i}", shape, dt) for i in range(2)]

        def sem(name):
            env["sems"].append(nc.alloc_semaphore(name="h_" + name))
            return env["sems"][-1]

        ident = consts[:, K_ID:K_ID + P]
        wq, wk, wv, wo = (sb(n, [P, DC, D], F32) for n in ("wq", "wk", "wv", "wo"))
        bq, bk = sb("bq", [P, DC], F32), sb("bk", [P, DC], F32)
        bqs = sb("bqs", [P, DC], F32)
        bv, bo = sb("bv", [P, D], F32), sb("bo", [1, D], F32)
        ones_row = sb("ones_row", [1, P], F32)
        gate_w16, gate_w = sb("gate_w16", [P, DC, E1], BF16), sb("gate_w", [P, DC, E1], F32)
        gate_b = sb("gate_b", [P, E1], F32)
        ident_bf = sb("ident_bf", [P, P], BF16)
        causal_bf = sb("causal_bf", [P, HPB, CTX], BF16)
        eps = sb("eps", [P, 1], F32)
        tok_no = sb("tok_no", [P, TILES], F32)
        counts = two("counts", [P, E1], BF16)

        slots = two("slots", [P, NC], U32)
        wts = two("wts", [P, NC], F32)
        yg = two("yg", [P, NC, D], F32)
        ct = two("ct", [P, DC, CTX], F32)
        stats, mv = two("stats", [P, HALVES, 6], F32), two("mv", [P, HALVES, 2], F32)
        lnv, rstd, newton = (two(n, [P, HALVES], F32) for n in ("lnv", "rstd", "newton"))
        stats3, mv3 = two("stats3", [P, HALVES, 6], F32), two("mv3", [P, HALVES, 2], F32)
        lnv3, rstd3, newton3 = (two(n, [P, HALVES], F32) for n in ("lnv3", "rstd3", "newton3"))
        xn = two("xn", [P, HALVES, D], F32)
        x_t = two("x_t", [P, DC, SEQ], F32)
        qf = [sb("qf", [P, DC, SEQ], F32)] * 2
        q_hi, q_lo = two("q_hi", [P, DC, SEQ], F32R), two("q_lo", [P, DC, SEQ], F32R)
        kf, k_hi, k_lo = (sb(n, [P, DC, CTX], d) for n, d in (("kf", F32), ("k_hi", F32R), ("k_lo", F32)))
        kd_hi, kd_lo = two("kd_hi", [P, DC, HPC, CTX], F32R), two("kd_lo", [P, DC, HPC, CTX], F32R)
        vm = two("vm", [CTX, HEADS, 2 * HD], F32)
        mx = two("mx", [P, HPB], F32)
        sums, rec = two("sums", [P, HALVES, HEADS], F32), two("rec", [P, HALVES, HEADS], F32)
        recx = sb("recx", [P, HALVES, HEADS, HD], F32)
        pr = two("pr", [P, HPB, CTX], F32)
        pt = sb("pt", [CTX, HEADS, SEQ], F32)
        o_sb, o_t = sb("o_sb", [P, DC, SEQ], F32), two("o_t", [P, DC, SEQ], F32)
        row = two("row", [P, HALVES, ROW], F32)
        x3_t = [sb("x3_t", [P, DC, SEQ], F32)] * 2
        ex, sg, sel = (two(n, [P, HALVES, E1], F32) for n in ("ex", "sg", "sel"))
        top8, idx8 = two("top8", [P, HALVES, 8], F32), two("idx8", [P, HALVES, 8], U32)
        idf = two("idf", [P, HALVES, TOP1], F32)
        hot = two("hot", [P, NR, E1], F32)
        hot_any = two("hot_any", [P, HALVES, E1], BF16)
        own = [sb("own", [P, NR, E1], F32)] * 2
        wk8, wsum, wrec = two("wk8", [P, NR], F32), two("wsum", [P, HALVES], F32), two("wrec", [P, HALVES], F32)
        csum = sb("csum", [P, E1], BF16)
        pfx = [sb("pfx", [P, HALVES, E1], F32)] * 2
        pos, over = two("pos", [P, NR], F32), two("over", [P, NR], F32)
        dest = two("dest", [P, NR], U32)

        def bank(name):
            return ctx.enter_context(nc.psum_tensor("h_" + name, [P, 512], F32))

        ps_s = [bank(f"ps_s{i}") for i in range(3)]
        ps_p, ps_q, ps_kv, ps_o, ps_w = bank("ps_p"), bank("ps_q"), bank("ps_kv"), bank("ps_o"), bank("ps_w")

        names = ("par prep tokn yi_done mixed0 mixed st_done mv_done ln_done rs_done nw_done xn_done xt_ps xt_sb q_ps "
                 "qf_done qh_done ql_done kv_ps kf_done kh_done kl_done kdh_done kdl_done v_done s_ps mx_done "
                 "exp_done rec_done recx_done r_ps p_ps pt_done o_ps ot_done w_ps o_sb x_done st3_done mv3_done ln3_done "
                 "rs3_done nw3_done xn3_done x3t_ps x3t_sb lg_ps ex_done e1_done sg_done sel_done t8_done i8_done "
                 "idf_done hot_done any_done own_done wk_done ws_done wr_done wn_done cs_done cnt_done pf_ps pf_done "
                 "own2_done pos_done ov_done dest_done rowx_done zero").split()
        S = {n: sem(n) for n in names}
        loaded = [sem("loaded0"), sem("loaded1")]
        yin = [sem("yin0"), sem("yin1")]
        sent = [sem("sent0"), sem("sent1")]
        stored = [sem("stored0"), sem("stored1")]
        PARAMS = 12
        ROWX = 3

        def tiles(t):
            return x_res[:, bass.ds(t.n * HALVES, HALVES), :]

        block = ctx.enter_context(nc.Block())

        @block.sync
        def _(sp):
            for dst, src in ((wk[:], a["wk_t"]), (wv[:], a["wv_t"]), (wq[:], a["wq_t"]), (wo[:], a["wo_t"]),
                             (bq[:], a["bq"]), (bk[:], a["bk"]), (bv[:], a["bv"].partition_broadcast(P)),
                             (bo[:], a["bo"]), (gate_w16[:], a["gate_w"]),
                             (gate_b[:], a["gate_b"].partition_broadcast(P))):
                sp.dma_start(dst, src).then_inc(S["par"], 16)

            def load(t):
                wait_apart(sp, loaded[t.p], t.h * 16, gate)
                wait_apart(sp, S["kv_ps"], t.n - 1, gate)
                sp.dma_start(ct[t.p][:], a["ctx_t"][bass.ds(t.n, 1)].rearrange("a p k j -> (a p) k j")).then_inc(loaded[t.p], 16)

            def store(t):
                wait_apart(sp, stored[t.p], t.h * 16, gate)
                wait_apart(sp, S["xn3_done"], (t.n + 1) * HALVES, gate)
                sp.dma_start(xn3_d.rearrange("(t p) d -> p t d", p=P)[:, bass.ds(t.n * HALVES, HALVES), :],
                             row[t.p][:, :, 0:D]).then_inc(stored[t.p], 16)

            pipelined(sp, [[(0, load)],
                           [],
                           [],
                           [(1, store)]], BATCH)
            for q in range(2):
                sp.wait_ge(stored[q], BATCH // 2 * 16)

        @block.gpsimd
        def _(pool):
            pool.iota(tok_no[:], [[P, TILES]], base=0, channel_multiplier=1,
                      allow_small_or_imprecise_dtypes=True).then_inc(S["tokn"], 1)

            def gather(t):
                wait(pool, S["yi_done"], (t.n + 1) * 2)
                wait(pool, S["mixed"], (t.n - 1) * NC)
                apart(pool, gate)
                for c in range(NC):
                    pool.indirect_dma_start(yg[t.p][:, c, :], None, y0_d,
                                            bass.IndirectOffsetOnAxis(ap=slots[t.p][:, c:c + 1], axis=0)
                                            ).then_inc(yin[t.p], 16)

            def split_k(t):
                wait(pool, S["kf_done"], (t.n + 1) * DC)
                wait(pool, S["kh_done"], (t.n + 1) * DC)
                wait(pool, S["kdl_done"], t.n * DC)
                pool.tensor_tensor(k_lo[:], kf[:], k_hi[:], ALU.subtract).then_inc(S["kl_done"], 1)

            def spread_k(t):
                wait(pool, S["kl_done"], t.n + 1)
                wait(pool, S["s_ps"], (t.n - 1) * NG)
                for c in range(DC):
                    pool.tensor_tensor(kd_lo[t.p][:, c], k_lo[:, c, :].unsqueeze(1).to_broadcast([P, HPC, CTX]),
                                       consts[:, K_HEAD:K_HEAD + HPC].unsqueeze(2).to_broadcast([P, HPC, CTX]),
                                       ALU.mult).then_inc(S["kdl_done"], 1)

            def split_q(t):
                wait(pool, S["qf_done"], (t.n + 1) * DC)
                wait(pool, S["qh_done"], (t.n + 1) * DC)
                wait(pool, S["s_ps"], (t.n - 1) * NG)
                pool.tensor_tensor(q_lo[t.p][:], qf[t.p][:], q_hi[t.p][:], ALU.subtract).then_inc(S["ql_done"], 1)

            def scatter(t):
                wait(pool, S["dest_done"], t.n + 1)
                wait(pool, S["rowx_done"], (t.n + 1) * ROWX)
                wait(pool, S["xn3_done"], (t.n + 1) * HALVES)
                apart(pool, gate)
                for n in range(NR):
                    pool.indirect_dma_start(rows_d, bass.IndirectOffsetOnAxis(ap=dest[t.p][:, n:n + 1], axis=0),
                                            row[t.p][:, n // TOP1, :], None, bounds_check=SLOTS1 - 1,
                                            oob_is_err=False).then_inc(sent[t.p], 16)

            pipelined(pool, [[(3, gather)],
                             [(0, split_k), (1, spread_k), (4, split_q)],
                             [],
                             [],
                             [],
                             [(2, scatter)]], BATCH)
            for q in range(2):
                pool.wait_ge(sent[q], BATCH // 2 * NR * 16)

        @block.tensor
        def _(pe):
            pe.wait_ge(S["par"], 10 * 16)
            pe.wait_ge(S["prep"], 1)

            def keys_values(t):
                wait(pe, loaded[t.p], (t.h + 1) * 16)
                wait(pe, S["ot_done"], t.n - 2)
                wait(pe, S["kf_done"], t.n * DC)
                wait(pe, S["kh_done"], t.n * DC)
                wait(pe, S["v_done"], t.n * 2)
                for o in range(DC):
                    for k in range(DC):
                        pe.matmul(ps_kv[:, o * CTX:(o + 1) * CTX], wk[:, k, o * P:(o + 1) * P], ct[t.p][:, k, :],
                                  start=k == 0, stop=k == DC - 1)
                for k in range(DC):
                    mm = pe.matmul(ps_kv[0:CTX, D:2 * D], ct[t.p][:, k, :], wv[:, k, :], start=k == 0, stop=k == DC - 1)
                mm.then_inc(S["kv_ps"], 1)

            def turn_x(t):
                wait(pe, S["xn_done"], (t.n + 1) * HALVES)
                wait(pe, S["qh_done"], t.n * DC)
                wait(pe, S["qf_done"], t.n * DC)
                for s in range(HALVES):
                    for k in range(DC):
                        mm = pe.transpose(ps_q[:, k * SEQ + s * P:k * SEQ + (s + 1) * P], xn[t.p][:, s, k * P:(k + 1) * P], ident)
                mm.then_inc(S["xt_ps"], 1)

            def queries(t):
                wait(pe, S["xt_sb"], t.n + 1)
                for o in range(DC):
                    for k in range(DC):
                        mm = pe.matmul(ps_q[:, o * SEQ:(o + 1) * SEQ], wq[:, k, o * P:(o + 1) * P], x_t[t.p][:, k, :],
                                       start=k == 0, stop=k == DC - 1)
                mm.then_inc(S["q_ps"], 1)

            def scores(n):
                def part(t):
                    s, g = n // GROUPS, n % GROUPS
                    c, h = g * HPB // HPC, g * HPB % HPC
                    if n == 0:
                        wait(pe, S["qh_done"], (t.n + 1) * DC)
                        wait(pe, S["ql_done"], t.n + 1)
                        wait(pe, S["kdh_done"], (t.n + 1) * DC)
                        wait(pe, S["kdl_done"], (t.n + 1) * DC)
                    before = n - 3 if n >= 3 else max(m for m in range(NG) if m % 3 == n) - NG
                    wait(pe, S["exp_done"], (t.n * NG + before + 1) * HPB)
                    i = 0
                    terms = ((q_hi, kd_hi), (q_hi, kd_lo), (q_lo, kd_hi))
                    for l, r in terms:
                        mm = pe.matmul(ps_s[n % 3][:, 0:HPB * CTX], l[t.p][:, c, s * P:(s + 1) * P],
                                       r[t.p][:, c, h:h + HPB, :].rearrange("p h j -> p (h j)"),
                                       start=i == 0, stop=s > 0 and i == len(terms) - 1)
                        i += 1
                    if s == 0:
                        mm = pe.matmul(ps_s[n % 3][:, 0:HPB * CTX], ident_bf[:], causal_bf[:].rearrange("p h j -> p (h j)"),
                                       start=False, stop=True)
                    mm.then_inc(S["s_ps"], 1)
                return part

            def turn(n):
                def part(t):
                    wait(pe, S["exp_done"], (t.n * NG + n + 1) * HPB)
                    wait(pe, S["pt_done"], t.n * NG + n)
                    for h in range(HPB):
                        mm = pe.transpose(ps_p[0:CTX, h * P:(h + 1) * P], pr[n % 2][:, h, :], ident)
                    mm.then_inc(S["p_ps"], 1)
                return part

            def attend(t):
                wait(pe, S["pt_done"], (t.n + 1) * NG)
                wait(pe, S["v_done"], (t.n + 1) * 2)
                wait(pe, S["o_sb"], t.n)
                for c in range(DC):
                    for odd in range(2):
                        for j in range(HPC // 2):
                            h = c * HPC + 2 * j + odd
                            mm = pe.matmul(ps_o[32 * j:32 * (j + 1), c * SEQ:(c + 1) * SEQ], vm[t.p][:, h, :], pt[:, h, :],
                                           start=odd == 0, stop=odd == 1, tile_position=(0, 32 * j),
                                           skip_group_check=True)
                mm.then_inc(S["o_ps"], 1)

            def inverse_sums(t):
                wait(pe, S["recx_done"], t.n + 1)
                later = min(t.n + 3, BATCH) if isinstance(t.n, int) else t.n + 3
                wait(pe, S["kf_done"], later * DC)
                wait(pe, S["kh_done"], later * DC)
                wait(pe, S["v_done"], later * 2)
                for s in range(HALVES):
                    for c in range(DC):
                        mm = pe.transpose(ps_kv[:, c * SEQ + s * P:c * SEQ + (s + 1) * P],
                                          recx[:, s, c * HPC:(c + 1) * HPC, :].rearrange("p h x -> p (h x)"), ident)
                mm.then_inc(S["r_ps"], 1)

            def project(t):
                wait(pe, S["ot_done"], t.n + 1)
                wait(pe, S["ex_done"], t.n)
                for s in range(HALVES):
                    for c in range(DC):
                        pe.matmul(ps_w[:, s * D:(s + 1) * D], o_t[t.p][:, c, s * P:(s + 1) * P], wo[:, c, :],
                                  start=c == 0, stop=False)
                    mm = pe.matmul(ps_w[:, s * D:(s + 1) * D], ones_row[:], bo[:], start=False, stop=True)
                mm.then_inc(S["w_ps"], 1)

            def turn_x3(t):
                wait(pe, S["xn3_done"], (t.n + 1) * HALVES)
                wait(pe, S["pf_done"], t.n)
                wait(pe, S["x_done"], t.n + 1)
                for s in range(HALVES):
                    for k in range(DC):
                        mm = pe.transpose(ps_w[:, k * SEQ + s * P:k * SEQ + (s + 1) * P], row[t.p][:, s, k * P:(k + 1) * P], ident)
                mm.then_inc(S["x3t_ps"], 1)

            def gates(t):
                wait(pe, S["x3t_sb"], t.n + 1)
                for s in range(HALVES):
                    for k in range(DC):
                        mm = pe.matmul(ps_w[:, s * E1:(s + 1) * E1], x3_t[t.p][:, k, s * P:(s + 1) * P], gate_w[:, k, :],
                                       start=k == 0, stop=k == DC - 1)
                mm.then_inc(S["lg_ps"], 1)

            def prefix(t):
                wait(pe, S["any_done"], t.n + 1)
                wait(pe, S["cnt_done"], t.n)
                wait(pe, S["ex_done"], t.n + 1)
                wait(pe, S["x_done"], min(t.n + 2, BATCH) if isinstance(t.n, int) else t.n + 2)
                for s in range(HALVES):
                    out = ps_w[:, s * E1:(s + 1) * E1]
                    pe.matmul(out, tri_bf[:], hot_any[t.p][:, s, :], start=True, stop=False)
                    if s:
                        pe.matmul(out, ones_bf[:], hot_any[t.p][:, 0, :], start=False, stop=False)
                    mm = pe.matmul(out, ones_bf[:], counts[t.p][:], start=False, stop=True)
                mm.then_inc(S["pf_ps"], 1)

            pipelined(pe, [[],
                           [(0, keys_values), (17, turn_x), (21, queries)],
                           placed(scores, (2, 4, 7, 8, 12, 13, 18, 19)) + placed(turn, (6, 10, 14, 16, 20, 23, 24)),
                           [(3, turn(NG - 1)), (5, attend), (11, inverse_sums), (15, project)],
                           [(1, turn_x3), (9, gates), (22, prefix)]], BATCH)

        @block.scalar
        def _(act):
            act.preload_act_table_set("natural_log_exp_and_others")
            act.wait_ge(S["par"], 10 * 16)
            act.wait_ge(S["prep"], 2)

            def root(t, m, lv, r, m_s, l_s, r_s, nw_s):
                wait(act, S[m_s], (t.n + 1) * HALVES)
                wait(act, S[nw_s], (t.n - 1) * 3)
                act.activation(lv[t.p][:], m[t.p][:, :, 1], ACT.Ln, bias=eps[:]).then_inc(S[l_s], 1)
                wait(act, S[l_s], t.n + 1)
                act.activation(r[t.p][:], lv[t.p][:], ACT.Exp, scale=-0.5).then_inc(S[r_s], 1)

            def keys(t):
                wait(act, S["kv_ps"], t.n + 1)
                wait(act, S["kl_done"], t.n)
                wait(act, S["kdh_done"], t.n * DC)
                for o in range(DC):
                    act.activation(kf[:, o, :], ps_kv[:, o * CTX:(o + 1) * CTX], ACT.Identity, bias=bk[:, o:o + 1]
                                   ).then_inc(S["kf_done"], 1)
                    act.activation(k_hi[:, o, :], ps_kv[:, o * CTX:(o + 1) * CTX], ACT.Identity, bias=bk[:, o:o + 1]
                                   ).then_inc(S["kh_done"], 1)

            def root1(t):
                root(t, mv, lnv, rstd, "mv_done", "ln_done", "rs_done", "nw_done")

            def turned(t):
                wait(act, S["xt_ps"], t.n + 1)
                wait(act, S["q_ps"], t.n - 1)
                act.activation(x_t[t.p][:], ps_q[:].rearrange("p (k i) -> p k i", k=DC), ACT.Copy).then_inc(S["xt_sb"], 1)

            def queries(t):
                wait(act, S["q_ps"], t.n + 1)
                wait(act, S["ql_done"], t.n)
                wait(act, S["s_ps"], (t.n - 1) * NG)
                for o in range(DC):
                    act.activation(q_hi[t.p][:, o, :], ps_q[:, o * SEQ:(o + 1) * SEQ], ACT.Identity, bias=bqs[:, o:o + 1],
                                   scale=SCALE).then_inc(S["qh_done"], 1)
                    act.activation(qf[t.p][:, o, :], ps_q[:, o * SEQ:(o + 1) * SEQ], ACT.Identity, bias=bqs[:, o:o + 1],
                                   scale=SCALE).then_inc(S["qf_done"], 1)

            def exps(n):
                def part(t):
                    wait(act, S["mx_done"], t.n * NG + n + 1)
                    wait(act, S["p_ps"], t.n * NG + n - 1)
                    s, g = n // GROUPS, n % GROUPS
                    if n == 0:
                        wait(act, S["rec_done"], t.n - 1)
                    for h in range(HPB):
                        act.activation(pr[n % 2][:, h, :], ps_s[n % 3][:, h * CTX:(h + 1) * CTX], ACT.Exp,
                                       bias=mx[n % 2][:, h:h + 1], accum_out=sums[t.p][:, s, g * HPB + h:g * HPB + h + 1]).then_inc(S["exp_done"], 1)
                return part

            def keep(n):
                def part(t):
                    s, g = n // GROUPS, n % GROUPS
                    wait(act, S["p_ps"], t.n * NG + n + 1)
                    if n == 0:
                        wait(act, S["o_ps"], t.n)
                    act.activation(pt[:, g * HPB:(g + 1) * HPB, s * P:(s + 1) * P],
                                   ps_p[0:CTX, :].rearrange("p (h i) -> p h i", h=HPB), ACT.Copy).then_inc(S["pt_done"], 1)
                return part

            def attended(t):
                wait(act, S["o_ps"], t.n + 1)
                wait(act, S["ot_done"], t.n)
                act.activation(o_sb[:], ps_o[:].rearrange("p (k i) -> p k i", k=DC), ACT.Copy).then_inc(S["o_sb"], 1)

            def root3(t):
                root(t, mv3, lnv3, rstd3, "mv3_done", "ln3_done", "rs3_done", "nw3_done")

            def turned_x3(t):
                wait(act, S["x3t_ps"], t.n + 1)
                wait(act, S["lg_ps"], t.n)
                act.activation(x3_t[t.p][:], ps_w[:].rearrange("p (k i) -> p k i", k=DC), ACT.Copy).then_inc(S["x3t_sb"], 1)

            def gates(t):
                wait(act, S["lg_ps"], t.n + 1)
                wait(act, S["e1_done"], t.n - 1)
                act.activation(ex[t.p][:].rearrange("p s e -> p (s e)"), ps_w[:, 0:HALVES * E1], ACT.Exp, scale=-1.0
                               ).then_inc(S["ex_done"], 1)

            pipelined(act, [[],
                            [(0, keys), (7, root1), (15, turned), (21, queries)],
                            placed(exps, (3, 4, 8, 11, 13, 16, 18, 22)) + placed(keep, (5, 10, 12, 14, 17, 20, 23)),
                            [(2, keep(NG - 1)), (6, attended), (19, root3)],
                            [(1, turned_x3), (9, gates)]], BATCH)

        @block.vector
        def _(ve):
            ve.memset(eps[:], LN_EPS).then_inc(S["zero"], 1)
            ve.memset(ones_row[:], 1.0).then_inc(S["zero"], 1)
            for i in range(2):
                ve.memset(vm[i][:], 0.0).then_inc(S["zero"], 1)
                ve.memset(counts[i][:], 0.0).then_inc(S["zero"], 1)
                ve.memset(row[i][:], 0.0).then_inc(S["zero"], 1)
            ve.tensor_copy(ident_bf[:], ident).then_inc(S["zero"], 1)
            ve.tensor_copy(causal_bf[:], consts[:, K_CAUSAL:K_CAUSAL + CTX].unsqueeze(1).to_broadcast([P, HPB, CTX])).then_inc(S["zero"], 1)
            ve.wait_ge(S["par"], 10 * 16)
            ve.wait_ge(S["zero"], 10)
            ve.wait_ge(S["tokn"], 1)
            ve.tensor_copy(gate_w[:], gate_w16[:]).then_inc(S["prep"], 1)
            ve.tensor_scalar(bqs[:], bq[:], SCALE, None, ALU.mult).then_inc(S["prep"], 1)

            def moments(t, src, st, st_s):
                apart(ve, gate)
                for s in range(HALVES):
                    ve.bn_stats(st[t.p][:, s, :], src[:, s, :]).then_inc(S[st_s], 1)

            def variance(t, st, m, st_s, m_s):
                wait(ve, S[st_s], (t.n + 1) * HALVES)
                apart(ve, gate)
                for s in range(HALVES):
                    ve.bn_aggr(m[t.p][:, s, :], st[t.p][:, s, :]).then_inc(S[m_s], 1)

            def newton_a(t, m, r, nw, r_s, nw_s):
                wait(ve, S[r_s], t.n + 1)
                ve.scalar_tensor_tensor(nw[t.p][:], m[t.p][:, :, 1], LN_EPS, r[t.p][:], ALU.add, ALU.mult).then_inc(S[nw_s], 1)

            def newton_b(t, r, nw, nw_s):
                wait(ve, S[nw_s], t.n * 3 + 1)
                ve.scalar_tensor_tensor(nw[t.p][:], nw[t.p][:], -0.5, r[t.p][:], ALU.mult, ALU.mult).then_inc(S[nw_s], 1)

            def newton_c(t, r, nw, nw_s):
                wait(ve, S[nw_s], t.n * 3 + 2)
                ve.scalar_tensor_tensor(nw[t.p][:], nw[t.p][:], 1.5, r[t.p][:], ALU.add, ALU.mult).then_inc(S[nw_s], 1)

            def normed(t, src, m, nw, dst, nw_s, dst_s):
                wait(ve, S[nw_s], t.n * 3 + 3)
                for s in range(HALVES):
                    ve.tensor_scalar(dst[t.p][:, s, 0:D], src[:, s, :], m[t.p][:, s, 0:1], nw[t.p][:, s:s + 1],
                                     ALU.subtract, ALU.mult).then_inc(S[dst_s], 1)

            def first_norm(t):
                moments(t, tiles(t), stats, "st_done")

            def first_norm_var(t):
                variance(t, stats, mv, "st_done", "mv_done")

            def first_norm_a(t):
                newton_a(t, mv, rstd, newton, "rs_done", "nw_done")

            def first_norm_b(t):
                newton_b(t, rstd, newton, "nw_done")

            def first_norm_c(t):
                newton_c(t, rstd, newton, "nw_done")

            def first_normed(t):
                wait(ve, S["xt_ps"], t.n - 1)
                normed(t, tiles(t), mv, newton, xn, "nw_done", "xn_done")

            def second_norm(t):
                wait(ve, S["x_done"], t.n + 1)
                moments(t, tiles(t), stats3, "st3_done")

            def second_norm_var(t):
                variance(t, stats3, mv3, "st3_done", "mv3_done")

            def second_norm_a(t):
                newton_a(t, mv3, rstd3, newton3, "rs3_done", "nw3_done")

            def second_norm_b(t):
                newton_b(t, rstd3, newton3, "nw3_done")

            def second_norm_c(t):
                newton_c(t, rstd3, newton3, "nw3_done")

            def second_normed(t):
                wait(ve, S["x3t_ps"], t.n - 1)
                wait(ve, stored[t.p], t.h * 16)
                wait(ve, sent[t.p], t.h * NR * 16)
                normed(t, tiles(t), mv3, newton3, row, "nw3_done", "xn3_done")

            def pick(t):
                wait(ve, yin[t.p], t.h * NC * 16)
                wait(ve, S["mixed"], (t.n - 1) * NC)
                own_tiles = bass.ds(t.n * HALVES, HALVES)
                ve.tensor_copy(slots[t.p][:].rearrange("p (s k) -> p s k", k=TOP0), slot_own[:, own_tiles, :]).then_inc(S["yi_done"], 1)
                ve.tensor_copy(wts[t.p][:].rearrange("p (s k) -> p s k", k=TOP0), w_own[:, own_tiles, :]).then_inc(S["yi_done"], 1)

            def mix(k):
                def part(t):
                    wait(ve, yin[t.p], (t.h + 1) * NC * 16)
                    wait(ve, S["yi_done"], (t.n + 1) * 2)
                    wait(ve, S["mixed"], t.n * NC + k * HALVES)
                    for s in range(HALVES):
                        c = s * TOP0 + k
                        xt = x_res[:, bass.ds(t.n * HALVES + s, 1), :].rearrange("p a d -> p (a d)")
                        ve.scalar_tensor_tensor(xt, yg[t.p][:, c, :], wts[t.p][:, c:c + 1], xt, ALU.mult, ALU.add
                                                ).then_inc(S["mixed"], 1)
                return part

            def mix_done(t):
                wait(ve, S["mixed"], (t.n + 1) * NC)
                first_norm(t)

            def values(t):
                wait(ve, S["kf_done"], (t.n + 1) * DC)
                wait(ve, S["kh_done"], (t.n + 1) * DC)
                wait(ve, S["o_ps"], t.n - 1)
                for odd in range(2):
                    ve.tensor_tensor(vm[t.p][:, odd::2, odd * HD:(odd + 1) * HD],
                                     ps_kv[0:CTX, D:2 * D].rearrange("p (h x) -> p h x", x=HD)[:, odd::2, :],
                                     bv[0:CTX, :].rearrange("p (h x) -> p h x", x=HD)[:, odd::2, :], ALU.add
                                     ).then_inc(S["v_done"], 1)

            def spread_k(c):
                def part(t):
                    wait(ve, S["kh_done"], (t.n + 1) * DC)
                    wait(ve, S["s_ps"], (t.n - 1) * NG)
                    ve.tensor_tensor(kd_hi[t.p][:, c], k_hi[:, c, :].unsqueeze(1).to_broadcast([P, HPC, CTX]),
                                     consts[:, K_HEAD:K_HEAD + HPC].unsqueeze(2).to_broadcast([P, HPC, CTX]),
                                     ALU.mult).then_inc(S["kdh_done"], 1)
                return part

            def peaks(n):
                def part(t):
                    wait(ve, S["s_ps"], t.n * NG + n + 1)
                    wait(ve, S["exp_done"], (t.n * NG + n - 1) * HPB)
                    ve.tensor_reduce(mx[n % 2][:], ps_s[n % 3][:, 0:HPB * CTX].rearrange("p (h j) -> p h j", h=HPB), AX.X, ALU.max,
                                     negate=True).then_inc(S["mx_done"], 1)
                return part

            def inverse(t):
                wait(ve, S["exp_done"], (t.n + 1) * NG * HPB)
                ve.reciprocal(rec[t.p][:], sums[t.p][:]).then_inc(S["rec_done"], 1)

            def inverse_spread(t):
                wait(ve, S["rec_done"], t.n + 1)
                wait(ve, S["r_ps"], t.n)
                ve.tensor_copy(recx[:], rec[t.p][:].unsqueeze(3).to_broadcast([P, HALVES, HEADS, HD])).then_inc(S["recx_done"], 1)

            def attended(t):
                wait(ve, S["o_sb"], t.n + 1)
                wait(ve, S["r_ps"], t.n + 1)
                wait(ve, S["w_ps"], t.n - 1)
                ve.tensor_tensor(o_t[t.p][:], ps_kv[:].rearrange("p (k i) -> p k i", k=DC), o_sb[:], ALU.mult
                                 ).then_inc(S["ot_done"], 1)

            def add(t):
                wait(ve, S["w_ps"], t.n + 1)
                ve.tensor_tensor(tiles(t), ps_w[:].rearrange("p (s d) -> p s d", s=HALVES), tiles(t), ALU.add
                                 ).then_inc(S["x_done"], 1)

            def gates(t):
                wait(ve, S["ex_done"], t.n + 1)
                ve.tensor_scalar(ex[t.p][:], ex[t.p][:], 1.0, None, ALU.add).then_inc(S["e1_done"], 1)

            def gate_score(t):
                wait(ve, S["e1_done"], t.n + 1)
                ve.reciprocal(sg[t.p][:], ex[t.p][:]).then_inc(S["sg_done"], 1)

            def biased(t):
                wait(ve, S["sg_done"], t.n + 1)
                ve.tensor_tensor(sel[t.p][:], sg[t.p][:], gate_b[:].unsqueeze(1).to_broadcast([P, HALVES, E1]), ALU.add
                                 ).then_inc(S["sel_done"], 1)

            def largest(t):
                wait(ve, S["sel_done"], t.n + 1)
                apart(ve, gate)
                for s in range(HALVES):
                    ve.max(top8[t.p][:, s, :], sel[t.p][:, s, :]).then_inc(S["t8_done"], 1)

            def places(t):
                wait(ve, S["t8_done"], (t.n + 1) * HALVES)
                apart(ve, gate)
                for s in range(HALVES):
                    ve.max_index(idx8[t.p][:, s, :], top8[t.p][:, s, :], sel[t.p][:, s, :]).then_inc(S["i8_done"], 1)

            def experts(t):
                wait(ve, S["i8_done"], (t.n + 1) * HALVES)
                ve.tensor_copy(idf[t.p][:], idx8[t.p][:, :, 0:TOP1]).then_inc(S["idf_done"], 1)

            def one_hot(t):
                wait(ve, S["idf_done"], t.n + 1)
                ve.tensor_tensor(hot[t.p][:], idf[t.p][:].rearrange("p s k -> p (s k)").unsqueeze(2).to_broadcast([P, NR, E1]),
                                 consts[:, K_IOTA:K_IOTA + E1].unsqueeze(1).to_broadcast([P, NR, E1]), ALU.is_equal
                                 ).then_inc(S["hot_done"], 1)

            def any_hot(t):
                wait(ve, S["hot_done"], t.n + 1)
                wait(ve, S["pf_ps"], t.n - 1)
                with nc.allow_low_precision(reason="sums of zeros and at most one 1"):
                    ve.tensor_reduce(hot_any[t.p][:], hot[t.p][:].rearrange("p (s k) e -> p s e k", k=TOP1), AX.X,
                                     ALU.add).then_inc(S["any_done"], 1)

            def own_scores(t):
                wait(ve, S["hot_done"], t.n + 1)
                wait(ve, S["pos_done"], t.n)
                for s in range(HALVES):
                    k = slice(s * TOP1, (s + 1) * TOP1)
                    ve.tensor_tensor(own[t.p][:, k, :], hot[t.p][:, k, :],
                                     sg[t.p][:, s:s + 1, :].to_broadcast([P, TOP1, E1]), ALU.mult).then_inc(S["own_done"], 1)

            def chosen(t):
                wait(ve, S["own_done"], (t.n + 1) * HALVES)
                ve.tensor_reduce(wk8[t.p][:], own[t.p][:], AX.X, ALU.add).then_inc(S["wk_done"], 1)

            def chosen_sum(t):
                wait(ve, S["wk_done"], t.n + 1)
                ve.tensor_reduce(wsum[t.p][:], wk8[t.p][:].rearrange("p (s k) -> p s k", k=TOP1), AX.X, ALU.add
                                 ).then_inc(S["ws_done"], 1)

            def sum_guard(t):
                wait(ve, S["ws_done"], t.n * 2 + 1)
                ve.tensor_scalar(wsum[t.p][:], wsum[t.p][:], 1e-12, None, ALU.max).then_inc(S["ws_done"], 1)

            def sum_inverse(t):
                wait(ve, S["ws_done"], t.n * 2 + 2)
                ve.reciprocal(wrec[t.p][:], wsum[t.p][:]).then_inc(S["wr_done"], 1)

            def row_tail(t):
                wait(ve, S["wr_done"], t.n + 1)
                ve.tensor_tensor(row[t.p][:, :, C_W:C_W + TOP1], wk8[t.p][:].rearrange("p (s k) -> p s k", k=TOP1),
                                 wrec[t.p][:].unsqueeze(2).to_broadcast([P, HALVES, TOP1]), ALU.mult).then_inc(S["rowx_done"], 1)
                ve.tensor_copy(row[t.p][:, :, C_E:C_E + TOP1], idf[t.p][:]).then_inc(S["rowx_done"], 1)
                ve.tensor_copy(row[t.p][:, :, C_TOK:C_TOK + 1], tok_no[:, bass.ds(t.n * HALVES, HALVES)].unsqueeze(2)
                               ).then_inc(S["rowx_done"], 1)

            def prefix(t):
                wait(ve, S["pf_ps"], t.n + 1)
                wait(ve, S["pos_done"], t.n)
                ve.tensor_copy(pfx[t.p][:], ps_w[:, 0:HALVES * E1].rearrange("p (s e) -> p s e", s=HALVES)).then_inc(S["pf_done"], 1)

            def count_a(t):
                wait(ve, S["any_done"], t.n + 1)
                wait(ve, S["cnt_done"], t.n)
                ve.tensor_tensor(csum[:], counts[t.p][:], hot_any[t.p][:, 0, :], ALU.add).then_inc(S["cs_done"], 1)

            def count_b(t):
                wait(ve, S["cs_done"], t.n + 1)
                ve.tensor_tensor(counts[1 - t.p][:], csum[:], hot_any[t.p][:, 1, :], ALU.add).then_inc(S["cnt_done"], 1)

            def own_prefix(t):
                wait(ve, S["pf_done"], t.n + 1)
                wait(ve, S["wk_done"], t.n + 1)
                for s in range(HALVES):
                    k = slice(s * TOP1, (s + 1) * TOP1)
                    ve.tensor_tensor(own[t.p][:, k, :], hot[t.p][:, k, :],
                                     pfx[t.p][:, s:s + 1, :].to_broadcast([P, TOP1, E1]), ALU.mult).then_inc(S["own2_done"], 1)

            def position(t):
                wait(ve, S["own2_done"], (t.n + 1) * HALVES)
                ve.tensor_reduce(pos[t.p][:], own[t.p][:], AX.X, ALU.add).then_inc(S["pos_done"], 1)

            def past_end(t):
                wait(ve, S["pos_done"], t.n + 1)
                ve.tensor_scalar(over[t.p][:], pos[t.p][:], float(CAP1), float(DROPPED), ALU.is_ge, ALU.mult).then_inc(S["ov_done"], 1)

            def past_end_far(t):
                wait(ve, S["ov_done"], t.n * 2 + 1)
                ve.tensor_tensor(over[t.p][:], over[t.p][:], pos[t.p][:], ALU.add).then_inc(S["ov_done"], 1)

            def slot(t):
                wait(ve, S["ov_done"], t.n * 2 + 2)
                wait(ve, sent[t.p], t.h * NR * 16)
                ve.scalar_tensor_tensor(dest[t.p][:], idf[t.p][:].rearrange("p s k -> p (s k)"), float(CAP1), over[t.p][:],
                                        ALU.mult, ALU.add).then_inc(S["dest_done"], 1)

            pipelined(ve, [[(23, pick)],
                           [(2, mix(0)), (7, mix(1)), (10, mix_done), (12, first_norm_var), (15, values), (18, first_norm_a),
                            (22, first_norm_b), (25, first_norm_c), (27, first_normed), (36, spread_k(0)), (50, spread_k(1))],
                           placed(peaks, (3, 5, 14, 16, 20, 29, 35, 39)),
                           [(4, inverse), (13, inverse_spread), (17, attended), (31, add), (33, second_norm),
                            (37, second_norm_var), (41, second_norm_a), (44, second_norm_b), (46, second_norm_c),
                            (49, second_normed)],
                           [(19, gates), (21, gate_score), (24, biased), (26, largest), (28, places), (30, experts),
                            (32, one_hot), (34, any_hot), (38, own_scores), (40, chosen), (42, count_a), (43, prefix),
                            (45, chosen_sum), (47, count_b), (48, sum_guard), (51, sum_inverse)],
                           [(0, own_prefix), (1, position), (6, past_end), (8, row_tail), (9, past_end_far), (11, slot)]], BATCH)


def phase_moe(nc, env):
    a, x_res, consts, gate, rows_d, xn3_d, sums_d, out = (env[k] for k in (
        "a", "x_res", "consts", "gate", "rows_d", "xn3_d", "sums_d", "out"))
    W_UP = 2 * DC * INNER
    ctx = ExitStack()
    with ctx:
        def sb(name, shape, dt):
            return ctx.enter_context(nc.sbuf_tensor("m_" + name, shape, dt))

        def two(name, shape, dt):
            return [sb(f"{name}{i}", shape, dt) for i in range(2)]

        def sem(name):
            env["sems"].append(nc.alloc_semaphore(name="m_" + name))
            return env["sems"][-1]

        ident = consts[:, K_ID:K_ID + P]
        sw16 = sb("sw16", [P, W_UP + D], BF16)
        sw = sb("sw", [P, W_UP + D], F32R)
        w16 = two("w16", [P, W_UP + D], BF16)
        w = two("w", [P, W_UP + D], F32R)
        xr = two("xr", [P, HALVES, ROW], F32)
        xn3 = sb("xn3", [P, TILES, D], F32)
        x_hi, x_lo = two("x_hi", [P, DC, SEQ], F32R), two("x_lo", [P, DC, SEQ], F32R)
        s1, hid = two("s1", [P, SEQ], F32), two("hid", [P, SEQ], F32)
        h_hi, h_lo = two("h_hi", [P, SEQ], F32R), two("h_lo", [P, SEQ], F32R)
        yo = two("yo", [P, HALVES, D], F32)
        wsel, wrow = two("wsel", [P, HALVES, TOP1], F32), two("wrow", [P, HALVES], F32)
        row_tok, tok = two("row_tok", [P, HALVES], F32), two("tok", [P, HALVES], U32)
        part0, part1 = two("part0", [P, HALVES, D], F32), two("part1", [P, HALVES, D], F32)
        routed, ysum = two("routed", [P, HALVES, D], F32), two("ysum", [P, HALVES, D], F32)

        def banks(name):
            return [ctx.enter_context(nc.psum_tensor(f"m_{name}{i}", [P, 512], F32)) for i in range(2)]

        ps_t, ps_1, ps_3, ps_y = banks("ps_t"), banks("ps_1"), banks("ps_3"), banks("ps_y")
        names = ("sw_ld sw_done xn3_ld tokens parts0 parts1 routed ysum w_ld0 w_ld1 w_done wd_done row_tok x_ld0 x_ld1 tok_done wsel_done wrow_done t_ps xh_done "
                 "xl_done up_ps s1_done hid_done hh_done hl_done y_ps yo_done st0 st1 added0 added1").split()
        S = {n: sem(n) for n in names}
        w_ld, x_ld, st, added, parts = ([S[f"{n}{i}"] for i in range(2)] for n in ("w_ld", "x_ld", "st", "added", "parts"))
        ADDS = E1 // 2 * SLOT_TILES1 * 16

        def loops(eng, experts, shared):
            pipelined(eng, experts, E1)
            pipelined(eng, shared, BATCH, E1)

        block = ctx.enter_context(nc.Block())

        @block.sync
        def _(sp):
            sp.dma_start(sw16[:], a["sw"]).then_inc(S["sw_ld"], 16)

            def load_slots(t):
                wait_apart(sp, x_ld[t.p], t.h * 16, gate)
                wait_apart(sp, S["t_ps"], t.n - 1, gate)
                wait_apart(sp, S["wsel_done"], t.n - 1, gate)
                wait_apart(sp, S["row_tok"], t.n - 1, gate)
                sp.dma_start(xr[t.p][:], rows_d.rearrange("(t p) d -> p t d", p=P)[:, bass.ds(t.n * SLOT_TILES1, SLOT_TILES1), :]
                             ).then_inc(x_ld[t.p], 16)
                wait_apart(sp, w_ld[t.p], t.h * 16, gate)
                wait_apart(sp, S["w_done"], t.n - 1, gate)
                wait_apart(sp, S["wd_done"], t.n - 1, gate)
                sp.dma_start(w16[t.p][:], a["moe_w"][bass.ds(t.n, 1)].rearrange("e p n -> (e p) n")).then_inc(w_ld[t.p], 16)

            def batch_rows(t):
                return bass.ds((t.n - E1) * HALVES, HALVES)

            def load_parts(t):
                if isinstance(t.n, int) and t.n == E1:
                    for q in range(2):
                        sp.wait_ge(added[q], ADDS)
                wait_apart(sp, S["routed"], t.n - E1 - 1, gate)
                wait_apart(sp, parts[t.p], (t.h - E1 // 2) * 32, gate)
                for part, sums in zip((part0, part1), sums_d):
                    sp.dma_start(part[t.p][:], sums[0:TOKENS, :].rearrange("(t p) d -> p t d", p=P)[:, batch_rows(t), :]
                                 ).then_inc(parts[t.p], 16)

            def store(t):
                wait_apart(sp, S["yo_done"], (t.n + 1) * HALVES, gate)
                wait_apart(sp, st[t.p], (t.h - E1 // 2) * 16, gate)
                sp.dma_start(out.rearrange("(t p) d -> p t d", p=P)[:, batch_rows(t), :], yo[t.p][:]
                             ).then_inc(st[t.p], 16)

            QUARTER = TILES // 4

            def load_and_tokens(t):
                load_slots(t)
                if isinstance(t.n, int) and t.n == 1:
                    for q in range(4):
                        sp.dma_start(xn3[:, q * QUARTER:(q + 1) * QUARTER, :],
                                     xn3_d.rearrange("(t p) d -> p t d", p=P)[:, q * QUARTER:(q + 1) * QUARTER, :]
                                     ).then_inc(S["xn3_ld"], 16)

            loops(sp, [[(0, load_and_tokens)]], [[(0, load_parts)], [], [], [(1, store)]])
            for q in range(2):
                sp.wait_ge(st[q], BATCH // 2 * 16)

        @block.gpsimd
        def _(pool):
            def add(t):
                wait(pool, added[t.p], t.h * SLOT_TILES1 * 16)
                wait(pool, S["tok_done"], t.n + 1)
                wait(pool, S["yo_done"], (t.n + 1) * HALVES)
                apart(pool, gate)
                for c in range(SLOT_TILES1):
                    pool.indirect_dma_start(sums_d[t.p], bass.IndirectOffsetOnAxis(ap=tok[t.p][:, c:c + 1], axis=0), yo[t.p][:, c, :],
                                            None, compute_op=ALU.add).then_inc(added[t.p], 16)

            def routed_sum(t):
                wait(pool, parts[t.p], (t.h - E1 // 2 + 1) * 32)
                wait(pool, S["yo_done"], (t.n - 1) * HALVES)
                pool.tensor_tensor(routed[t.p][:], part0[t.p][:], part1[t.p][:], ALU.add).then_inc(S["routed"], 1)

            def tokens(t):
                if isinstance(t.n, int) and t.n == E1:
                    pool.wait_ge(S["xn3_ld"], 4 * 16)
                wait(pool, S["t_ps"], t.n - 1)
                wait(pool, S["wsel_done"], E1)
                wait(pool, S["row_tok"], E1)
                pool.tensor_copy(xr[t.p][:, :, 0:D], xn3[:, bass.ds((t.n - E1) * HALVES, HALVES), :]).then_inc(S["tokens"], 1)

            loops(pool, [[], [], [(0, add)]], [[(-1, tokens)], [], [(0, routed_sum)]])

        @block.tensor
        def _(pe):
            def turn_slots(t):
                wait(pe, x_ld[t.p], (t.h + 1) * 16)
                turn(t)

            def turn_tokens(t):
                wait(pe, S["tokens"], t.n - E1 + 1)
                turn(t)

            def turn(t):
                wait(pe, S["xl_done"], t.n - 1)
                for s in range(HALVES):
                    for k in range(DC):
                        mm = pe.transpose(ps_t[t.p][:, k * SEQ + s * P:k * SEQ + (s + 1) * P], xr[t.p][:, s, k * P:(k + 1) * P], ident)
                mm.then_inc(S["t_ps"], 1)

            def up(t, wts):
                wait(pe, S["xl_done"], t.n + 1)
                wait(pe, S["hid_done"], t.n - 1)
                for n, ps in enumerate((ps_1, ps_3)):
                    i = 0
                    for k in range(DC):
                        for x in (x_hi, x_lo):
                            c = (n * DC + k) * INNER
                            mm = pe.matmul(ps[t.p][:, 0:SEQ], wts[:, c:c + INNER], x[t.p][:, k, :], start=i == 0, stop=i == 2 * DC - 1)
                            i += 1
                mm.then_inc(S["up_ps"], 1)

            def down(t, wts):
                wait(pe, S["hl_done"], t.n + 1)
                wait(pe, S["yo_done"], (t.n - 1) * HALVES)
                for s in range(HALVES):
                    for i, h in enumerate((h_hi, h_lo)):
                        mm = pe.matmul(ps_y[t.p][:, s * D:(s + 1) * D], h[t.p][:, s * P:(s + 1) * P], wts[:, W_UP:W_UP + D],
                                       start=i == 0, stop=i == 1)
                mm.then_inc(S["y_ps"], 1)

            def up_shared(t):
                up(t, sw)

            def down_shared(t):
                down(t, sw)

            def up_expert(t):
                wait(pe, S["w_done"], t.n + 1)
                up(t, w[t.p])

            def down_expert(t):
                wait(pe, S["wd_done"], t.n + 1)
                down(t, w[t.p])

            pe.wait_ge(S["sw_done"], 1)
            loops(pe, [[(0, turn_slots)], [(1, up_expert)], [(2, down_expert)]], [[(0, turn_tokens)], [(1, up_shared)], [(2, down_shared)]])

        @block.scalar
        def _(act):
            def turn(t):
                wait(act, S["t_ps"], t.n + 1)
                wait(act, S["up_ps"], t.n - 1)
                act.activation(x_hi[t.p][:], ps_t[t.p][:].rearrange("p (k i) -> p k i", k=DC), ACT.Copy).then_inc(S["xh_done"], 1)

            def up(t):
                wait(act, S["up_ps"], t.n + 1)
                wait(act, S["hid_done"], t.n - 1)
                act.activation(s1[t.p][:], ps_1[t.p][:, 0:SEQ], ACT.Silu).then_inc(S["s1_done"], 1)

            def split_hidden(t):
                wait(act, S["hid_done"], t.n + 1)
                wait(act, S["y_ps"], t.n - 1)
                act.activation(h_hi[t.p][:], hid[t.p][:], ACT.Copy).then_inc(S["hh_done"], 1)

            def down_expert(t):
                wait(act, S["y_ps"], t.n + 1)
                wait(act, S["wrow_done"], t.n + 1)
                wait(act, added[t.p], t.h * SLOT_TILES1 * 16)
                for s in range(HALVES):
                    act.activation(yo[t.p][:, s, :], ps_y[t.p][:, s * D:(s + 1) * D], ACT.Copy, scale=wrow[t.p][:, s:s + 1]
                                   ).then_inc(S["yo_done"], 1)

            loops(act, [[(0, turn)], [(1, up), (1.5, split_hidden)], [(2, down_expert)]],
                  [[(0, turn)], [(1, up), (1.5, split_hidden)]])

        @block.vector
        def _(ve):
            ve.wait_ge(S["sw_ld"], 16)
            ve.tensor_copy(sw[:], sw16[:]).then_inc(S["sw_done"], 1)

            def turn(t):
                wait(ve, S["xh_done"], t.n + 1)
                wait(ve, S["up_ps"], t.n - 1)
                ve.tensor_tensor(x_lo[t.p][:], ps_t[t.p][:].rearrange("p (k i) -> p k i", k=DC), x_hi[t.p][:], ALU.subtract
                                 ).then_inc(S["xl_done"], 1)

            def weights_up(t):
                wait(ve, w_ld[t.p], (t.h + 1) * 16)
                wait(ve, S["up_ps"], t.n - 1)
                ve.tensor_copy(w[t.p][:, 0:W_UP], w16[t.p][:, 0:W_UP]).then_inc(S["w_done"], 1)

            def weights_down(t):
                wait(ve, S["y_ps"], t.n - 1)
                ve.tensor_copy(w[t.p][:, W_UP:W_UP + D], w16[t.p][:, W_UP:W_UP + D]).then_inc(S["wd_done"], 1)

            def row_ends(t):
                wait(ve, x_ld[t.p], (t.h + 1) * 16)
                wait(ve, S["wrow_done"], t.n - 1)
                wait(ve, S["tok_done"], t.n - 1)
                ve.scalar_tensor_tensor(wsel[t.p][:], xr[t.p][:, :, C_E:C_E + TOP1], consts[:, bass.ds(t.n + K_IOTA, 1)],
                                        xr[t.p][:, :, C_W:C_W + TOP1], ALU.is_equal, ALU.mult).then_inc(S["wsel_done"], 1)
                ve.tensor_copy(row_tok[t.p][:], xr[t.p][:, :, C_TOK]).then_inc(S["row_tok"], 1)

            def row_weight(t):
                wait(ve, S["wsel_done"], t.n + 1)
                wait(ve, S["yo_done"], (t.n - 1) * HALVES)
                ve.tensor_reduce(wrow[t.p][:], wsel[t.p][:], AX.X, ALU.add).then_inc(S["wrow_done"], 1)
                wait(ve, S["row_tok"], t.n + 1)
                wait(ve, added[t.p], t.h * SLOT_TILES1 * 16)
                ve.tensor_copy(tok[t.p][:], row_tok[t.p][:]).then_inc(S["tok_done"], 1)

            def up(t):
                wait(ve, S["s1_done"], t.n + 1)
                wait(ve, S["hh_done"], t.n - 1)
                wait(ve, S["hl_done"], t.n - 1)
                ve.tensor_tensor(hid[t.p][:], s1[t.p][:], ps_3[t.p][:, 0:SEQ], ALU.mult).then_inc(S["hid_done"], 1)

            def split_hidden(t):
                wait(ve, S["hh_done"], t.n + 1)
                wait(ve, S["y_ps"], t.n - 1)
                ve.tensor_tensor(h_lo[t.p][:], hid[t.p][:], h_hi[t.p][:], ALU.subtract).then_inc(S["hl_done"], 1)

            def down_shared(t):
                wait(ve, S["y_ps"], t.n + 1)
                ve.tensor_tensor(ysum[t.p][:], ps_y[t.p][:].rearrange("p (s d) -> p s d", s=HALVES),
                                 x_res[:, bass.ds((t.n - E1) * HALVES, HALVES), :], ALU.add).then_inc(S["ysum"], 1)
                wait(ve, S["ysum"], t.n - E1 + 1)
                wait(ve, S["routed"], t.n - E1 + 1)
                if isinstance(t.n, int) and t.n == E1:
                    for q in range(2):
                        ve.wait_ge(added[q], ADDS)
                wait(ve, st[t.p], (t.h - E1 // 2) * 16)
                for s in range(HALVES):
                    ve.tensor_tensor(yo[t.p][:, s, :], ysum[t.p][:, s, :], routed[t.p][:, s, :], ALU.add
                                     ).then_inc(S["yo_done"], 1)

            loops(ve, [[(0.7, turn), (1.3, row_ends), (1.7, weights_up)],
                       [(0, weights_down), (1.2, up), (1.6, split_hidden), (1.8, row_weight)]],
                  [[(0, turn)], [(1, up), (1.5, split_hidden)], [(2, down_shared)]])


def kernel(**inputs):
    import numpy as np
    import concourse.bacc as bacc
    from concourse.bass_utils import run_bass_kernel_spmd

    nc = bacc.Bacc("TRN2", target_bir_lowering=False, num_devices=1)
    arrays, aps = lay_out(np, inputs), {}
    for name, array in arrays.items():
        aps[name] = nc.dram_tensor(f"in_{name}", array.shape, mybir.dt.from_np(array.dtype), kind="ExternalInput").ap()
    out = nc.dram_tensor("out", (TOKENS, D), F32, kind="ExternalOutput").ap()
    build(nc, aps, out)
    r = run_bass_kernel_spmd(nc, [{f"in_{k}": v for k, v in arrays.items()}], core_ids=[0])
    return r.results[0]["out"].reshape(BATCH, SEQ, D)


def lay_out(np, inputs):
    g = {k: np.asarray(v) for k, v in inputs.items()}

    def chunks(w):
        return np.ascontiguousarray(w.reshape(-1, P, w.shape[-1]).transpose(1, 0, 2))

    def unit(w):
        return w.reshape(-1, DC, P, INNER).transpose(0, 2, 1, 3).reshape(-1, P, DC * INNER)

    c = np.zeros((P, K_END), np.float32)
    p = np.arange(P)
    c[:, K_ID:K_ID + P] = np.eye(P)
    c[:, K_SU:K_SU + P] = p[:, None] < p[None, :]
    c[:, K_IOTA:K_IOTA + P] = p[None, :]
    c[:, K_P] = p
    c[:, K_HEAD:K_HEAD + HPC] = p[:, None] // HD == np.arange(HPC)[None, :]
    c[:, K_CAUSAL:K_CAUSAL + CTX] = np.where(np.arange(CTX)[None, :] > p[:, None], MASKED, 0.0)
    ctx = g["ctx_1024"]
    return {
        "consts": c,
        "x": np.ascontiguousarray(g["x"].reshape(TILES, P, D).transpose(1, 0, 2)),
        "ctx": ctx,
        "ctx_t": np.ascontiguousarray(ctx.transpose(0, 2, 1).reshape(BATCH, DC, P, CTX).transpose(0, 2, 1, 3)),
        "wsim": np.ascontiguousarray(g["L0_xattn_w_sim"].reshape(3, DC, P).transpose(2, 0, 1)),
        "b_sim": g["L0_xattn_b_sim"],
        "wqv": chunks(g["L0_xattn_W_qv"]),
        "bqv2": np.stack([g["L0_xattn_b_qv"]] * HALVES),
        "router_w": chunks(g["L0_ffn_router_w"].T),
        "router_b": g["L0_ffn_router_b"],
        "fc1_t": np.ascontiguousarray(g["L0_ffn_fc1_w"].transpose(0, 2, 1).reshape(E0, DC, P, HID0).transpose(0, 2, 1, 3)),
        "fc1_b": np.ascontiguousarray(g["L0_ffn_fc1_b"].reshape(E0, HC0, P).transpose(0, 2, 1)),
        "fc2_t": np.ascontiguousarray(g["L0_ffn_fc2_w"].transpose(0, 2, 1).reshape(E0, HC0, P, D).transpose(0, 2, 1, 3)),
        "fc2_b": g["L0_ffn_fc2_b"],
        "ls": g["L0_ffn_layer_scale"],
        "wq_t": chunks(g["L1_xattn_Wq"].T),
        "wk_t": chunks(g["L1_xattn_Wk"].T),
        "wv_t": chunks(g["L1_xattn_Wv"].T),
        "wo_t": chunks(g["L1_xattn_Wo"].T),
        "bq": np.ascontiguousarray(g["L1_xattn_bq"].reshape(DC, P).T),
        "bk": np.ascontiguousarray(g["L1_xattn_bk"].reshape(DC, P).T),
        "bv": g["L1_xattn_bv"],
        "bo": g["L1_xattn_bo"].reshape(1, D),
        "gate_w": chunks(g["L1_ffn_gate_w"].T),
        "gate_b": g["L1_ffn_bias"],
        "moe_w": np.concatenate([unit(g["L1_ffn_W1"]), unit(g["L1_ffn_W3"]), g["L1_ffn_W2"]], axis=2),
        "sw": np.concatenate([unit(g["L1_ffn_sw1"].T[None]), unit(g["L1_ffn_sw3"].T[None]), g["L1_ffn_sw2"].T[None]], axis=2)[0],
    }
```

```python
import concourse.bass as bass
from concourse import mybir
from contextlib import ExitStack

F32, F32R, BF16 = mybir.dt.float32, mybir.dt.float32r, mybir.dt.bfloat16
I32, U32 = mybir.dt.int32, mybir.dt.uint32
ALU, ACT, AX = mybir.AluOpType, mybir.ActivationFunctionType, mybir.AxisListType

P = 128
BATCH, SEQ, D = 16, 256, 256
CTX = 120
DC = D // P
HALVES = SEQ // P
TILES = BATCH * HALVES
TOKENS = BATCH * SEQ
LN_EPS = 1e-5
E0, HID0, TOP0, W_EPS = 8, 1024, 2, 1e-9
CAP0 = int(1.2 * (TOKENS // E0 + 1))
SLOT_TILES0 = -(-CAP0 // P)
SLOTS0 = SLOT_TILES0 * P
HALF0 = -(-CAP0 // 2)
USED0 = 2 * HALF0
HC0 = HID0 // P
HI0 = E0 * SLOT_TILES0
HEADS, HD = 16, 16
HPC = P // HD
HPB = 4
GROUPS = HEADS // HPB
SCALE = HD ** -0.5
MASKED = -1e30
E1, INNER, TOP1 = 32, 128, 4
CAP1 = 2 * 1024 * TOP1 // E1
SLOTS1 = E1 * CAP1
SLOT_TILES1 = CAP1 // P
DROPPED = 1 << 20
ROW = D + 16
C_TOK, C_W, C_E = D, D + 1, D + 1 + TOP1
K_ID, K_SU, K_IOTA, K_P, K_HEAD, K_CAUSAL, K_END = 0, 128, 256, 384, 385, 400, 520


class At:

    def __init__(self, n, half, par):
        self.n, self.h, self.p = n, half, par


def wait(eng, sem, count):
    if not isinstance(count, int) or count > 0:
        eng.wait_ge(sem, count)


def pipelined(eng, stages, n, base=0):
    parts = [(place, -k, i, part) for k, stage in enumerate(stages) for i, (place, part) in enumerate(stage)]
    parts.sort(key=lambda x: x[:3])
    lag = len(stages) - 1
    first = (lag + 3) // 2 * 2
    pairs = (n - first) // 2

    def peeled(s):
        for _, k, _, part in parts:
            if 0 <= s + k < n:
                part(At(base + s + k, (base + s + k) // 2, (s + k) % 2))

    for s in range(first):
        peeled(s)
    if pairs:
        with eng.Fori(0, pairs) as i:
            for u in range(2):
                for _, k, _, part in parts:
                    part(At(i * 2 + (base + first + u + k), i + (base + first + u + k) // 2, (u + k) % 2))
    for s in range(first + 2 * pairs, n + lag):
        peeled(s)


def placed(part, places):
    return [(place, part(n)) for n, place in enumerate(places)]


def build(nc, a, out):
    ctx = ExitStack()
    with ctx:
        def sb(name, shape, dt):
            return ctx.enter_context(nc.sbuf_tensor(name, shape, dt))

        x_res = sb("x_res", [P, TILES, D], F32)
        consts = sb("consts", [P, K_END], F32)
        tri_bf = sb("tri_bf", [P, P], BF16)
        ones_bf = sb("ones_bf", [P, P], BF16)
        logits = sb("logits", [P, TILES, E0], F32)
        top2 = sb("top2", [P, TILES, TOP0], F32)
        exp2 = sb("exp2", [P, TILES, TOP0], F32)
        w_own = sb("w_own", [P, TILES, TOP0], F32)
        slot_own = sb("slot_own", [P, TILES, TOP0], U32)
        gate = ctx.enter_context(nc.semaphore("gate"))

        xn1_d = nc.dram_tensor("xn1_d", (TOKENS, D), F32).ap()
        y0_d = nc.dram_tensor("y0_d", (E0 * SLOTS0, D), F32).ap()
        rows_d = nc.dram_tensor("rows_d", (SLOTS1, ROW), F32).ap()
        xn3_d = nc.dram_tensor("xn3_d", (TOKENS, D), F32).ap()
        sums_d = [nc.dram_tensor(f"sums{i}_d", (TOKENS + CAP1, D), F32).ap() for i in range(2)]
        env = dict(locals())
        env["sems"] = []
        for phase in (phase_attend, phase_experts, phase_heads, phase_moe):
            phase(nc, env)
            nc.clear_and_free_semaphores(env["sems"])
            nc.all_engine_barrier()
            env["sems"] = []


def wait_apart(eng, sem, count, gate):
    if not isinstance(count, int) or count > 0:
        eng.wait_ge(sem, count)
        if not isinstance(count, int):
            apart(eng, gate)


def apart(eng, gate):
    eng.sem_inc(gate, 1)


def phase_attend(nc, env):
    a, x_res, consts, tri_bf, ones_bf = (env[k] for k in ("a", "x_res", "consts", "tri_bf", "ones_bf"))
    logits, top2, exp2, gate, xn1_d, rows_d, sums_d = (env[k] for k in (
        "logits", "top2", "exp2", "gate", "xn1_d", "rows_d", "sums_d"))
    ctx = ExitStack()
    with ctx:
        def sb(name, shape, dt):
            return ctx.enter_context(nc.sbuf_tensor("a_" + name, shape, dt))

        def two(name, shape, dt):
            return [sb(f"{name}{i}", shape, dt) for i in range(2)]

        def sem(name):
            env["sems"].append(nc.alloc_semaphore(name="a_" + name))
            return env["sems"][-1]

        def bank(name, shape, dt=F32):
            return ctx.enter_context(nc.psum_tensor("a_" + name, shape, dt))

        ident = consts[:, K_ID:K_ID + P]
        wqv = sb("wqv", [P, 4 * DC, D], F32)
        wqv_hi = sb("wqv_hi", [P, 2 * DC, D], F32R)
        wqv_lo = sb("wqv_lo", [P, 2 * DC, D], F32R)
        bqv = sb("bqv", [P, HALVES, D], F32)
        wsim = sb("wsim", [P, 3, DC], F32)
        bsim = sb("bsim", [P, 1], F32)
        w2rep = sb("w2rep", [P, DC, P], F32)
        ones_row = sb("ones_row", [1, P], F32)
        router_w = sb("router_w", [P, DC, E0], F32)
        router_b = sb("router_b", [P, E0], F32)
        empty_rows = sb("empty_rows", [P, SLOT_TILES1, ROW], F32)
        zeros = sb("zeros", [P, D], F32)
        cn = two("cn", [CTX, D], F32)
        ct = two("ct", [P, DC, CTX], F32)
        stats = two("stats", [P, HALVES, 6], F32)
        mv = two("mv", [P, HALVES, 2], F32)
        rstd = two("rstd", [P, HALVES], F32)
        newton = two("newton", [P, HALVES], F32)
        lnv = two("lnv", [P, HALVES], F32)
        xn = two("xn", [P, HALVES, D], F32)
        enc_t = two("enc_t", [P, DC, SEQ], F32)
        enc_hi = two("enc_hi", [P, DC, SEQ], F32R)
        enc_lo = two("enc_lo", [P, DC, SEQ], F32R)
        simw = two("simw", [P, DC, CTX], F32)
        rowb = two("rowb", [P, CTX], F32)
        sim = two("sim", [P, HALVES, CTX], F32)
        mx = two("mx", [P, HALVES], F32)
        nmx = two("nmx", [P, HALVES], F32)
        probs = two("probs", [P, HALVES, CTX], F32)
        psums = two("psums", [P, HALVES], F32)
        prec = two("prec", [P, HALVES], F32)
        probs_n = two("probs_n", [P, HALVES, CTX], F32)
        gm = two("gm", [1, 1], F32)
        ngm = two("ngm", [1, 1], F32)
        brow = two("brow", [1, SEQ], F32)
        bsum = two("bsum", [1, 1], F32)
        brec = two("brec", [1, 1], F32)
        brow_n = two("brow_n", [1, SEQ], F32)
        bjunk = two("bjunk", [P, DC, SEQ], F32)
        hc = two("hc", [P, DC], F32)
        wc = two("wc", [P, DC, D], F32)
        wc_hi = two("wc_hi", [P, DC, D], F32R)
        wc_lo = two("wc_lo", [P, DC, D], F32R)
        at_sb = two("at_sb", [CTX, SEQ], F32)
        hq_hi = two("hq_hi", [P, DC, SEQ], F32R)
        hq_lo = two("hq_lo", [P, DC, SEQ], F32R)
        prod = two("prod", [P, DC, SEQ], F32)
        prod_hi = two("prod_hi", [P, DC, SEQ], F32R)
        prod_lo = two("prod_lo", [P, DC, SEQ], F32R)
        x_in, x1 = two("x_in", [P, HALVES, D], F32), two("x1", [P, HALVES, D], F32)
        xb = two("xb", [P, HALVES, D], F32)
        stats1 = two("stats1", [P, HALVES, 6], F32)
        mv1 = two("mv1", [P, HALVES, 2], F32)
        rstd1 = two("rstd1", [P, HALVES], F32)
        newton1 = two("newton1", [P, HALVES], F32)
        lnv1 = two("lnv1", [P, HALVES], F32)
        eps = sb("eps", [P, 1], F32)
        xn1 = two("xn1", [P, HALVES, D], F32)
        x1_t = two("x1_t", [P, DC, SEQ], F32)
        lg = two("lg", [P, HALVES, E0], F32)
        mx8 = two("mx8", [P, HALVES, 8], F32)
        ix8 = two("ix8", [P, HALVES, 8], U32)

        ps_enc = bank("ps_enc", [P, DC, SEQ])
        ps_sim = bank("ps_sim", [P, 4, P])
        ps_row = bank("ps_row", [P, 512])
        ps_bc = bank("ps_bc", [P, 512])
        ps_at = bank("ps_at", [P, 512])
        ps_hq = bank("ps_hq", [P, DC, SEQ])
        ps_out = bank("ps_out", [P, HALVES, D])
        ps_x1 = bank("ps_x1", [P, DC, SEQ])

        s_const, s_par, s_prep, s_empty, s_rows = (sem(n) for n in ("s_const", "s_par", "s_prep", "s_empty", "s_rows"))
        s_w2, s_wqh, s_wql, s_zero = (sem(n) for n in ("s_w2", "s_wqh", "s_wql", "s_zero"))
        loaded = [sem("loaded0"), sem("loaded1")]
        stored = [sem("stored0"), sem("stored1")]
        stored_x = [sem("stored_x0"), sem("stored_x1")]
        cn_loaded = [sem("cn_loaded0"), sem("cn_loaded1")]
        (st_done, mv_done, rs_done, xn_done, simw_done, enc_ps, enc_sb, enc_h, enc_l, sim_ps, rowb_done, sim_done,
         mx_done, nmx_done, exp_done, prec_done, pn_done, row_ps, gm_done, ngm_done, brow_done, brec_done, bn_done,
         bc_ps, hc_done, wc_done, wch_done, wcl_done, at_ps, at_done, hq_ps, hqh_done, hql_done, pr_done, prh_done,
         prl_done, out_ps, xs_done, x1_done, st1_done, mv1_done, rs1_done, xn1_done, x1t_ps, x1t_sb, lg_ps, lg_done,
         mx8_done, ix8_done, keep_done, ln_done, ln1_done, nw_done, nw1_done) = (sem(n) for n in (
             "st_done mv_done rs_done xn_done simw_done enc_ps enc_sb enc_h enc_l sim_ps rowb_done sim_done "
             "mx_done nmx_done exp_done prec_done pn_done row_ps gm_done ngm_done brow_done brec_done bn_done "
             "bc_ps hc_done wc_done wch_done wcl_done at_ps at_done hq_ps hqh_done hql_done pr_done prh_done "
             "prl_done out_ps xs_done x1_done st1_done mv1_done rs1_done xn1_done x1t_ps x1t_sb lg_ps lg_done "
             "mx8_done ix8_done keep_done ln_done ln1_done nw_done nw1_done").split())
        LOADS = 2 * 16
        CLEARED = E1 // BATCH

        block = ctx.enter_context(nc.Block())

        @block.sync
        def _(sp):
            sp.dma_start(consts[:], a["consts"]).then_inc(s_const, 16)
            sp.dma_start(wsim[:], a["wsim"]).then_inc(s_par, 16)
            sp.dma_start(bsim[:], a["b_sim"].partition_broadcast(P)).then_inc(s_par, 16)

            def load(t):
                wait_apart(sp, loaded[t.p], t.h * LOADS, gate)
                wait_apart(sp, sim_ps, t.n - 1, gate)
                wait_apart(sp, simw_done, (t.n - 1) * DC, gate)
                wait_apart(sp, xs_done, t.n - 1, gate)
                wait_apart(sp, xn_done, (t.n - 1) * HALVES, gate)
                sp.dma_start(x_in[t.p][:], a["x"][:, bass.ds(t.n * HALVES, HALVES), :]).then_inc(loaded[t.p], 16)
                sp.dma_start(ct[t.p][:], a["ctx_t"][bass.ds(t.n, 1)].rearrange("a p k j -> (a p) k j")).then_inc(loaded[t.p], 16)

            def load_cn(t):
                wait_apart(sp, cn_loaded[t.p], t.h * 16, gate)
                wait_apart(sp, hq_ps, t.n - 1, gate)
                sp.dma_start(cn[t.p][:], a["ctx"][bass.ds(t.n, 1)].rearrange("a j d -> (a j) d")).then_inc(cn_loaded[t.p], 16)

            def first_loads():
                load(At(0, 0, 0))
                sp.dma_start(wqv[:], a["wqv"]).then_inc(s_par, 16)
                sp.dma_start(bqv[:], a["bqv2"].partition_broadcast(P)).then_inc(s_par, 16)
                sp.dma_start(router_w[:], a["router_w"]).then_inc(s_par, 16)
                sp.dma_start(router_b[:], a["router_b"].partition_broadcast(P)).then_inc(s_par, 16)
                load(At(1, 0, 1))

            def fetch(t):
                if not isinstance(t.n, int) or t.n >= 2:
                    load(t)

            def store(t):
                wait_apart(sp, stored[t.p], t.h * 16, gate)
                wait_apart(sp, xn1_done, (t.n + 1) * HALVES, gate)
                wait_apart(sp, stored_x[t.p], t.h * 16, gate)
                sp.dma_start(x_res[:, bass.ds(t.n * HALVES, HALVES), :], x1[t.p][:]).then_inc(stored_x[t.p], 16)
                sp.dma_start(xn1_d.rearrange("(t p) d -> p t d", p=P)[:, bass.ds(t.n * HALVES, HALVES), :],
                             xn1[t.p][:]).then_inc(stored[t.p], 16)

            first_loads()
            def clear_sums(tiles):
                for sums in sums_d:
                    sp.dma_start(sums.rearrange("(c p) d -> p c d", p=P)[:, tiles, :],
                                 zeros[:].unsqueeze(1).to_broadcast([P, HALVES, D])).then_inc(s_rows, 16)

            def clear(t):
                if isinstance(t.n, int) and t.n == 0:
                    sp.wait_ge(s_empty, SLOT_TILES1)
                    sp.wait_ge(s_zero, 2)
                for c in range(SLOT_TILES1):
                    sp.dma_start(rows_d.rearrange("(e c p) r -> c p e r", c=SLOT_TILES1, p=P)[c][:, bass.ds(t.n * CLEARED, CLEARED), :],
                                 empty_rows[:, c:c + 1, :].to_broadcast([P, CLEARED, ROW])).then_inc(s_rows, 16)
                clear_sums(bass.ds(t.n * HALVES, HALVES))

            pipelined(sp, [[(1, fetch)],
                           [(0, clear), (2, load_cn)],
                           [],
                           [(3, store)]], BATCH)
            clear_sums(slice(TILES, TILES + SLOT_TILES1))
            sp.wait_ge(s_rows, (BATCH * (SLOT_TILES1 + len(sums_d)) + len(sums_d)) * 16)
            for q in range(2):
                sp.wait_ge(stored[q], BATCH // 2 * 16)
                sp.wait_ge(stored_x[q], BATCH // 2 * 16)

        @block.gpsimd
        def _(pool):
            pool.memset(empty_rows[:], 0.0).then_inc(s_zero, 1)
            pool.memset(zeros[:], 0.0).then_inc(s_zero, 1)
            pool.wait_ge(s_const, 16)
            pool.wait_ge(s_zero, 2)
            for c in range(SLOT_TILES1):
                pool.tensor_scalar(empty_rows[:, c, C_TOK:C_TOK + 1], consts[:, K_P:K_P + 1],
                                   float(TOKENS + c * P), None, ALU.add).then_inc(s_empty, 1)
            pool.wait_ge(s_par, 6 * 16)
            pool.wait_ge(s_wqh, 1)
            pool.tensor_tensor(wqv_lo[:], wqv[:, DC:3 * DC, :], wqv_hi[:], ALU.subtract).then_inc(s_wql, 1)

            def split_enc(t):
                pool.wait_ge(enc_sb, t.n + 1)
                pool.wait_ge(enc_h, t.n + 1)
                wait(pool, out_ps, t.n - 1)
                pool.tensor_tensor(enc_lo[t.p][:], enc_t[t.p][:], enc_hi[t.p][:], ALU.subtract).then_inc(enc_l, 1)

            def split_wc(t):
                pool.wait_ge(wc_done, (t.n + 1) * DC)
                pool.wait_ge(wch_done, t.n + 1)
                wait(pool, out_ps, t.n - 1)
                pool.tensor_tensor(wc_lo[t.p][:], wc[t.p][:], wc_hi[t.p][:], ALU.subtract).then_inc(wcl_done, 1)

            def split_prod(t):
                pool.wait_ge(pr_done, t.n + 1)
                pool.wait_ge(prh_done, t.n + 1)
                wait(pool, out_ps, t.n - 1)
                pool.tensor_tensor(prod_lo[t.p][:], prod[t.p][:], prod_hi[t.p][:], ALU.subtract).then_inc(prl_done, 1)

            def biased(t):
                pool.wait_ge(loaded[t.p], (t.h + 1) * LOADS)
                wait(pool, x1_done, t.n - 1)
                pool.tensor_tensor(xb[t.p][:], x_in[t.p][:], bqv[:], ALU.add).then_inc(xs_done, 1)

            pipelined(pool, [[],
                             [(2, biased), (3, split_enc)],
                             [(0, split_wc), (1, split_prod)]], BATCH)

        @block.tensor
        def _(pe):
            pe.wait_ge(s_const, 16)

            def turn(t):
                pe.wait_ge(xn_done, (t.n + 1) * HALVES)
                wait(pe, enc_sb, t.n)
                for s in range(HALVES):
                    for k in range(DC):
                        mm = pe.transpose(ps_enc[:, k, s * P:(s + 1) * P], xn[t.p][:, s, k * P:(k + 1) * P], ident)
                mm.then_inc(enc_ps, 1)

            def similarity(t):
                pe.wait_ge(simw_done, (t.n + 1) * DC)
                wait(pe, rowb_done, t.n)
                wait(pe, sim_done, t.n * HALVES)
                pe.wait_ge(s_w2, DC)
                for k in range(DC):
                    pe.matmul(ps_sim[:, 2, 0:CTX], w2rep[:, k, :], ct[t.p][:, k, :], start=k == 0, stop=k == DC - 1)
                pe.wait_ge(enc_sb, t.n + 1)
                for s in range(HALVES):
                    for k in range(DC):
                        mm = pe.matmul(ps_sim[:, s, 0:CTX], enc_t[t.p][:, k, s * P:(s + 1) * P], simw[t.p][:, k, :],
                                       start=k == 0, stop=k == DC - 1)
                mm.then_inc(sim_ps, 1)

            def peaks(t):
                pe.wait_ge(mx_done, t.n + 1)
                wait(pe, gm_done, t.n)
                wait(pe, brow_done, t.n)
                for s in range(HALVES):
                    mm = pe.matmul(ps_row[0:1, s * P:(s + 1) * P], mx[t.p][:, s:s + 1], ident, start=True, stop=True)
                mm.then_inc(row_ps, 1)

            def turn_probs(t):
                pe.wait_ge(pn_done, (t.n + 1) * HALVES)
                wait(pe, at_done, t.n)
                for s in range(HALVES):
                    mm = pe.transpose(ps_at[0:CTX, s * P:(s + 1) * P], probs_n[t.p][:, s, :], ident)
                mm.then_inc(at_ps, 1)

            def attend(t):
                pe.wait_ge(cn_loaded[t.p], (t.h + 1) * 16)
                pe.wait_ge(at_done, t.n + 1)
                wait(pe, hql_done, t.n)
                wait(pe, pr_done, t.n)
                for k in range(DC):
                    mm = pe.matmul(ps_hq[:, k, :], cn[t.p][:, k * P:(k + 1) * P], at_sb[t.p][:], start=True, stop=True)
                mm.then_inc(hq_ps, 1)

            def spread(t):
                pe.wait_ge(bn_done, t.n + 1)
                wait(pe, hc_done, t.n * DC)
                pe.matmul(ps_bc[:, 0:SEQ], ones_row[:], brow_n[t.p][:], start=True, stop=True).then_inc(bc_ps, 1)

            def project(s, part):
                def step(t):
                    if part == 0:
                        if s == 0:
                            wait(pe, x1_done, t.n)
                            pe.wait_ge(hqh_done, t.n + 1)
                            pe.wait_ge(hql_done, t.n + 1)
                            pe.wait_ge(s_wql, 1)
                        xh, xl, wh, wl = hq_hi, hq_lo, wqv_hi[:, 0:DC], wqv_lo[:, 0:DC]
                    elif part == 1:
                        if s == 0:
                            pe.wait_ge(prh_done, t.n + 1)
                            pe.wait_ge(prl_done, t.n + 1)
                        xh, xl, wh, wl = prod_hi, prod_lo, wqv_hi[:, DC:2 * DC], wqv_lo[:, DC:2 * DC]
                    else:
                        if s == 0:
                            pe.wait_ge(enc_l, t.n + 1)
                            pe.wait_ge(wch_done, t.n + 1)
                            pe.wait_ge(wcl_done, t.n + 1)
                        xh, xl, wh, wl = enc_hi, enc_lo, wc_hi[t.p], wc_lo[t.p]
                    n = 0
                    for k in range(DC):
                        for l, r in ((xh, wh), (xh, wl), (xl, wh)):
                            mm = pe.matmul(ps_out[:, s, :], l[t.p][:, k, s * P:(s + 1) * P], r[:, k, :],
                                           start=part == 0 and n == 0, stop=part == 2 and n == 3 * DC - 1)
                            n += 1
                    if s == HALVES - 1 and part == 2:
                        mm.then_inc(out_ps, 1)
                return step

            def turn_x1(t):
                pe.wait_ge(xn1_done, (t.n + 1) * HALVES)
                wait(pe, x1t_sb, t.n)
                wait(pe, lg_done, t.n * HALVES)
                for s in range(HALVES):
                    for k in range(DC):
                        mm = pe.transpose(ps_x1[:, k, s * P:(s + 1) * P], xn1[t.p][:, s, k * P:(k + 1) * P], ident)
                mm.then_inc(x1t_ps, 1)

            def router(t):
                pe.wait_ge(x1t_sb, t.n + 1)
                for s in range(HALVES):
                    for k in range(DC):
                        mm = pe.matmul(ps_x1[:, 0, s * E0:(s + 1) * E0], x1_t[t.p][:, k, s * P:(s + 1) * P], router_w[:, k, :],
                                       start=k == 0, stop=k == DC - 1)
                mm.then_inc(lg_ps, 1)

            pipelined(pe, [[],
                           [(0, turn), (1, similarity), (4, peaks), (10, turn_probs), (11, spread), (12, attend)],
                           [(2, project(0, 0)), (3, project(0, 1)), (5, project(0, 2)), (6, project(1, 0)), (8, project(1, 1)),
                            (13, project(1, 2))],
                           [(7, turn_x1), (9, router)]], BATCH)

        @block.scalar
        def _(act):
            act.preload_act_table_set("natural_log_exp_and_others")
            act.wait_ge(s_par, 6 * 16)
            act.wait_ge(s_prep, 4)
            act.activation(wqv_hi[:], wqv[:, DC:3 * DC, :], ACT.Copy).then_inc(s_wqh, 1)

            def root(t, m, lv, r, m_s, l_s, r_s, nw_s):
                act.wait_ge(m_s, (t.n + 1) * HALVES)
                wait(act, nw_s, (t.n - 1) * 3)
                act.activation(lv[t.p][:], m[t.p][:, :, 1], ACT.Ln, bias=eps[:]).then_inc(l_s, 1)
                act.wait_ge(l_s, t.n + 1)
                act.activation(r[t.p][:], lv[t.p][:], ACT.Exp, scale=-0.5).then_inc(r_s, 1)

            def root0(t):
                root(t, mv, lnv, rstd, mv_done, ln_done, rs_done, nw_done)

            def turned(t):
                act.wait_ge(enc_ps, t.n + 1)
                wait(act, sim_ps, t.n - 1)
                wait(act, hc_done, (t.n - 1) * DC)
                wait(act, pr_done, t.n - 1)
                wait(act, enc_l, t.n - 1)
                act.activation(enc_t[t.p][:], ps_enc[:], ACT.Copy).then_inc(enc_sb, 1)

            def split_enc(t):
                act.wait_ge(enc_sb, t.n + 1)
                wait(act, out_ps, t.n - 1)
                act.activation(enc_hi[t.p][:], enc_t[t.p][:], ACT.Copy).then_inc(enc_h, 1)

            def row_bias(t):
                act.wait_ge(sim_ps, t.n + 1)
                wait(act, sim_done, (t.n - 1) * HALVES)
                act.activation(rowb[t.p][:], ps_sim[:, 2, 0:CTX], ACT.Identity, bias=bsim[:]).then_inc(rowb_done, 1)

            def exps(t):
                act.wait_ge(nmx_done, t.n + 1)
                act.wait_ge(sim_done, (t.n + 1) * HALVES)
                wait(act, pn_done, (t.n - 1) * HALVES)
                wait(act, prec_done, t.n - 1)
                for s in range(HALVES):
                    act.activation(probs[t.p][:, s, :], sim[t.p][:, s, :], ACT.Exp, bias=nmx[t.p][:, s:s + 1],
                                   accum_out=psums[t.p][:, s:s + 1]).then_inc(exp_done, 1)

            def exps_row(t):
                act.wait_ge(row_ps, t.n + 1)
                act.wait_ge(ngm_done, t.n + 1)
                wait(act, bn_done, t.n - 1)
                wait(act, brec_done, t.n - 1)
                act.activation(brow[t.p][:], ps_row[0:1, 0:SEQ], ACT.Exp, bias=ngm[t.p][:], accum_out=bsum[t.p][:]).then_inc(brow_done, 1)

            def probs_t(t):
                act.wait_ge(at_ps, t.n + 1)
                wait(act, hq_ps, t.n - 1)
                act.activation(at_sb[t.p][:], ps_at[0:CTX, 0:SEQ], ACT.Copy).then_inc(at_done, 1)

            def attended(t):
                act.wait_ge(hq_ps, t.n + 1)
                wait(act, out_ps, t.n - 1)
                wait(act, hql_done, t.n - 1)
                act.activation(hq_hi[t.p][:], ps_hq[:], ACT.Copy).then_inc(hqh_done, 1)

            def product(t):
                act.wait_ge(pr_done, t.n + 1)
                wait(act, prl_done, t.n - 1)
                act.activation(prod_hi[t.p][:], prod[t.p][:], ACT.Copy).then_inc(prh_done, 1)

            def weights(t):
                act.wait_ge(wc_done, (t.n + 1) * DC)
                wait(act, wcl_done, t.n - 1)
                act.activation(wc_hi[t.p][:], wc[t.p][:], ACT.Copy).then_inc(wch_done, 1)

            def root1(t):
                root(t, mv1, lnv1, rstd1, mv1_done, ln1_done, rs1_done, nw1_done)

            def turned_x1(t):
                act.wait_ge(x1t_ps, t.n + 1)
                wait(act, lg_ps, t.n - 1)
                act.activation(x1_t[t.p][:], ps_x1[:], ACT.Copy).then_inc(x1t_sb, 1)

            pipelined(act, [[(8, root0)],
                            [(0, turned), (3, split_enc), (4, row_bias), (6, exps), (9, exps_row), (10, probs_t),
                             (11, attended)],
                            [(1, weights), (2, product)],
                            [(5, root1), (7, turned_x1)]], BATCH)

        @block.vector
        def _(ve):
            ve.memset(ones_bf[:], 1.0).then_inc(s_prep, 1)
            ve.memset(w2rep[:], 1.0).then_inc(s_prep, 1)
            ve.memset(ones_row[:], 1.0).then_inc(s_prep, 1)
            ve.memset(eps[:], LN_EPS).then_inc(s_prep, 1)
            ve.wait_ge(s_const, 16)
            ve.wait_ge(s_prep, 4)
            ve.tensor_copy(tri_bf[:], consts[:, K_SU:K_SU + P]).then_inc(s_prep, 1)
            ve.wait_ge(s_par, 6 * 16)
            for k in range(DC):
                ve.tensor_scalar(w2rep[:, k, :], w2rep[:, k, :], wsim[:, 1, k:k + 1], None, ALU.mult).then_inc(s_w2, 1)

            def moments(t, src, st, m, st_s, m_s):
                apart(ve, gate)
                for s in range(HALVES):
                    ve.bn_stats(st[t.p][:, s, :], src[:, s, :]).then_inc(st_s, 1)
                ve.wait_ge(st_s, (t.n + 1) * HALVES)
                apart(ve, gate)
                for s in range(HALVES):
                    ve.bn_aggr(m[t.p][:, s, :], st[t.p][:, s, :]).then_inc(m_s, 1)

            def newton_step(t, m, r, nw, r_s, nw_s):
                ve.wait_ge(r_s, t.n + 1)
                ve.scalar_tensor_tensor(nw[t.p][:], m[t.p][:, :, 1], LN_EPS, r[t.p][:], ALU.add, ALU.mult).then_inc(nw_s, 1)
                ve.wait_ge(nw_s, t.n * 3 + 1)
                ve.scalar_tensor_tensor(nw[t.p][:], nw[t.p][:], -0.5, r[t.p][:], ALU.mult, ALU.mult).then_inc(nw_s, 1)
                ve.wait_ge(nw_s, t.n * 3 + 2)
                ve.scalar_tensor_tensor(nw[t.p][:], nw[t.p][:], 1.5, r[t.p][:], ALU.add, ALU.mult).then_inc(nw_s, 1)

            def normed(t, src, m, nw, dst, nw_s, dst_s):
                ve.wait_ge(nw_s, t.n * 3 + 3)
                for s in range(HALVES):
                    ve.tensor_scalar(dst[t.p][:, s, :], src[:, s, :], m[t.p][:, s, 0:1], nw[t.p][:, s:s + 1],
                                     ALU.subtract, ALU.mult).then_inc(dst_s, 1)

            def normed0(t):
                wait(ve, enc_ps, t.n - 1)
                normed(t, x_in[t.p], mv, newton, xn, nw_done, xn_done)

            def normed1(t):
                wait(ve, x1t_ps, t.n - 1)
                wait(ve, stored[t.p], t.h * 16)
                normed(t, x1[t.p], mv1, newton1, xn1, nw1_done, xn1_done)

            def context(t):
                ve.wait_ge(loaded[t.p], (t.h + 1) * LOADS)
                wait(ve, sim_ps, t.n - 1)
                for k in range(DC):
                    ve.tensor_scalar(simw[t.p][:, k, :], ct[t.p][:, k, :], wsim[:, 2, k:k + 1], wsim[:, 0, k:k + 1],
                                     ALU.mult, ALU.add).then_inc(simw_done, 1)
                moments(t, x_in[t.p], stats, mv, st_done, mv_done)

            def newton0(t):
                newton_step(t, mv, rstd, newton, rs_done, nw_done)

            def sims(t):
                ve.wait_ge(rowb_done, t.n + 1)
                wait(ve, exp_done, (t.n - 1) * HALVES)
                for s in range(HALVES):
                    ve.tensor_tensor(sim[t.p][:, s, :], ps_sim[:, s, 0:CTX], rowb[t.p][:], ALU.add).then_inc(sim_done, 1)
                ve.wait_ge(sim_done, (t.n + 1) * HALVES)
                wait(ve, row_ps, t.n - 1)
                ve.tensor_reduce(mx[t.p][:], sim[t.p][:], AX.X, ALU.max).then_inc(mx_done, 1)
                ve.wait_ge(mx_done, t.n + 1)
                ve.tensor_scalar(nmx[t.p][:], mx[t.p][:], -1.0, None, ALU.mult).then_inc(nmx_done, 1)

            def probs_norm(t):
                ve.wait_ge(exp_done, (t.n + 1) * HALVES)
                ve.reciprocal(prec[t.p][:], psums[t.p][:]).then_inc(prec_done, 1)
                ve.wait_ge(prec_done, t.n + 1)
                wait(ve, at_ps, t.n - 1)
                for s in range(HALVES):
                    ve.tensor_scalar(probs_n[t.p][:, s, :], probs[t.p][:, s, :], prec[t.p][:, s:s + 1], None,
                                     ALU.mult).then_inc(pn_done, 1)

            def peak(t):
                ve.wait_ge(row_ps, t.n + 1)
                ve.tensor_reduce(gm[t.p][:], ps_row[0:1, 0:SEQ], AX.X, ALU.max).then_inc(gm_done, 1)
                ve.wait_ge(gm_done, t.n + 1)
                wait(ve, brow_done, t.n - 1)
                ve.tensor_scalar(ngm[t.p][:], gm[t.p][:], -1.0, None, ALU.mult).then_inc(ngm_done, 1)

            def row_norm(t):
                ve.wait_ge(brow_done, t.n + 1)
                ve.reciprocal(brec[t.p][:], bsum[t.p][:]).then_inc(brec_done, 1)
                ve.wait_ge(brec_done, t.n + 1)
                wait(ve, bc_ps, t.n - 1)
                ve.tensor_scalar(brow_n[t.p][:], brow[t.p][:], brec[t.p][:], None, ALU.mult).then_inc(bn_done, 1)

            def product(t):
                ve.wait_ge(hqh_done, t.n + 1)
                ve.wait_ge(enc_sb, t.n + 1)
                wait(ve, prh_done, t.n - 1)
                wait(ve, prl_done, t.n - 1)
                ve.tensor_tensor(prod[t.p][:], ps_hq[:], enc_t[t.p][:], ALU.mult).then_inc(pr_done, 1)
                wait(ve, out_ps, t.n - 1)
                ve.tensor_tensor(hq_lo[t.p][:], ps_hq[:], hq_hi[t.p][:], ALU.subtract).then_inc(hql_done, 1)

            def weights(t):
                ve.wait_ge(bc_ps, t.n + 1)
                for k in range(DC):
                    wait(ve, wc_done, (t.n - 1) * DC)
                    ve.tensor_tensor_reduce(bjunk[t.p][:, k, :], enc_t[t.p][:, k, :], ps_bc[:, 0:SEQ], 1.0, 0.0,
                                            ALU.mult, ALU.add, hc[t.p][:, k:k + 1]).then_inc(hc_done, 1)
                ve.wait_ge(hc_done, (t.n + 1) * DC)
                wait(ve, wch_done, t.n - 1)
                wait(ve, wcl_done, t.n - 1)
                for k in range(DC):
                    ve.scalar_tensor_tensor(wc[t.p][:, k, :], wqv[:, 3 * DC + k, :], hc[t.p][:, k:k + 1], wqv[:, k, :],
                                            ALU.mult, ALU.add).then_inc(wc_done, 1)

            def add(t):
                ve.wait_ge(out_ps, t.n + 1)
                ve.wait_ge(xs_done, t.n + 1)
                wait(ve, xn1_done, (t.n - 1) * HALVES)
                wait(ve, stored_x[t.p], t.h * 16)
                ve.tensor_tensor(x1[t.p][:], ps_out[:], xb[t.p][:], ALU.add).then_inc(x1_done, 1)
                ve.wait_ge(x1_done, t.n + 1)
                moments(t, x1[t.p], stats1, mv1, st1_done, mv1_done)

            def newton1_step(t):
                newton_step(t, mv1, rstd1, newton1, rs1_done, nw1_done)

            def route(t):
                ve.wait_ge(lg_ps, t.n + 1)
                wait(ve, ix8_done, (t.n - 1) * HALVES)
                for s in range(HALVES):
                    ve.tensor_tensor(lg[t.p][:, s, :], ps_x1[:, 0, s * E0:(s + 1) * E0], router_b[:],
                                     ALU.add).then_inc(lg_done, 1)

            def largest(t):
                ve.wait_ge(lg_done, (t.n + 1) * HALVES)
                apart(ve, gate)
                for s in range(HALVES):
                    ve.max(mx8[t.p][:, s, :], lg[t.p][:, s, :]).then_inc(mx8_done, 1)

            def places(t):
                ve.wait_ge(mx8_done, (t.n + 1) * HALVES)
                apart(ve, gate)
                for s in range(HALVES):
                    ve.max_index(ix8[t.p][:, s, :], mx8[t.p][:, s, :], lg[t.p][:, s, :]).then_inc(ix8_done, 1)

            def keep(t):
                ve.wait_ge(ix8_done, (t.n + 1) * HALVES)
                apart(ve, gate)
                own = bass.ds(t.n * HALVES, HALVES)
                ve.tensor_copy(logits[:, own, :], lg[t.p][:]).then_inc(keep_done, 1)
                ve.tensor_copy(top2[:, own, :], mx8[t.p][:, :, 0:TOP0]).then_inc(keep_done, 1)
                ve.tensor_copy(exp2[:, own, :], ix8[t.p][:, :, 0:TOP0]).then_inc(keep_done, 1)

            pipelined(ve, [[(4, context), (7, newton0), (10, normed0)],
                           [(1, sims), (5, peak), (6, probs_norm), (8, row_norm), (12, weights), (14, product)],
                           [],
                           [(0, add), (2, newton1_step), (3, normed1), (9, route), (11, largest), (13, places), (15, keep)]], BATCH)


def phase_experts(nc, env):
    a, consts, tri_bf, ones_bf, gate = (env[k] for k in ("a", "consts", "tri_bf", "ones_bf", "gate"))
    logits, top2, exp2, w_own, slot_own, xn1_d, y0_d = (env[k] for k in (
        "logits", "top2", "exp2", "w_own", "slot_own", "xn1_d", "y0_d"))
    NT = TOP0 * TILES
    CHUNK = NT // 4
    ctx = ExitStack()
    with ctx:
        def sb(name, shape, dt):
            return ctx.enter_context(nc.sbuf_tensor("e_" + name, shape, dt))

        def two(name, shape, dt):
            return [sb(f"{name}{i}", shape, dt) for i in range(2)]

        def sem(name):
            env["sems"].append(nc.alloc_semaphore(name="e_" + name))
            return env["sems"][-1]

        ident = consts[:, K_ID:K_ID + P]
        expl = sb("expl", [P, TILES, E0], F32)
        zsum = sb("zsum", [P, TILES], F32)
        zrec = sb("zrec", [P, TILES], F32)
        pr = sb("pr", [P, TOP0, TILES], F32)
        den = sb("den", [P, TILES], F32)
        wt = sb("wt", [P, TOP0, TILES], F32)
        valid = sb("valid", [P, TOP0, TILES], F32)
        hot = sb("hot", [P, TOP0, TILES, E0], F32)
        hot_bf = sb("hot_bf", [P, NT * E0], BF16)
        total = sb("total", [P, NT * E0], F32)
        ran = sb("ran", [P, NT * E0], F32)
        ones_nt = sb("ones_nt", [P, NT], F32)
        before = sb("before", [P, NT * E0], F32)
        pos = sb("pos", [P, NT], F32)
        keep = sb("keep", [P, NT], F32)
        slot = sb("slot", [P, NT], F32)
        slot_i = sb("slot_i", [P, NT], I32)
        hi_i = sb("hi_i", [P, NT], I32)
        lo_i = sb("lo_i", [P, NT], I32)
        hi = sb("hi", [P, NT], F32)
        lo = sb("lo", [P, NT], F32)
        tile_no = sb("tile_no", [P, TILES], F32)
        in_lo = sb("in_lo", [P, 2, CHUNK, P], BF16)
        xg_all = sb("xg_all", [P, 2, SLOT_TILES0, D], F32)
        hid_all = sb("hid_all", [P, 2, SLOTS0], F32)
        is_hi = hid_all[:].rearrange("p a b -> p (a b)").bitcast(BF16).rearrange("p (n h) -> p n h", h=HI0)
        in_hi = xg_all[:].rearrange("p a b c -> p (a b c)").bitcast(BF16).rearrange("p (n a h) -> p n a h", a=2, h=HI0)
        tok = sb("tok", [P, 2, HI0], F32)
        tok_of = sb("tok_of", [P, HI0], U32)
        fc1 = sb("fc1", [P, DC, HID0], F32)
        fc2 = sb("fc2", [P, HC0, D], F32)
        fc1_hi, fc1_lo = two("fc1_hi", [P, DC, HID0], F32R), two("fc1_lo", [P, DC, HID0], F32R)
        fc2_hi, fc2_lo = sb("fc2_hi", [P, HC0, D], F32R), sb("fc2_lo", [P, HC0, D], F32R)
        b1 = two("b1", [P, HC0], F32)
        b2 = two("b2", [P, D], F32)
        ls = two("ls", [P, D], F32)
        b2ls = sb("b2ls", [P, D], F32)
        own = two("own", [P, SLOT_TILES0], U32)
        xg = [xg_all[:, i] for i in range(2)]
        xt_hi, xt_lo = two("xt_hi", [P, DC, SLOTS0], F32R), two("xt_lo", [P, DC, SLOTS0], F32R)
        hid = [hid_all[:, i] for i in range(2)]
        hid_hi, hid_lo = sb("hid_hi", [P, HC0, SLOTS0], F32R), sb("hid_lo", [P, HC0, SLOTS0], F32R)
        ys = two("ys", [P, D], F32)
        yo = two("yo", [P, D], F32)

        ps_x = [ctx.enter_context(nc.psum_tensor(f"e_ps_x{i}", [P, 512], F32)) for i in range(2)]
        ps_f = [ctx.enter_context(nc.psum_tensor(f"e_ps_f{i}", [P, 2, 512], F32)) for i in range(2)]
        ps_y = [ctx.enter_context(nc.psum_tensor(f"e_ps_y{i}", [P, 512], F32)) for i in range(2)]

        s_chain, s_exp, s_hot, s_pre, s_oh, s_tok, s_own, s_tile = (sem(n) for n in (
            "s_chain", "s_exp", "s_hot", "s_pre", "s_oh", "s_tok", "s_own", "s_tile"))
        (w_ld, w_hi, w_lo, b_ld, b2_done, own_done, xt_ps, xth_done, xtl_done, f_ps, hid_done, hh_done, hl_done,
         y_ps, ys_done, yt_done, yo_done, w2_ld, w2_hi, w2_lo) = (sem(n) for n in (
             "w_ld w_hi w_lo b_ld b2_done own_done xt_ps xth_done xtl_done f_ps hid_done hh_done hl_done "
             "y_ps ys_done yt_done yo_done w2_ld w2_hi w2_lo").split())
        gathered = [sem("gathered0"), sem("gathered1")]
        y_st = [sem("y_st0"), sem("y_st1")]
        CH = HC0
        ST = SLOT_TILES0
        TURN_SLOTS = [5, 5.2] + [c + 4.4 for c in range(2, ST)]

        def used(c):
            return min(P, USED0 - c * P)

        block = ctx.enter_context(nc.Block())

        @block.sync
        def _(sp):
            def load(t):
                e = bass.ds(t.n, 1)
                wait_apart(sp, w_ld, t.n * 16, gate)
                wait_apart(sp, w_hi, t.n, gate)
                wait_apart(sp, w_lo, t.n, gate)
                sp.dma_start(fc1[:], a["fc1_t"][e].rearrange("e p k h -> (e p) k h")).then_inc(w_ld, 16)
                wait_apart(sp, w2_ld, t.n * 16, gate)
                wait_apart(sp, w2_hi, t.n, gate)
                wait_apart(sp, w2_lo, t.n, gate)
                sp.dma_start(fc2[:], a["fc2_t"][e].rearrange("e p m c -> (e p) m c")).then_inc(w2_ld, 16)
                wait_apart(sp, b_ld, t.n * 48, gate)
                wait_apart(sp, hid_done, (t.n - 1) * CH, gate)
                wait_apart(sp, yo_done, (t.n - 1) * ST, gate)
                sp.dma_start(b1[t.p][:], a["fc1_b"][e].rearrange("e p m -> (e p) m")).then_inc(b_ld, 16)
                sp.dma_start(b2[t.p][:], a["fc2_b"][e].rearrange("e c -> (e c)").partition_broadcast(P)).then_inc(b_ld, 16)
                sp.dma_start(ls[t.p][:], a["ls"][e].rearrange("e c -> (e c)").partition_broadcast(P)).then_inc(b_ld, 16)

            def store(c):
                def part(t):
                    q = (t.p * ST + c) % 2
                    wait_apart(sp, yo_done, t.n * ST + c + 1, gate)
                    sp.dma_start(y0_d.rearrange("(e c p) d -> c p e d", c=ST, p=P)[c][:, bass.ds(t.n, 1), :].rearrange("p e d -> p (e d)"),
                                 yo[q][:]).then_inc(y_st[q], 16)
                return part

            pipelined(sp, [[(0, load)], [(6 + c, store(c)) for c in range(ST)]], E0)
            for q in range(2):
                sp.wait_ge(y_st[q], E0 * ST // 2 * 16)

        @block.gpsimd
        def _(pool):
            pool.iota(tile_no[:], [[1, TILES]], base=0, channel_multiplier=0,
                      allow_small_or_imprecise_dtypes=True).then_inc(s_tile, 1)

            def gather(t):
                pool.wait_ge(own_done, t.n + 1)
                wait(pool, xt_ps, (t.n - 1) * ST)
                wait(pool, yt_done, (t.n - 1) * ST)
                apart(pool, gate)
                for c in range(ST):
                    pool.indirect_dma_start(xg[t.p][:, c, :], None, xn1_d,
                                            bass.IndirectOffsetOnAxis(ap=own[t.p][:, c:c + 1], axis=0)
                                            ).then_inc(gathered[t.p], 16)

            def split_up(t):
                pool.wait_ge(w_ld, (t.n + 1) * 16)
                pool.wait_ge(w_hi, t.n + 1)
                wait(pool, f_ps, (t.n - 1) * CH)
                pool.tensor_tensor(fc1_lo[t.p][:], fc1[:], fc1_hi[t.p][:], ALU.subtract).then_inc(w_lo, 1)

            def split_later_up(t):
                if not isinstance(t.n, int) or t.n > 0:
                    split_up(t)

            def split_down(t):
                pool.wait_ge(w2_ld, (t.n + 1) * 16)
                pool.wait_ge(w2_hi, t.n + 1)
                wait(pool, y_ps, t.n * ST)
                pool.tensor_tensor(fc2_lo[:], fc2[:], fc2_hi[:], ALU.subtract).then_inc(w2_lo, 1)

            split_up(At(0, 0, 0))
            pipelined(pool, [[(0, gather), (4, split_later_up)], [(-1, split_down)]], E0)

        @block.tensor
        def _(pe):
            pe.wait_ge(s_hot, 1)
            pe.matmul(ps_y[0][:], tri_bf[:], hot_bf[:], start=True, stop=True)
            pe.matmul(ps_y[1][:], ones_bf[:], hot_bf[:], start=True, stop=True).then_inc(s_pre, 1)
            for c in range(NT // CHUNK):
                pe.wait_ge(s_oh, c + 1)
                for n in range(CHUNK):
                    mm = pe.matmul(ps_x[0][:, 0:2 * HI0], in_lo[:, c % 2, n, :],
                                   in_hi[:, c * CHUNK + n, :, :].rearrange("p a b -> p (a b)"),
                                   start=c == 0 and n == 0, stop=c == NT // CHUNK - 1 and n == CHUNK - 1)
                mm.then_inc(s_tok, 1)

            def turn(c):
                def part(t):
                    pe.wait_ge(gathered[t.p], (t.h + 1) * ST * 16)
                    q = (t.p * ST + c) % 2
                    wait(pe, xtl_done, t.n * ST + c - 1)
                    for k in range(DC):
                        mm = pe.transpose(ps_x[q][:, k * P:(k + 1) * P], xg[t.p][:, c, k * P:(k + 1) * P], ident)
                    mm.then_inc(xt_ps, 1)
                return part

            def up(t):
                pe.wait_ge(xtl_done, (t.n + 1) * ST)
                pe.wait_ge(w_lo, t.n + 1)
                for m in range(CH):
                    wait(pe, hid_done, t.n * CH + m - 1)
                    for n in range(2):
                        i = 0
                        for k in range(DC):
                            for l, r in ((fc1_hi, xt_hi), (fc1_hi, xt_lo), (fc1_lo, xt_hi)):
                                mm = pe.matmul(ps_f[m % 2][:, n, 0:HALF0], l[t.p][:, k, m * P:(m + 1) * P],
                                               r[t.p][:, k, n * HALF0:(n + 1) * HALF0], start=i == 0, stop=i == 3 * DC - 1)
                                i += 1
                    mm.then_inc(f_ps, 1)

            def down(c):
                def part(t):
                    if c == 0:
                        pe.wait_ge(w2_lo, t.n + 1)
                    q = (t.p * ST + c) % 2
                    wait(pe, ys_done, t.n * ST + c - 1)
                    i = 0
                    for m in range(CH):
                        if c == 0:
                            pe.wait_ge(hl_done, t.n * CH + m + 1)
                        for l, r in ((hid_hi, fc2_hi), (hid_hi, fc2_lo), (hid_lo, fc2_hi)):
                            mm = pe.matmul(ps_y[q][0:used(c), 0:D], l[:, m, c * P:c * P + used(c)], r[:, m, :],
                                           start=i == 0, stop=i == 3 * CH - 1)
                            i += 1
                    mm.then_inc(y_ps, 1)
                return part

            pipelined(pe, [[(TURN_SLOTS[c], turn(c)) for c in range(ST)], [(0, up)] + [(6 + c, down(c)) for c in range(ST)]], E0)

        @block.scalar
        def _(act):
            act.preload_act_table_set("exp_and_others")
            act.wait_ge(w_ld, 16)
            act.activation(fc1_hi[0][:], fc1[:], ACT.Copy).then_inc(w_hi, 1)
            act.wait_ge(s_chain, 2)
            act.activation(expl[:], expl[:], ACT.Exp).then_inc(s_exp, 1)
            act.activation(pr[:, 1, :], pr[:, 1, :], ACT.Exp).then_inc(s_exp, 1)

            def split_up(t):
                act.wait_ge(w_ld, (t.n + 1) * 16)
                wait(act, f_ps, (t.n - 1) * CH)
                wait(act, w_lo, t.n - 1)
                act.activation(fc1_hi[t.p][:], fc1[:], ACT.Copy).then_inc(w_hi, 1)

            def split_later_up(t):
                if not isinstance(t.n, int) or t.n > 0:
                    split_up(t)

            def split_down(t):
                act.wait_ge(w2_ld, (t.n + 1) * 16)
                wait(act, y_ps, t.n * ST)
                wait(act, w2_lo, t.n)
                act.activation(fc2_hi[:], fc2[:], ACT.Copy).then_inc(w2_hi, 1)

            def turned(c):
                def part(t):
                    q = (t.p * ST + c) % 2
                    act.wait_ge(xt_ps, t.n * ST + c + 1)
                    if c == 0:
                        wait(act, f_ps, (t.n - 1) * CH)
                    act.activation(xt_hi[t.p][:, :, c * P:(c + 1) * P], ps_x[q][:, 0:DC * P].rearrange("p (k s) -> p k s", k=DC),
                                   ACT.Copy).then_inc(xth_done, 1)
                return part

            def gelu(m):
                def part(t):
                    act.wait_ge(b_ld, (t.n + 1) * 48)
                    act.wait_ge(f_ps, t.n * CH + m + 1)
                    wait(act, hl_done, t.n * CH + m - 1)
                    act.activation(hid[m % 2][:, 0:USED0].rearrange("p (n s) -> p n s", n=2), ps_f[m % 2][:, :, 0:HALF0], ACT.Gelu,
                                   bias=b1[t.p][:, m:m + 1]).then_inc(hid_done, 1)
                return part

            pipelined(act, [[(4.5, split_later_up)] + [(TURN_SLOTS[c], turned(c)) for c in range(ST)],
                            [(-1, split_down)] + [(m / 2, gelu(m)) for m in range(CH)]], E0)

        @block.vector
        def _(ve):
            n_chain = [0]

            def link(ins):
                n_chain[0] += 1
                ins.then_inc(s_chain, 1)
                ve.wait_ge(s_chain, n_chain[0])

            def beside(ins):
                n_chain[0] += 1
                ins.then_inc(s_chain, 1)

            def wide(ap, n):
                return ap.unsqueeze(2).to_broadcast([P, TILES, n])

            ve.tensor_tensor(expl[:], logits[:], wide(top2[:, :, 0], E0), ALU.subtract).then_inc(s_chain, 1)
            n_chain[0] += 1
            link(ve.tensor_tensor(pr[:, 1, :], top2[:, :, 1], top2[:, :, 0], ALU.subtract))
            ve.memset(ones_nt[:], 1.0).then_inc(s_own, 1)
            ve.wait_ge(s_exp, 2)
            link(ve.tensor_reduce(zsum[:], expl[:], AX.X, ALU.add))
            link(ve.reciprocal(pr[:, 0, :], zsum[:]))
            link(ve.tensor_tensor(pr[:, 1, :], pr[:, 1, :], pr[:, 0, :], ALU.mult))
            link(ve.scalar_tensor_tensor(den[:], pr[:, 0, :], W_EPS, pr[:, 1, :], ALU.add, ALU.add))
            link(ve.reciprocal(zrec[:], den[:]))
            beside(ve.tensor_tensor(wt[:, 0, :], pr[:, 0, :], zrec[:], ALU.mult))
            link(ve.tensor_tensor(wt[:, 1, :], pr[:, 1, :], zrec[:], ALU.mult))
            link(ve.tensor_scalar(valid[:], wt[:], W_EPS, None, ALU.is_gt))
            for k, step in ((0, beside), (1, link)):
                step(ve.tensor_tensor(hot[:, k], wide(exp2[:, :, k], E0),
                                      consts[:, K_IOTA:K_IOTA + E0].unsqueeze(1).to_broadcast([P, TILES, E0]), ALU.is_equal))
            for k, step in ((0, beside), (1, link)):
                step(ve.tensor_tensor(hot[:, k], hot[:, k], wide(valid[:, k, :], E0), ALU.mult))
            ve.tensor_copy(hot_bf[:], hot[:].rearrange("p k t e -> p (k t e)")).then_inc(s_hot, 1)
            ve.wait_ge(s_pre, 1)
            ve.wait_ge(s_own, 1)
            link(ve.tensor_copy(total[:], ps_y[1][:]))
            for e in range(E0):
                v = slice(e, NT * E0, E0)
                step = link if e == E0 - 1 else beside
                step(ve.tensor_tensor_scan(ran[:, v], ones_nt[:], total[:, v], 0.0, ALU.mult, ALU.add))
            link(ve.tensor_tensor(before[:], ran[:], total[:], ALU.subtract))
            link(ve.tensor_tensor(before[:], before[:], ps_y[0][:], ALU.add))
            link(ve.tensor_tensor(before[:], before[:], hot[:].rearrange("p k t e -> p (k t e)"), ALU.mult))
            link(ve.tensor_reduce(pos[:], before[:].rearrange("p (n e) -> p n e", e=E0), AX.X, ALU.add))
            link(ve.tensor_scalar(keep[:], pos[:], float(CAP0), None, ALU.is_lt))
            link(ve.tensor_tensor(keep[:], keep[:], valid[:].rearrange("p k t -> p (k t)"), ALU.mult))
            halves = [slice(k * TILES, (k + 1) * TILES) for k in range(TOP0)]
            for k, step in ((0, beside), (1, link)):
                n = halves[k]
                step(ve.scalar_tensor_tensor(slot[:, n], exp2[:, :, k], float(SLOTS0), pos[:, n], ALU.mult, ALU.add))
            link(ve.tensor_tensor(slot[:], slot[:], keep[:], ALU.mult))
            for k, n in enumerate(halves):
                beside(ve.tensor_copy(slot_own[:, :, k], slot[:, n]))
                beside(ve.tensor_tensor(w_own[:, :, k], wt[:, k, :], keep[:, n], ALU.mult))
            link(ve.tensor_copy(slot_i[:], slot[:]))
            beside(ve.tensor_scalar(hi_i[:], slot_i[:], 7, None, ALU.logical_shift_right))
            link(ve.tensor_scalar(lo_i[:], slot_i[:], P - 1, None, ALU.bitwise_and))
            beside(ve.tensor_copy(hi[:], hi_i[:]))
            link(ve.tensor_copy(lo[:], lo_i[:]))
            link(ve.scalar_tensor_tensor(lo[:], lo[:], 1.0, keep[:], ALU.add, ALU.mult))
            link(ve.tensor_scalar(lo[:], lo[:], -1.0, None, ALU.add))
            link(ve.tensor_tensor(is_hi, hi[:].unsqueeze(2).to_broadcast([P, NT, HI0]),
                                  consts[:, K_IOTA:K_IOTA + HI0].unsqueeze(1).to_broadcast([P, NT, HI0]), ALU.is_equal))
            ve.wait_ge(s_tile, 1)
            for k in range(TOP0):
                n = slice(k * TILES, (k + 1) * TILES)
                beside(ve.tensor_tensor(in_hi[:, n, 0, :], is_hi[:, n, :], wide(tile_no[:], HI0), ALU.mult))
            link(ve.tensor_scalar(in_hi[:, :, 1, :], is_hi, consts[:, K_P:K_P + 1], None, ALU.mult))
            for c in range(NT // CHUNK):
                if c >= 2:
                    ve.wait_ge(s_tok, c - 1)
                ve.tensor_tensor(in_lo[:, c % 2], lo[:, c * CHUNK:(c + 1) * CHUNK].unsqueeze(2).to_broadcast([P, CHUNK, P]),
                                 consts[:, K_IOTA:K_IOTA + P].unsqueeze(1).to_broadcast([P, CHUNK, P]),
                                 ALU.is_equal).then_inc(s_oh, 1)
            ve.wait_ge(s_tok, NT // CHUNK)
            link(ve.tensor_copy(tok[:], ps_x[0][:, 0:2 * HI0].rearrange("p (a b) -> p a b", a=2)))
            link(ve.scalar_tensor_tensor(tok_of[:], tok[:, 0, :], float(P), tok[:, 1, :], ALU.mult, ALU.add))

            def pick(t):
                wait(ve, gathered[t.p], t.h * ST * 16)
                ve.tensor_copy(own[t.p][:], tok_of[:, bass.ds(t.n * ST, ST)]).then_inc(own_done, 1)

            def turned(c):
                def part(t):
                    q = (t.p * ST + c) % 2
                    ve.wait_ge(xth_done, t.n * ST + c + 1)
                    if c == 0:
                        wait(ve, f_ps, (t.n - 1) * CH)
                    ve.tensor_tensor(xt_lo[t.p][:, :, c * P:(c + 1) * P], ps_x[q][:, 0:DC * P].rearrange("p (k s) -> p k s", k=DC),
                                     xt_hi[t.p][:, :, c * P:(c + 1) * P], ALU.subtract).then_inc(xtl_done, 1)
                return part

            def hidden(m):
                def part(t):
                    wait(ve, y_ps, t.n * ST)
                    ve.wait_ge(hid_done, t.n * CH + m + 1)
                    ve.tensor_copy(hid_hi[:, m, 0:USED0], hid[m % 2][:, 0:USED0]).then_inc(hh_done, 1)
                    ve.wait_ge(hh_done, t.n * CH + m + 1)
                    ve.tensor_tensor(hid_lo[:, m, 0:USED0], hid[m % 2][:, 0:USED0], hid_hi[:, m, 0:USED0], ALU.subtract).then_inc(hl_done, 1)
                return part

            def bias(t):
                ve.wait_ge(b_ld, (t.n + 1) * 48)
                ve.tensor_tensor(b2ls[:], b2[t.p][:], ls[t.p][:], ALU.mult).then_inc(b2_done, 1)

            def rows(c):
                def part(t):
                    q = (t.p * ST + c) % 2
                    ve.wait_ge(y_ps, t.n * ST + c + 1)
                    n = used(c)
                    ve.tensor_tensor(ys[q][0:n], ps_y[q][0:n, 0:D], ls[t.p][0:n], ALU.mult).then_inc(ys_done, 1)
                    ve.wait_ge(ys_done, t.n * ST + c + 1)
                    if c == 0:
                        ve.wait_ge(b2_done, t.n + 1)
                    if t.p == 0:
                        wait(ve, y_st[q], t.h * ST * 16 + (c // 2) * 16)
                    else:
                        wait(ve, y_st[q], t.h * ST * 16 + ((ST + c) // 2) * 16)
                    ve.tensor_tensor(ys[q][0:n], ys[q][0:n], b2ls[0:n], ALU.add).then_inc(yt_done, 1)
                    ve.wait_ge(yt_done, t.n * ST + c + 1)
                    ve.tensor_tensor(yo[q][0:n], ys[q][0:n], xg[t.p][0:n, c, :], ALU.add).then_inc(yo_done, 1)
                return part

            pipelined(ve, [[(-1, pick)] + [(TURN_SLOTS[c], turned(c)) for c in range(ST)],
                           [(m / 2 + 0.1, hidden(m)) for m in range(CH)] + [(5.5, bias)] +
                           [(6.7 + c, rows(c)) for c in range(ST)]], E0)


def phase_heads(nc, env):
    a, x_res, consts, tri_bf, ones_bf, gate = (env[k] for k in ("a", "x_res", "consts", "tri_bf", "ones_bf", "gate"))
    w_own, slot_own, y0_d, rows_d, xn3_d = (env[k] for k in ("w_own", "slot_own", "y0_d", "rows_d", "xn3_d"))
    NC = HALVES * TOP0
    NR = HALVES * TOP1
    NG = HALVES * GROUPS
    ctx = ExitStack()
    with ctx:
        def sb(name, shape, dt):
            return ctx.enter_context(nc.sbuf_tensor("h_" + name, shape, dt))

        def two(name, shape, dt):
            return [sb(f"{name}{i}", shape, dt) for i in range(2)]

        def sem(name):
            env["sems"].append(nc.alloc_semaphore(name="h_" + name))
            return env["sems"][-1]

        ident = consts[:, K_ID:K_ID + P]
        wq, wk, wv, wo = (sb(n, [P, DC, D], F32) for n in ("wq", "wk", "wv", "wo"))
        bq, bk = sb("bq", [P, DC], F32), sb("bk", [P, DC], F32)
        bqs = sb("bqs", [P, DC], F32)
        bv, bo = sb("bv", [P, D], F32), sb("bo", [1, D], F32)
        ones_row = sb("ones_row", [1, P], F32)
        gate_w16, gate_w = sb("gate_w16", [P, DC, E1], BF16), sb("gate_w", [P, DC, E1], F32)
        gate_b = sb("gate_b", [P, E1], F32)
        ident_bf = sb("ident_bf", [P, P], BF16)
        causal_bf = sb("causal_bf", [P, HPB, CTX], BF16)
        eps = sb("eps", [P, 1], F32)
        tok_no = sb("tok_no", [P, TILES], F32)
        counts = two("counts", [P, E1], BF16)

        slots = two("slots", [P, NC], U32)
        wts = two("wts", [P, NC], F32)
        yg = two("yg", [P, NC, D], F32)
        ct = two("ct", [P, DC, CTX], F32)
        stats, mv = two("stats", [P, HALVES, 6], F32), two("mv", [P, HALVES, 2], F32)
        lnv, rstd, newton = (two(n, [P, HALVES], F32) for n in ("lnv", "rstd", "newton"))
        stats3, mv3 = two("stats3", [P, HALVES, 6], F32), two("mv3", [P, HALVES, 2], F32)
        lnv3, rstd3, newton3 = (two(n, [P, HALVES], F32) for n in ("lnv3", "rstd3", "newton3"))
        xn = two("xn", [P, HALVES, D], F32)
        x_t = two("x_t", [P, DC, SEQ], F32)
        qf = sb("qf", [P, DC, SEQ], F32)
        q_hi, q_lo = two("q_hi", [P, DC, SEQ], F32R), two("q_lo", [P, DC, SEQ], F32R)
        kf, k_hi, k_lo = (sb(n, [P, DC, CTX], d) for n, d in (("kf", F32), ("k_hi", F32R), ("k_lo", F32)))
        kd_hi, kd_lo = two("kd_hi", [P, DC, HPC, CTX], F32R), two("kd_lo", [P, DC, HPC, CTX], F32R)
        vm = two("vm", [CTX, HEADS, 2 * HD], F32)
        mx = two("mx", [P, HPB], F32)
        sums, rec = two("sums", [P, HALVES, HEADS], F32), two("rec", [P, HALVES, HEADS], F32)
        recx = sb("recx", [P, HALVES, HEADS, HD], F32)
        pr = two("pr", [P, HPB, CTX], F32)
        pt = sb("pt", [CTX, HEADS, SEQ], F32)
        o_sb, o_t = sb("o_sb", [P, DC, SEQ], F32), two("o_t", [P, DC, SEQ], F32)
        row = two("row", [P, HALVES, ROW], F32)
        x3_t = sb("x3_t", [P, DC, SEQ], F32)
        ex, sg, sel = (two(n, [P, HALVES, E1], F32) for n in ("ex", "sg", "sel"))
        top8, idx8 = two("top8", [P, HALVES, 8], F32), two("idx8", [P, HALVES, 8], U32)
        idf = two("idf", [P, HALVES, TOP1], F32)
        hot = two("hot", [P, NR, E1], F32)
        hot_any = two("hot_any", [P, HALVES, E1], BF16)
        own = sb("own", [P, NR, E1], F32)
        wk8, wsum, wrec = two("wk8", [P, NR], F32), two("wsum", [P, HALVES], F32), two("wrec", [P, HALVES], F32)
        csum = sb("csum", [P, E1], BF16)
        pfx = sb("pfx", [P, HALVES, E1], F32)
        pos, over = two("pos", [P, NR], F32), two("over", [P, NR], F32)
        dest = two("dest", [P, NR], U32)

        def bank(name):
            return ctx.enter_context(nc.psum_tensor("h_" + name, [P, 512], F32))

        ps_s = [bank(f"ps_s{i}") for i in range(3)]
        ps_p, ps_q, ps_kv, ps_o, ps_w = bank("ps_p"), bank("ps_q"), bank("ps_kv"), bank("ps_o"), bank("ps_w")

        names = ("par prep tokn yi_done mixed0 mixed st_done mv_done ln_done rs_done nw_done xn_done xt_ps xt_sb q_ps "
                 "qf_done qh_done ql_done kv_ps kf_done kh_done kl_done kdh_done kdl_done v_done s_ps mx_done "
                 "exp_done rec_done recx_done r_ps p_ps pt_done o_ps ot_done w_ps o_sb x_done st3_done mv3_done ln3_done "
                 "rs3_done nw3_done xn3_done x3t_ps x3t_sb lg_ps ex_done e1_done sg_done sel_done t8_done i8_done "
                 "idf_done hot_done any_done own_done wk_done ws_done wr_done wn_done cs_done cnt_done pf_ps pf_done "
                 "own2_done pos_done ov_done dest_done rowx_done zero").split()
        S = {n: sem(n) for n in names}
        loaded = [sem("loaded0"), sem("loaded1")]
        yin = [sem("yin0"), sem("yin1")]
        sent = [sem("sent0"), sem("sent1")]
        stored = [sem("stored0"), sem("stored1")]
        ROWX = 3

        def tiles(t):
            return x_res[:, bass.ds(t.n * HALVES, HALVES), :]

        block = ctx.enter_context(nc.Block())

        @block.sync
        def _(sp):
            for dst, src in ((wk[:], a["wk_t"]), (wv[:], a["wv_t"]), (wq[:], a["wq_t"]), (wo[:], a["wo_t"]),
                             (bq[:], a["bq"]), (bk[:], a["bk"]), (bv[:], a["bv"].partition_broadcast(P)),
                             (bo[:], a["bo"]), (gate_w16[:], a["gate_w"]),
                             (gate_b[:], a["gate_b"].partition_broadcast(P))):
                sp.dma_start(dst, src).then_inc(S["par"], 16)

            def load(t):
                wait_apart(sp, loaded[t.p], t.h * 16, gate)
                wait_apart(sp, S["kv_ps"], t.n - 1, gate)
                sp.dma_start(ct[t.p][:], a["ctx_t"][bass.ds(t.n, 1)].rearrange("a p k j -> (a p) k j")).then_inc(loaded[t.p], 16)

            def store(t):
                wait_apart(sp, stored[t.p], t.h * 16, gate)
                wait_apart(sp, S["xn3_done"], (t.n + 1) * HALVES, gate)
                sp.dma_start(xn3_d.rearrange("(t p) d -> p t d", p=P)[:, bass.ds(t.n * HALVES, HALVES), :],
                             row[t.p][:, :, 0:D]).then_inc(stored[t.p], 16)

            pipelined(sp, [[(0, load)],
                           [],
                           [],
                           [(1, store)]], BATCH)
            for q in range(2):
                sp.wait_ge(stored[q], BATCH // 2 * 16)

        @block.gpsimd
        def _(pool):
            pool.iota(tok_no[:], [[P, TILES]], base=0, channel_multiplier=1,
                      allow_small_or_imprecise_dtypes=True).then_inc(S["tokn"], 1)

            def gather(t):
                pool.wait_ge(S["yi_done"], (t.n + 1) * 2)
                wait(pool, S["mixed"], (t.n - 1) * NC)
                apart(pool, gate)
                for c in range(NC):
                    pool.indirect_dma_start(yg[t.p][:, c, :], None, y0_d,
                                            bass.IndirectOffsetOnAxis(ap=slots[t.p][:, c:c + 1], axis=0)
                                            ).then_inc(yin[t.p], 16)

            def split_k(t):
                pool.wait_ge(S["kf_done"], (t.n + 1) * DC)
                pool.wait_ge(S["kh_done"], (t.n + 1) * DC)
                wait(pool, S["kdl_done"], t.n * DC)
                pool.tensor_tensor(k_lo[:], kf[:], k_hi[:], ALU.subtract).then_inc(S["kl_done"], 1)

            def spread_k(t):
                pool.wait_ge(S["kl_done"], t.n + 1)
                wait(pool, S["s_ps"], (t.n - 1) * NG)
                for c in range(DC):
                    pool.tensor_tensor(kd_lo[t.p][:, c], k_lo[:, c, :].unsqueeze(1).to_broadcast([P, HPC, CTX]),
                                       consts[:, K_HEAD:K_HEAD + HPC].unsqueeze(2).to_broadcast([P, HPC, CTX]),
                                       ALU.mult).then_inc(S["kdl_done"], 1)

            def split_q(t):
                pool.wait_ge(S["qf_done"], (t.n + 1) * DC)
                pool.wait_ge(S["qh_done"], (t.n + 1) * DC)
                wait(pool, S["s_ps"], (t.n - 1) * NG)
                pool.tensor_tensor(q_lo[t.p][:], qf[:], q_hi[t.p][:], ALU.subtract).then_inc(S["ql_done"], 1)

            def scatter(t):
                pool.wait_ge(S["dest_done"], t.n + 1)
                pool.wait_ge(S["rowx_done"], (t.n + 1) * ROWX)
                pool.wait_ge(S["xn3_done"], (t.n + 1) * HALVES)
                apart(pool, gate)
                for n in range(NR):
                    pool.indirect_dma_start(rows_d, bass.IndirectOffsetOnAxis(ap=dest[t.p][:, n:n + 1], axis=0),
                                            row[t.p][:, n // TOP1, :], None, bounds_check=SLOTS1 - 1,
                                            oob_is_err=False).then_inc(sent[t.p], 16)

            pipelined(pool, [[(3, gather)],
                             [(0, split_k), (1, spread_k), (4, split_q)],
                             [],
                             [],
                             [],
                             [(2, scatter)]], BATCH)
            for q in range(2):
                pool.wait_ge(sent[q], BATCH // 2 * NR * 16)

        @block.tensor
        def _(pe):
            pe.wait_ge(S["par"], 10 * 16)
            pe.wait_ge(S["prep"], 1)

            def keys_values(t):
                pe.wait_ge(loaded[t.p], (t.h + 1) * 16)
                wait(pe, S["ot_done"], t.n - 2)
                wait(pe, S["kf_done"], t.n * DC)
                wait(pe, S["kh_done"], t.n * DC)
                wait(pe, S["v_done"], t.n * 2)
                for o in range(DC):
                    for k in range(DC):
                        pe.matmul(ps_kv[:, o * CTX:(o + 1) * CTX], wk[:, k, o * P:(o + 1) * P], ct[t.p][:, k, :],
                                  start=k == 0, stop=k == DC - 1)
                for k in range(DC):
                    mm = pe.matmul(ps_kv[0:CTX, D:2 * D], ct[t.p][:, k, :], wv[:, k, :], start=k == 0, stop=k == DC - 1)
                mm.then_inc(S["kv_ps"], 1)

            def turn_x(t):
                pe.wait_ge(S["xn_done"], (t.n + 1) * HALVES)
                wait(pe, S["qh_done"], t.n * DC)
                wait(pe, S["qf_done"], t.n * DC)
                for s in range(HALVES):
                    for k in range(DC):
                        mm = pe.transpose(ps_q[:, k * SEQ + s * P:k * SEQ + (s + 1) * P], xn[t.p][:, s, k * P:(k + 1) * P], ident)
                mm.then_inc(S["xt_ps"], 1)

            def queries(t):
                pe.wait_ge(S["xt_sb"], t.n + 1)
                for o in range(DC):
                    for k in range(DC):
                        mm = pe.matmul(ps_q[:, o * SEQ:(o + 1) * SEQ], wq[:, k, o * P:(o + 1) * P], x_t[t.p][:, k, :],
                                       start=k == 0, stop=k == DC - 1)
                mm.then_inc(S["q_ps"], 1)

            def scores(n):
                def part(t):
                    s, g = n // GROUPS, n % GROUPS
                    c, h = g * HPB // HPC, g * HPB % HPC
                    if n == 0:
                        pe.wait_ge(S["qh_done"], (t.n + 1) * DC)
                        pe.wait_ge(S["ql_done"], t.n + 1)
                        pe.wait_ge(S["kdh_done"], (t.n + 1) * DC)
                        pe.wait_ge(S["kdl_done"], (t.n + 1) * DC)
                    before = n - 3 if n >= 3 else max(m for m in range(NG) if m % 3 == n) - NG
                    wait(pe, S["exp_done"], (t.n * NG + before + 1) * HPB)
                    i = 0
                    terms = ((q_hi, kd_hi), (q_hi, kd_lo), (q_lo, kd_hi))
                    for l, r in terms:
                        mm = pe.matmul(ps_s[n % 3][:, 0:HPB * CTX], l[t.p][:, c, s * P:(s + 1) * P],
                                       r[t.p][:, c, h:h + HPB, :].rearrange("p h j -> p (h j)"),
                                       start=i == 0, stop=s > 0 and i == len(terms) - 1)
                        i += 1
                    if s == 0:
                        mm = pe.matmul(ps_s[n % 3][:, 0:HPB * CTX], ident_bf[:], causal_bf[:].rearrange("p h j -> p (h j)"),
                                       start=False, stop=True)
                    mm.then_inc(S["s_ps"], 1)
                return part

            def turn(n):
                def part(t):
                    pe.wait_ge(S["exp_done"], (t.n * NG + n + 1) * HPB)
                    wait(pe, S["pt_done"], t.n * NG + n)
                    for h in range(HPB):
                        mm = pe.transpose(ps_p[0:CTX, h * P:(h + 1) * P], pr[n % 2][:, h, :], ident)
                    mm.then_inc(S["p_ps"], 1)
                return part

            def attend(t):
                pe.wait_ge(S["pt_done"], (t.n + 1) * NG)
                pe.wait_ge(S["v_done"], (t.n + 1) * 2)
                wait(pe, S["o_sb"], t.n)
                for c in range(DC):
                    for odd in range(2):
                        for j in range(HPC // 2):
                            h = c * HPC + 2 * j + odd
                            mm = pe.matmul(ps_o[32 * j:32 * (j + 1), c * SEQ:(c + 1) * SEQ], vm[t.p][:, h, :], pt[:, h, :],
                                           start=odd == 0, stop=odd == 1, tile_position=(0, 32 * j),
                                           skip_group_check=True)
                mm.then_inc(S["o_ps"], 1)

            def inverse_sums(t):
                pe.wait_ge(S["recx_done"], t.n + 1)
                later = min(t.n + 3, BATCH) if isinstance(t.n, int) else t.n + 3
                wait(pe, S["kf_done"], later * DC)
                wait(pe, S["kh_done"], later * DC)
                wait(pe, S["v_done"], later * 2)
                for s in range(HALVES):
                    for c in range(DC):
                        mm = pe.transpose(ps_kv[:, c * SEQ + s * P:c * SEQ + (s + 1) * P],
                                          recx[:, s, c * HPC:(c + 1) * HPC, :].rearrange("p h x -> p (h x)"), ident)
                mm.then_inc(S["r_ps"], 1)

            def project(t):
                pe.wait_ge(S["ot_done"], t.n + 1)
                wait(pe, S["ex_done"], t.n)
                for s in range(HALVES):
                    for c in range(DC):
                        pe.matmul(ps_w[:, s * D:(s + 1) * D], o_t[t.p][:, c, s * P:(s + 1) * P], wo[:, c, :],
                                  start=c == 0, stop=False)
                    mm = pe.matmul(ps_w[:, s * D:(s + 1) * D], ones_row[:], bo[:], start=False, stop=True)
                mm.then_inc(S["w_ps"], 1)

            def turn_x3(t):
                pe.wait_ge(S["xn3_done"], (t.n + 1) * HALVES)
                wait(pe, S["pf_done"], t.n)
                pe.wait_ge(S["x_done"], t.n + 1)
                for s in range(HALVES):
                    for k in range(DC):
                        mm = pe.transpose(ps_w[:, k * SEQ + s * P:k * SEQ + (s + 1) * P], row[t.p][:, s, k * P:(k + 1) * P], ident)
                mm.then_inc(S["x3t_ps"], 1)

            def gates(t):
                pe.wait_ge(S["x3t_sb"], t.n + 1)
                for s in range(HALVES):
                    for k in range(DC):
                        mm = pe.matmul(ps_w[:, s * E1:(s + 1) * E1], x3_t[:, k, s * P:(s + 1) * P], gate_w[:, k, :],
                                       start=k == 0, stop=k == DC - 1)
                mm.then_inc(S["lg_ps"], 1)

            def prefix(t):
                pe.wait_ge(S["any_done"], t.n + 1)
                wait(pe, S["cnt_done"], t.n)
                pe.wait_ge(S["ex_done"], t.n + 1)
                wait(pe, S["x_done"], min(t.n + 2, BATCH) if isinstance(t.n, int) else t.n + 2)
                for s in range(HALVES):
                    out = ps_w[:, s * E1:(s + 1) * E1]
                    pe.matmul(out, tri_bf[:], hot_any[t.p][:, s, :], start=True, stop=False)
                    if s:
                        pe.matmul(out, ones_bf[:], hot_any[t.p][:, 0, :], start=False, stop=False)
                    mm = pe.matmul(out, ones_bf[:], counts[t.p][:], start=False, stop=True)
                mm.then_inc(S["pf_ps"], 1)

            pipelined(pe, [[],
                           [(0, keys_values), (17, turn_x), (21, queries)],
                           placed(scores, (2, 4, 8, 9, 11, 13, 18, 19)) + placed(turn, (7, 10, 14, 16, 20, 22, 24)),
                           [(3, turn(NG - 1)), (6, attend), (12, inverse_sums), (15, project)],
                           [(1, turn_x3), (5, gates), (23, prefix)]], BATCH)

        @block.scalar
        def _(act):
            act.preload_act_table_set("natural_log_exp_and_others")
            act.wait_ge(S["par"], 10 * 16)
            act.wait_ge(S["prep"], 2)

            def root(t, m, lv, r, m_s, l_s, r_s, nw_s):
                wait(act, S[m_s], (t.n + 1) * HALVES)
                wait(act, S[nw_s], (t.n - 1) * 3)
                act.activation(lv[t.p][:], m[t.p][:, :, 1], ACT.Ln, bias=eps[:]).then_inc(S[l_s], 1)
                wait(act, S[l_s], t.n + 1)
                act.activation(r[t.p][:], lv[t.p][:], ACT.Exp, scale=-0.5).then_inc(S[r_s], 1)

            def keys(t):
                act.wait_ge(S["kv_ps"], t.n + 1)
                wait(act, S["kl_done"], t.n)
                wait(act, S["kdh_done"], t.n * DC)
                for o in range(DC):
                    act.activation(kf[:, o, :], ps_kv[:, o * CTX:(o + 1) * CTX], ACT.Identity, bias=bk[:, o:o + 1]
                                   ).then_inc(S["kf_done"], 1)
                    act.activation(k_hi[:, o, :], ps_kv[:, o * CTX:(o + 1) * CTX], ACT.Identity, bias=bk[:, o:o + 1]
                                   ).then_inc(S["kh_done"], 1)

            def root1(t):
                root(t, mv, lnv, rstd, "mv_done", "ln_done", "rs_done", "nw_done")

            def turned(t):
                act.wait_ge(S["xt_ps"], t.n + 1)
                wait(act, S["q_ps"], t.n - 1)
                act.activation(x_t[t.p][:], ps_q[:].rearrange("p (k i) -> p k i", k=DC), ACT.Copy).then_inc(S["xt_sb"], 1)

            def queries(t):
                act.wait_ge(S["q_ps"], t.n + 1)
                wait(act, S["ql_done"], t.n)
                wait(act, S["s_ps"], (t.n - 1) * NG)
                for o in range(DC):
                    act.activation(q_hi[t.p][:, o, :], ps_q[:, o * SEQ:(o + 1) * SEQ], ACT.Identity, bias=bqs[:, o:o + 1],
                                   scale=SCALE).then_inc(S["qh_done"], 1)
                    act.activation(qf[:, o, :], ps_q[:, o * SEQ:(o + 1) * SEQ], ACT.Identity, bias=bqs[:, o:o + 1],
                                   scale=SCALE).then_inc(S["qf_done"], 1)

            def exps(n):
                def part(t):
                    act.wait_ge(S["mx_done"], t.n * NG + n + 1)
                    wait(act, S["p_ps"], t.n * NG + n - 1)
                    s, g = n // GROUPS, n % GROUPS
                    if n == 0:
                        wait(act, S["rec_done"], t.n - 1)
                    for h in range(HPB):
                        act.activation(pr[n % 2][:, h, :], ps_s[n % 3][:, h * CTX:(h + 1) * CTX], ACT.Exp,
                                       bias=mx[n % 2][:, h:h + 1], accum_out=sums[t.p][:, s, g * HPB + h:g * HPB + h + 1]).then_inc(S["exp_done"], 1)
                return part

            def keep(n):
                def part(t):
                    s, g = n // GROUPS, n % GROUPS
                    act.wait_ge(S["p_ps"], t.n * NG + n + 1)
                    if n == 0:
                        wait(act, S["o_ps"], t.n)
                    act.activation(pt[:, g * HPB:(g + 1) * HPB, s * P:(s + 1) * P],
                                   ps_p[0:CTX, :].rearrange("p (h i) -> p h i", h=HPB), ACT.Copy).then_inc(S["pt_done"], 1)
                return part

            def attended(t):
                act.wait_ge(S["o_ps"], t.n + 1)
                wait(act, S["ot_done"], t.n)
                act.activation(o_sb[:], ps_o[:].rearrange("p (k i) -> p k i", k=DC), ACT.Copy).then_inc(S["o_sb"], 1)

            def root3(t):
                root(t, mv3, lnv3, rstd3, "mv3_done", "ln3_done", "rs3_done", "nw3_done")

            def turned_x3(t):
                act.wait_ge(S["x3t_ps"], t.n + 1)
                wait(act, S["lg_ps"], t.n)
                act.activation(x3_t[:], ps_w[:].rearrange("p (k i) -> p k i", k=DC), ACT.Copy).then_inc(S["x3t_sb"], 1)

            def gates(t):
                act.wait_ge(S["lg_ps"], t.n + 1)
                wait(act, S["e1_done"], t.n - 1)
                act.activation(ex[t.p][:].rearrange("p s e -> p (s e)"), ps_w[:, 0:HALVES * E1], ACT.Exp, scale=-1.0
                               ).then_inc(S["ex_done"], 1)

            pipelined(act, [[],
                            [(0, keys), (8, root1), (15, turned), (21, queries)],
                            placed(exps, (3, 4, 9, 11, 13, 16, 19, 22)) + placed(keep, (7, 10, 12, 14, 17, 20, 23)),
                            [(2, keep(NG - 1)), (6, attended), (18, root3)],
                            [(1, turned_x3), (5, gates)]], BATCH)

        @block.vector
        def _(ve):
            def pick(t):
                wait(ve, yin[t.p], t.h * NC * 16)
                wait(ve, S["mixed"], (t.n - 1) * NC)
                own_tiles = bass.ds(t.n * HALVES, HALVES)
                ve.tensor_copy(slots[t.p][:].rearrange("p (s k) -> p s k", k=TOP0), slot_own[:, own_tiles, :]).then_inc(S["yi_done"], 1)
                ve.tensor_copy(wts[t.p][:].rearrange("p (s k) -> p s k", k=TOP0), w_own[:, own_tiles, :]).then_inc(S["yi_done"], 1)

            pick(At(0, 0, 0))
            ve.memset(eps[:], LN_EPS).then_inc(S["zero"], 1)
            ve.memset(ones_row[:], 1.0).then_inc(S["zero"], 1)
            for i in range(2):
                ve.memset(vm[i][:], 0.0).then_inc(S["zero"], 1)
                ve.memset(counts[i][:], 0.0).then_inc(S["zero"], 1)
                ve.memset(row[i][:], 0.0).then_inc(S["zero"], 1)
            ve.tensor_copy(ident_bf[:], ident).then_inc(S["zero"], 1)
            ve.tensor_copy(causal_bf[:], consts[:, K_CAUSAL:K_CAUSAL + CTX].unsqueeze(1).to_broadcast([P, HPB, CTX])).then_inc(S["zero"], 1)
            ve.wait_ge(S["par"], 10 * 16)
            ve.wait_ge(S["zero"], 10)
            ve.wait_ge(S["tokn"], 1)
            ve.tensor_copy(gate_w[:], gate_w16[:]).then_inc(S["prep"], 1)
            ve.tensor_scalar(bqs[:], bq[:], SCALE, None, ALU.mult).then_inc(S["prep"], 1)

            def moments(t, src, st, st_s):
                apart(ve, gate)
                for s in range(HALVES):
                    ve.bn_stats(st[t.p][:, s, :], src[:, s, :]).then_inc(S[st_s], 1)

            def variance(t, st, m, st_s, m_s):
                wait(ve, S[st_s], (t.n + 1) * HALVES)
                apart(ve, gate)
                for s in range(HALVES):
                    ve.bn_aggr(m[t.p][:, s, :], st[t.p][:, s, :]).then_inc(S[m_s], 1)

            def newton_a(t, m, r, nw, r_s, nw_s):
                wait(ve, S[r_s], t.n + 1)
                ve.scalar_tensor_tensor(nw[t.p][:], m[t.p][:, :, 1], LN_EPS, r[t.p][:], ALU.add, ALU.mult).then_inc(S[nw_s], 1)

            def newton_b(t, r, nw, nw_s):
                wait(ve, S[nw_s], t.n * 3 + 1)
                ve.scalar_tensor_tensor(nw[t.p][:], nw[t.p][:], -0.5, r[t.p][:], ALU.mult, ALU.mult).then_inc(S[nw_s], 1)

            def newton_c(t, r, nw, nw_s):
                wait(ve, S[nw_s], t.n * 3 + 2)
                ve.scalar_tensor_tensor(nw[t.p][:], nw[t.p][:], 1.5, r[t.p][:], ALU.add, ALU.mult).then_inc(S[nw_s], 1)

            def normed(t, src, m, nw, dst, nw_s, dst_s):
                wait(ve, S[nw_s], t.n * 3 + 3)
                for s in range(HALVES):
                    ve.tensor_scalar(dst[t.p][:, s, 0:D], src[:, s, :], m[t.p][:, s, 0:1], nw[t.p][:, s:s + 1],
                                     ALU.subtract, ALU.mult).then_inc(S[dst_s], 1)

            def first_norm(t):
                moments(t, tiles(t), stats, "st_done")

            def first_norm_var(t):
                variance(t, stats, mv, "st_done", "mv_done")

            def first_norm_a(t):
                newton_a(t, mv, rstd, newton, "rs_done", "nw_done")

            def first_norm_b(t):
                newton_b(t, rstd, newton, "nw_done")

            def first_norm_c(t):
                newton_c(t, rstd, newton, "nw_done")

            def first_normed(t):
                wait(ve, S["xt_ps"], t.n - 1)
                normed(t, tiles(t), mv, newton, xn, "nw_done", "xn_done")

            def second_norm(t):
                ve.wait_ge(S["x_done"], t.n + 1)
                moments(t, tiles(t), stats3, "st3_done")

            def second_norm_var(t):
                variance(t, stats3, mv3, "st3_done", "mv3_done")

            def second_norm_a(t):
                newton_a(t, mv3, rstd3, newton3, "rs3_done", "nw3_done")

            def second_norm_b(t):
                newton_b(t, rstd3, newton3, "nw3_done")

            def second_norm_c(t):
                newton_c(t, rstd3, newton3, "nw3_done")

            def second_normed(t):
                wait(ve, S["x3t_ps"], t.n - 1)
                wait(ve, stored[t.p], t.h * 16)
                wait(ve, sent[t.p], t.h * NR * 16)
                normed(t, tiles(t), mv3, newton3, row, "nw3_done", "xn3_done")

            def pick_later(t):
                if not isinstance(t.n, int) or t.n > 0:
                    pick(t)

            def mix(k):
                def part(t):
                    ve.wait_ge(yin[t.p], (t.h + 1) * NC * 16)
                    ve.wait_ge(S["yi_done"], (t.n + 1) * 2)
                    wait(ve, S["mixed"], t.n * NC + k * HALVES)
                    for s in range(HALVES):
                        c = s * TOP0 + k
                        xt = x_res[:, bass.ds(t.n * HALVES + s, 1), :].rearrange("p a d -> p (a d)")
                        ve.scalar_tensor_tensor(xt, yg[t.p][:, c, :], wts[t.p][:, c:c + 1], xt, ALU.mult, ALU.add
                                                ).then_inc(S["mixed"], 1)
                return part

            def mix_done(t):
                ve.wait_ge(S["mixed"], (t.n + 1) * NC)
                first_norm(t)

            def values(t):
                ve.wait_ge(S["kf_done"], (t.n + 1) * DC)
                ve.wait_ge(S["kh_done"], (t.n + 1) * DC)
                wait(ve, S["o_ps"], t.n - 1)
                for odd in range(2):
                    ve.tensor_tensor(vm[t.p][:, odd::2, odd * HD:(odd + 1) * HD],
                                     ps_kv[0:CTX, D:2 * D].rearrange("p (h x) -> p h x", x=HD)[:, odd::2, :],
                                     bv[0:CTX, :].rearrange("p (h x) -> p h x", x=HD)[:, odd::2, :], ALU.add
                                     ).then_inc(S["v_done"], 1)

            def spread_k(c):
                def part(t):
                    ve.wait_ge(S["kh_done"], (t.n + 1) * DC)
                    wait(ve, S["s_ps"], (t.n - 1) * NG)
                    ve.tensor_tensor(kd_hi[t.p][:, c], k_hi[:, c, :].unsqueeze(1).to_broadcast([P, HPC, CTX]),
                                     consts[:, K_HEAD:K_HEAD + HPC].unsqueeze(2).to_broadcast([P, HPC, CTX]),
                                     ALU.mult).then_inc(S["kdh_done"], 1)
                return part

            def peaks(n):
                def part(t):
                    ve.wait_ge(S["s_ps"], t.n * NG + n + 1)
                    wait(ve, S["exp_done"], (t.n * NG + n - 1) * HPB)
                    ve.tensor_reduce(mx[n % 2][:], ps_s[n % 3][:, 0:HPB * CTX].rearrange("p (h j) -> p h j", h=HPB), AX.X, ALU.max,
                                     negate=True).then_inc(S["mx_done"], 1)
                return part

            def inverse(t):
                ve.wait_ge(S["exp_done"], (t.n + 1) * NG * HPB)
                ve.reciprocal(rec[t.p][:], sums[t.p][:]).then_inc(S["rec_done"], 1)

            def inverse_spread(t):
                ve.wait_ge(S["rec_done"], t.n + 1)
                wait(ve, S["r_ps"], t.n)
                ve.tensor_copy(recx[:], rec[t.p][:].unsqueeze(3).to_broadcast([P, HALVES, HEADS, HD])).then_inc(S["recx_done"], 1)

            def attended(t):
                ve.wait_ge(S["o_sb"], t.n + 1)
                ve.wait_ge(S["r_ps"], t.n + 1)
                wait(ve, S["w_ps"], t.n - 1)
                ve.tensor_tensor(o_t[t.p][:], ps_kv[:].rearrange("p (k i) -> p k i", k=DC), o_sb[:], ALU.mult
                                 ).then_inc(S["ot_done"], 1)

            def add(t):
                ve.wait_ge(S["w_ps"], t.n + 1)
                ve.tensor_tensor(tiles(t), ps_w[:].rearrange("p (s d) -> p s d", s=HALVES), tiles(t), ALU.add
                                 ).then_inc(S["x_done"], 1)

            def gates(t):
                ve.wait_ge(S["ex_done"], t.n + 1)
                ve.tensor_scalar(ex[t.p][:], ex[t.p][:], 1.0, None, ALU.add).then_inc(S["e1_done"], 1)

            def gate_score(t):
                ve.wait_ge(S["e1_done"], t.n + 1)
                ve.reciprocal(sg[t.p][:], ex[t.p][:]).then_inc(S["sg_done"], 1)

            def biased(t):
                ve.wait_ge(S["sg_done"], t.n + 1)
                ve.tensor_tensor(sel[t.p][:], sg[t.p][:], gate_b[:].unsqueeze(1).to_broadcast([P, HALVES, E1]), ALU.add
                                 ).then_inc(S["sel_done"], 1)

            def largest(t):
                ve.wait_ge(S["sel_done"], t.n + 1)
                apart(ve, gate)
                for s in range(HALVES):
                    ve.max(top8[t.p][:, s, :], sel[t.p][:, s, :]).then_inc(S["t8_done"], 1)

            def places(t):
                ve.wait_ge(S["t8_done"], (t.n + 1) * HALVES)
                apart(ve, gate)
                for s in range(HALVES):
                    ve.max_index(idx8[t.p][:, s, :], top8[t.p][:, s, :], sel[t.p][:, s, :]).then_inc(S["i8_done"], 1)

            def experts(t):
                ve.wait_ge(S["i8_done"], (t.n + 1) * HALVES)
                ve.tensor_copy(idf[t.p][:], idx8[t.p][:, :, 0:TOP1]).then_inc(S["idf_done"], 1)

            def one_hot(t):
                ve.wait_ge(S["idf_done"], t.n + 1)
                ve.tensor_tensor(hot[t.p][:], idf[t.p][:].rearrange("p s k -> p (s k)").unsqueeze(2).to_broadcast([P, NR, E1]),
                                 consts[:, K_IOTA:K_IOTA + E1].unsqueeze(1).to_broadcast([P, NR, E1]), ALU.is_equal
                                 ).then_inc(S["hot_done"], 1)

            def any_hot(t):
                ve.wait_ge(S["hot_done"], t.n + 1)
                wait(ve, S["pf_ps"], t.n - 1)
                with nc.allow_low_precision(reason="sums of zeros and at most one 1"):
                    ve.tensor_reduce(hot_any[t.p][:], hot[t.p][:].rearrange("p (s k) e -> p s e k", k=TOP1), AX.X,
                                     ALU.add).then_inc(S["any_done"], 1)

            def own_scores(t):
                ve.wait_ge(S["hot_done"], t.n + 1)
                wait(ve, S["pos_done"], t.n)
                for s in range(HALVES):
                    k = slice(s * TOP1, (s + 1) * TOP1)
                    ve.tensor_tensor(own[:, k, :], hot[t.p][:, k, :],
                                     sg[t.p][:, s:s + 1, :].to_broadcast([P, TOP1, E1]), ALU.mult).then_inc(S["own_done"], 1)

            def chosen(t):
                ve.wait_ge(S["own_done"], (t.n + 1) * HALVES)
                ve.tensor_reduce(wk8[t.p][:], own[:], AX.X, ALU.add).then_inc(S["wk_done"], 1)

            def chosen_sum(t):
                ve.wait_ge(S["wk_done"], t.n + 1)
                ve.tensor_reduce(wsum[t.p][:], wk8[t.p][:].rearrange("p (s k) -> p s k", k=TOP1), AX.X, ALU.add
                                 ).then_inc(S["ws_done"], 1)

            def sum_guard(t):
                ve.wait_ge(S["ws_done"], t.n * 2 + 1)
                ve.tensor_scalar(wsum[t.p][:], wsum[t.p][:], 1e-12, None, ALU.max).then_inc(S["ws_done"], 1)

            def sum_inverse(t):
                ve.wait_ge(S["ws_done"], t.n * 2 + 2)
                ve.reciprocal(wrec[t.p][:], wsum[t.p][:]).then_inc(S["wr_done"], 1)

            def row_tail(t):
                ve.wait_ge(S["wr_done"], t.n + 1)
                ve.tensor_tensor(row[t.p][:, :, C_W:C_W + TOP1], wk8[t.p][:].rearrange("p (s k) -> p s k", k=TOP1),
                                 wrec[t.p][:].unsqueeze(2).to_broadcast([P, HALVES, TOP1]), ALU.mult).then_inc(S["rowx_done"], 1)
                ve.tensor_copy(row[t.p][:, :, C_E:C_E + TOP1], idf[t.p][:]).then_inc(S["rowx_done"], 1)
                ve.tensor_copy(row[t.p][:, :, C_TOK:C_TOK + 1], tok_no[:, bass.ds(t.n * HALVES, HALVES)].unsqueeze(2)
                               ).then_inc(S["rowx_done"], 1)

            def prefix(t):
                ve.wait_ge(S["pf_ps"], t.n + 1)
                wait(ve, S["pos_done"], t.n)
                ve.tensor_copy(pfx[:], ps_w[:, 0:HALVES * E1].rearrange("p (s e) -> p s e", s=HALVES)).then_inc(S["pf_done"], 1)

            def count_a(t):
                ve.wait_ge(S["any_done"], t.n + 1)
                wait(ve, S["cnt_done"], t.n)
                ve.tensor_tensor(csum[:], counts[t.p][:], hot_any[t.p][:, 0, :], ALU.add).then_inc(S["cs_done"], 1)

            def count_b(t):
                ve.wait_ge(S["cs_done"], t.n + 1)
                ve.tensor_tensor(counts[1 - t.p][:], csum[:], hot_any[t.p][:, 1, :], ALU.add).then_inc(S["cnt_done"], 1)

            def own_prefix(t):
                ve.wait_ge(S["pf_done"], t.n + 1)
                ve.wait_ge(S["wk_done"], t.n + 1)
                for s in range(HALVES):
                    k = slice(s * TOP1, (s + 1) * TOP1)
                    ve.tensor_tensor(own[:, k, :], hot[t.p][:, k, :],
                                     pfx[:, s:s + 1, :].to_broadcast([P, TOP1, E1]), ALU.mult).then_inc(S["own2_done"], 1)

            def position(t):
                ve.wait_ge(S["own2_done"], (t.n + 1) * HALVES)
                ve.tensor_reduce(pos[t.p][:], own[:], AX.X, ALU.add).then_inc(S["pos_done"], 1)

            def past_end(t):
                ve.wait_ge(S["pos_done"], t.n + 1)
                ve.tensor_scalar(over[t.p][:], pos[t.p][:], float(CAP1), float(DROPPED), ALU.is_ge, ALU.mult).then_inc(S["ov_done"], 1)

            def past_end_far(t):
                ve.wait_ge(S["ov_done"], t.n * 2 + 1)
                ve.tensor_tensor(over[t.p][:], over[t.p][:], pos[t.p][:], ALU.add).then_inc(S["ov_done"], 1)

            def slot(t):
                ve.wait_ge(S["ov_done"], t.n * 2 + 2)
                wait(ve, sent[t.p], t.h * NR * 16)
                ve.scalar_tensor_tensor(dest[t.p][:], idf[t.p][:].rearrange("p s k -> p (s k)"), float(CAP1), over[t.p][:],
                                        ALU.mult, ALU.add).then_inc(S["dest_done"], 1)

            pipelined(ve, [[(23, pick_later)],
                           [(2, mix(0)), (7, mix(1)), (10, mix_done), (12, first_norm_var), (15, values), (18, first_norm_a),
                            (19, first_norm_b), (24, first_norm_c), (27, first_normed), (39, spread_k(0)), (51, spread_k(1))],
                           placed(peaks, (3, 6, 14, 16, 22, 29, 36, 42)),
                           [(8, inverse), (11, inverse_spread), (21, attended), (31, add), (33, second_norm),
                            (35, second_norm_var), (41, second_norm_a), (44, second_norm_b), (46, second_norm_c),
                            (49, second_normed)],
                           [(17, gates), (20, gate_score), (25, biased), (26, largest), (28, places), (30, experts),
                            (32, one_hot), (34, any_hot), (37, own_scores), (38, count_a), (40, chosen), (43, prefix),
                            (45, chosen_sum), (47, sum_guard), (48, count_b), (50, sum_inverse)],
                           [(0, own_prefix), (1, row_tail), (4, position), (5, past_end), (9, past_end_far), (13, slot)]], BATCH)


def phase_moe(nc, env):
    a, x_res, consts, gate, rows_d, xn3_d, sums_d, out = (env[k] for k in (
        "a", "x_res", "consts", "gate", "rows_d", "xn3_d", "sums_d", "out"))
    W_UP = 2 * DC * INNER
    ctx = ExitStack()
    with ctx:
        def sb(name, shape, dt):
            return ctx.enter_context(nc.sbuf_tensor("m_" + name, shape, dt))

        def two(name, shape, dt):
            return [sb(f"{name}{i}", shape, dt) for i in range(2)]

        def sem(name):
            env["sems"].append(nc.alloc_semaphore(name="m_" + name))
            return env["sems"][-1]

        ident = consts[:, K_ID:K_ID + P]
        sw16 = sb("sw16", [P, W_UP + D], BF16)
        sw = sb("sw", [P, W_UP + D], F32R)
        w16 = two("w16", [P, W_UP + D], BF16)
        w = two("w", [P, W_UP + D], F32R)
        xr = two("xr", [P, HALVES, ROW], F32)
        xn3 = sb("xn3", [P, TILES, D], F32)
        x_hi, x_lo = two("x_hi", [P, DC, SEQ], F32R), two("x_lo", [P, DC, SEQ], F32R)
        s1, hid = two("s1", [P, SEQ], F32), two("hid", [P, SEQ], F32)
        h_hi, h_lo = two("h_hi", [P, SEQ], F32R), two("h_lo", [P, SEQ], F32R)
        yo = two("yo", [P, HALVES, D], F32)
        wsel, wrow = two("wsel", [P, HALVES, TOP1], F32), two("wrow", [P, HALVES], F32)
        row_tok, tok = two("row_tok", [P, HALVES], F32), two("tok", [P, HALVES], U32)
        part0, part1 = two("part0", [P, HALVES, D], F32), two("part1", [P, HALVES, D], F32)
        routed, ysum = two("routed", [P, HALVES, D], F32), two("ysum", [P, HALVES, D], F32)

        def banks(name):
            return [ctx.enter_context(nc.psum_tensor(f"m_{name}{i}", [P, 512], F32)) for i in range(2)]

        ps_t, ps_1, ps_3, ps_y = banks("ps_t"), banks("ps_1"), banks("ps_3"), banks("ps_y")
        names = ("sw_ld sw_done xn3_ld tokens parts0 parts1 routed ysum w_ld0 w_ld1 w_done wd_done row_tok x_ld0 x_ld1 tok_done wsel_done wrow_done t_ps xh_done "
                 "xl_done up_ps s1_done hid_done hh_done hl_done y_ps yo_done st0 st1 added0 added1").split()
        S = {n: sem(n) for n in names}
        w_ld, x_ld, st, added, parts = ([S[f"{n}{i}"] for i in range(2)] for n in ("w_ld", "x_ld", "st", "added", "parts"))
        ADDS = E1 // 2 * SLOT_TILES1 * 16

        def loops(eng, experts, shared):
            pipelined(eng, experts, E1)
            pipelined(eng, shared, BATCH, E1)

        block = ctx.enter_context(nc.Block())

        @block.sync
        def _(sp):

            def load_slots(t):
                wait_apart(sp, x_ld[t.p], t.h * 16, gate)
                wait_apart(sp, S["t_ps"], t.n - 1, gate)
                wait_apart(sp, S["wsel_done"], t.n - 1, gate)
                wait_apart(sp, S["row_tok"], t.n - 1, gate)
                sp.dma_start(xr[t.p][:], rows_d.rearrange("(t p) d -> p t d", p=P)[:, bass.ds(t.n * SLOT_TILES1, SLOT_TILES1), :]
                             ).then_inc(x_ld[t.p], 16)
                wait_apart(sp, w_ld[t.p], t.h * 16, gate)
                wait_apart(sp, S["w_done"], t.n - 1, gate)
                wait_apart(sp, S["wd_done"], t.n - 1, gate)
                sp.dma_start(w16[t.p][:], a["moe_w"][bass.ds(t.n, 1)].rearrange("e p n -> (e p) n")).then_inc(w_ld[t.p], 16)

            def batch_rows(t):
                return bass.ds((t.n - E1) * HALVES, HALVES)

            def load_parts(t):
                if isinstance(t.n, int) and t.n == E1:
                    for q in range(2):
                        sp.wait_ge(added[q], ADDS)
                wait_apart(sp, S["routed"], t.n - E1 - 1, gate)
                wait_apart(sp, parts[t.p], (t.h - E1 // 2) * 32, gate)
                for part, sums in zip((part0, part1), sums_d):
                    sp.dma_start(part[t.p][:], sums[0:TOKENS, :].rearrange("(t p) d -> p t d", p=P)[:, batch_rows(t), :]
                                 ).then_inc(parts[t.p], 16)

            def store(t):
                wait_apart(sp, S["yo_done"], (t.n + 1) * HALVES, gate)
                wait_apart(sp, st[t.p], (t.h - E1 // 2) * 16, gate)
                sp.dma_start(out.rearrange("(t p) d -> p t d", p=P)[:, batch_rows(t), :], yo[t.p][:]
                             ).then_inc(st[t.p], 16)

            QUARTER = TILES // 4

            def load_and_tokens(t):
                load_slots(t)
                if isinstance(t.n, int) and t.n == 1:
                    sp.dma_start(sw16[:], a["sw"]).then_inc(S["sw_ld"], 16)
                    for q in range(4):
                        sp.dma_start(xn3[:, q * QUARTER:(q + 1) * QUARTER, :],
                                     xn3_d.rearrange("(t p) d -> p t d", p=P)[:, q * QUARTER:(q + 1) * QUARTER, :]
                                     ).then_inc(S["xn3_ld"], 16)

            loops(sp, [[(0, load_and_tokens)]], [[(0, load_parts)], [], [], [(1, store)]])
            for q in range(2):
                sp.wait_ge(st[q], BATCH // 2 * 16)

        @block.gpsimd
        def _(pool):
            def add(t):
                wait(pool, added[t.p], t.h * SLOT_TILES1 * 16)
                pool.wait_ge(S["tok_done"], t.n + 1)
                pool.wait_ge(S["yo_done"], (t.n + 1) * HALVES)
                apart(pool, gate)
                for c in range(SLOT_TILES1):
                    pool.indirect_dma_start(sums_d[t.p], bass.IndirectOffsetOnAxis(ap=tok[t.p][:, c:c + 1], axis=0), yo[t.p][:, c, :],
                                            None, compute_op=ALU.add).then_inc(added[t.p], 16)

            def routed_sum(t):
                pool.wait_ge(parts[t.p], (t.h - E1 // 2 + 1) * 32)
                wait(pool, S["yo_done"], (t.n - 1) * HALVES)
                pool.tensor_tensor(routed[t.p][:], part0[t.p][:], part1[t.p][:], ALU.add).then_inc(S["routed"], 1)

            def tokens(t):
                if isinstance(t.n, int) and t.n == E1:
                    pool.wait_ge(S["xn3_ld"], 4 * 16)
                wait(pool, S["t_ps"], t.n - 1)
                wait(pool, S["wsel_done"], E1)
                wait(pool, S["row_tok"], E1)
                pool.tensor_copy(xr[t.p][:, :, 0:D], xn3[:, bass.ds((t.n - E1) * HALVES, HALVES), :]).then_inc(S["tokens"], 1)

            loops(pool, [[], [], [(0, add)]], [[(0, tokens)], [], [(1, routed_sum)]])

        @block.tensor
        def _(pe):
            def turn_slots(t):
                pe.wait_ge(x_ld[t.p], (t.h + 1) * 16)
                turn(t)

            def turn_tokens(t):
                pe.wait_ge(S["tokens"], t.n - E1 + 1)
                turn(t)

            def turn(t):
                wait(pe, S["xl_done"], t.n - 1)
                for s in range(HALVES):
                    for k in range(DC):
                        mm = pe.transpose(ps_t[t.p][:, k * SEQ + s * P:k * SEQ + (s + 1) * P], xr[t.p][:, s, k * P:(k + 1) * P], ident)
                mm.then_inc(S["t_ps"], 1)

            def up(t, wts):
                pe.wait_ge(S["xl_done"], t.n + 1)
                wait(pe, S["hid_done"], t.n - 1)
                for n, ps in enumerate((ps_1, ps_3)):
                    i = 0
                    for k in range(DC):
                        for x in (x_hi, x_lo):
                            c = (n * DC + k) * INNER
                            mm = pe.matmul(ps[t.p][:, 0:SEQ], wts[:, c:c + INNER], x[t.p][:, k, :], start=i == 0, stop=i == 2 * DC - 1)
                            i += 1
                mm.then_inc(S["up_ps"], 1)

            def down(t, wts):
                pe.wait_ge(S["hl_done"], t.n + 1)
                wait(pe, S["yo_done"], (t.n - 1) * HALVES)
                for s in range(HALVES):
                    for i, h in enumerate((h_hi, h_lo)):
                        mm = pe.matmul(ps_y[t.p][:, s * D:(s + 1) * D], h[t.p][:, s * P:(s + 1) * P], wts[:, W_UP:W_UP + D],
                                       start=i == 0, stop=i == 1)
                mm.then_inc(S["y_ps"], 1)

            def up_shared(t):
                if isinstance(t.n, int) and t.n == E1:
                    pe.wait_ge(S["sw_done"], 1)
                up(t, sw)

            def down_shared(t):
                down(t, sw)

            def up_expert(t):
                pe.wait_ge(S["w_done"], t.n + 1)
                up(t, w[t.p])

            def down_expert(t):
                pe.wait_ge(S["wd_done"], t.n + 1)
                down(t, w[t.p])

            loops(pe, [[(0, turn_slots)], [(1, up_expert)], [(2, down_expert)]], [[(0, turn_tokens)], [(1, up_shared)], [(2, down_shared)]])

        @block.scalar
        def _(act):
            def turn(t):
                act.wait_ge(S["t_ps"], t.n + 1)
                wait(act, S["up_ps"], t.n - 1)
                act.activation(x_hi[t.p][:], ps_t[t.p][:].rearrange("p (k i) -> p k i", k=DC), ACT.Copy).then_inc(S["xh_done"], 1)

            def up(t):
                act.wait_ge(S["up_ps"], t.n + 1)
                wait(act, S["hid_done"], t.n - 1)
                act.activation(s1[t.p][:], ps_1[t.p][:, 0:SEQ], ACT.Silu).then_inc(S["s1_done"], 1)

            def split_hidden(t):
                act.wait_ge(S["hid_done"], t.n + 1)
                wait(act, S["y_ps"], t.n - 1)
                act.activation(h_hi[t.p][:], hid[t.p][:], ACT.Copy).then_inc(S["hh_done"], 1)

            def down_expert(t):
                act.wait_ge(S["y_ps"], t.n + 1)
                act.wait_ge(S["wrow_done"], t.n + 1)
                wait(act, added[t.p], t.h * SLOT_TILES1 * 16)
                for s in range(HALVES):
                    act.activation(yo[t.p][:, s, :], ps_y[t.p][:, s * D:(s + 1) * D], ACT.Copy, scale=wrow[t.p][:, s:s + 1]
                                   ).then_inc(S["yo_done"], 1)

            loops(act, [[(0, turn)], [(1, up), (2, split_hidden)], [(3, down_expert)]],
                  [[(0, turn)], [(1, up), (2, split_hidden)]])

        @block.vector
        def _(ve):
            def turn(t):
                ve.wait_ge(S["xh_done"], t.n + 1)
                wait(ve, S["up_ps"], t.n - 1)
                if isinstance(t.n, int) and t.n == E1:
                    ve.wait_ge(S["sw_ld"], 16)
                    ve.tensor_copy(sw[:], sw16[:]).then_inc(S["sw_done"], 1)
                ve.tensor_tensor(x_lo[t.p][:], ps_t[t.p][:].rearrange("p (k i) -> p k i", k=DC), x_hi[t.p][:], ALU.subtract
                                 ).then_inc(S["xl_done"], 1)

            def weights_up(t):
                ve.wait_ge(w_ld[t.p], (t.h + 1) * 16)
                wait(ve, S["up_ps"], t.n - 1)
                ve.tensor_copy(w[t.p][:, 0:W_UP], w16[t.p][:, 0:W_UP]).then_inc(S["w_done"], 1)

            def weights_down(t):
                wait(ve, S["y_ps"], t.n - 1)
                ve.tensor_copy(w[t.p][:, W_UP:W_UP + D], w16[t.p][:, W_UP:W_UP + D]).then_inc(S["wd_done"], 1)

            def row_ends(t):
                ve.wait_ge(x_ld[t.p], (t.h + 1) * 16)
                wait(ve, S["wrow_done"], t.n - 1)
                wait(ve, S["tok_done"], t.n - 1)
                ve.scalar_tensor_tensor(wsel[t.p][:], xr[t.p][:, :, C_E:C_E + TOP1], consts[:, bass.ds(t.n + K_IOTA, 1)],
                                        xr[t.p][:, :, C_W:C_W + TOP1], ALU.is_equal, ALU.mult).then_inc(S["wsel_done"], 1)
                ve.tensor_copy(row_tok[t.p][:], xr[t.p][:, :, C_TOK]).then_inc(S["row_tok"], 1)

            def row_weight(t):
                ve.wait_ge(S["wsel_done"], t.n + 1)
                wait(ve, S["yo_done"], (t.n - 1) * HALVES)
                ve.tensor_reduce(wrow[t.p][:], wsel[t.p][:], AX.X, ALU.add).then_inc(S["wrow_done"], 1)
                ve.wait_ge(S["row_tok"], t.n + 1)
                wait(ve, added[t.p], t.h * SLOT_TILES1 * 16)
                ve.tensor_copy(tok[t.p][:], row_tok[t.p][:]).then_inc(S["tok_done"], 1)

            def up(t):
                ve.wait_ge(S["s1_done"], t.n + 1)
                wait(ve, S["hh_done"], t.n - 1)
                wait(ve, S["hl_done"], t.n - 1)
                ve.tensor_tensor(hid[t.p][:], s1[t.p][:], ps_3[t.p][:, 0:SEQ], ALU.mult).then_inc(S["hid_done"], 1)

            def split_hidden(t):
                ve.wait_ge(S["hh_done"], t.n + 1)
                wait(ve, S["y_ps"], t.n - 1)
                ve.tensor_tensor(h_lo[t.p][:], hid[t.p][:], h_hi[t.p][:], ALU.subtract).then_inc(S["hl_done"], 1)

            def down_shared(t):
                ve.wait_ge(S["y_ps"], t.n + 1)
                ve.tensor_tensor(ysum[t.p][:], ps_y[t.p][:].rearrange("p (s d) -> p s d", s=HALVES),
                                 x_res[:, bass.ds((t.n - E1) * HALVES, HALVES), :], ALU.add).then_inc(S["ysum"], 1)
                ve.wait_ge(S["ysum"], t.n - E1 + 1)
                ve.wait_ge(S["routed"], t.n - E1 + 1)
                if isinstance(t.n, int) and t.n == E1:
                    for q in range(2):
                        ve.wait_ge(added[q], ADDS)
                wait(ve, st[t.p], (t.h - E1 // 2) * 16)
                for s in range(HALVES):
                    ve.tensor_tensor(yo[t.p][:, s, :], ysum[t.p][:, s, :], routed[t.p][:, s, :], ALU.add
                                     ).then_inc(S["yo_done"], 1)

            loops(ve, [[(0, row_ends), (3, weights_up), (4, turn)],
                       [(1, weights_down), (2, up), (5, split_hidden), (6, row_weight)]],
                  [[(0, turn)], [(1, up), (3, split_hidden)], [(2, down_shared)]])


def kernel(**inputs):
    import numpy as np
    import concourse.bacc as bacc
    from concourse.bass_utils import run_bass_kernel_spmd

    nc = bacc.Bacc("TRN2", target_bir_lowering=False, num_devices=1)
    arrays, aps = lay_out(np, inputs), {}
    for name, array in arrays.items():
        aps[name] = nc.dram_tensor(f"in_{name}", array.shape, mybir.dt.from_np(array.dtype), kind="ExternalInput").ap()
    out = nc.dram_tensor("out", (TOKENS, D), F32, kind="ExternalOutput").ap()
    build(nc, aps, out)
    r = run_bass_kernel_spmd(nc, [{f"in_{k}": v for k, v in arrays.items()}], core_ids=[0])
    return r.results[0]["out"].reshape(BATCH, SEQ, D)


def lay_out(np, inputs):
    g = {k: np.asarray(v) for k, v in inputs.items()}

    def chunks(w):
        return np.ascontiguousarray(w.reshape(-1, P, w.shape[-1]).transpose(1, 0, 2))

    def unit(w):
        return w.reshape(-1, DC, P, INNER).transpose(0, 2, 1, 3).reshape(-1, P, DC * INNER)

    c = np.zeros((P, K_END), np.float32)
    p = np.arange(P)
    c[:, K_ID:K_ID + P] = np.eye(P)
    c[:, K_SU:K_SU + P] = p[:, None] < p[None, :]
    c[:, K_IOTA:K_IOTA + P] = p[None, :]
    c[:, K_P] = p
    c[:, K_HEAD:K_HEAD + HPC] = p[:, None] // HD == np.arange(HPC)[None, :]
    c[:, K_CAUSAL:K_CAUSAL + CTX] = np.where(np.arange(CTX)[None, :] > p[:, None], MASKED, 0.0)
    ctx = g["ctx_1024"]
    return {
        "consts": c,
        "x": np.ascontiguousarray(g["x"].reshape(TILES, P, D).transpose(1, 0, 2)),
        "ctx": ctx,
        "ctx_t": np.ascontiguousarray(ctx.transpose(0, 2, 1).reshape(BATCH, DC, P, CTX).transpose(0, 2, 1, 3)),
        "wsim": np.ascontiguousarray(g["L0_xattn_w_sim"].reshape(3, DC, P).transpose(2, 0, 1)),
        "b_sim": g["L0_xattn_b_sim"],
        "wqv": chunks(g["L0_xattn_W_qv"]),
        "bqv2": np.stack([g["L0_xattn_b_qv"]] * HALVES),
        "router_w": chunks(g["L0_ffn_router_w"].T),
        "router_b": g["L0_ffn_router_b"],
        "fc1_t": np.ascontiguousarray(g["L0_ffn_fc1_w"].transpose(0, 2, 1).reshape(E0, DC, P, HID0).transpose(0, 2, 1, 3)),
        "fc1_b": np.ascontiguousarray(g["L0_ffn_fc1_b"].reshape(E0, HC0, P).transpose(0, 2, 1)),
        "fc2_t": np.ascontiguousarray(g["L0_ffn_fc2_w"].transpose(0, 2, 1).reshape(E0, HC0, P, D).transpose(0, 2, 1, 3)),
        "fc2_b": g["L0_ffn_fc2_b"],
        "ls": g["L0_ffn_layer_scale"],
        "wq_t": chunks(g["L1_xattn_Wq"].T),
        "wk_t": chunks(g["L1_xattn_Wk"].T),
        "wv_t": chunks(g["L1_xattn_Wv"].T),
        "wo_t": chunks(g["L1_xattn_Wo"].T),
        "bq": np.ascontiguousarray(g["L1_xattn_bq"].reshape(DC, P).T),
        "bk": np.ascontiguousarray(g["L1_xattn_bk"].reshape(DC, P).T),
        "bv": g["L1_xattn_bv"],
        "bo": g["L1_xattn_bo"].reshape(1, D),
        "gate_w": chunks(g["L1_ffn_gate_w"].T),
        "gate_b": g["L1_ffn_bias"],
        "moe_w": np.concatenate([unit(g["L1_ffn_W1"]), unit(g["L1_ffn_W3"]), g["L1_ffn_W2"]], axis=2),
        "sw": np.concatenate([unit(g["L1_ffn_sw1"].T[None]), unit(g["L1_ffn_sw3"].T[None]), g["L1_ffn_sw2"].T[None]], axis=2)[0],
    }
```
